# Optimizing a Trainium2 kernel written in Bass

```python
import numpy as np
import jax
import jax.numpy as jnp

def _softmax(x, axis=-1):
    return jax.nn.softmax(x, axis=axis)

def _gelu(x):
    return jax.nn.gelu(x, approximate=True)

def _silu(x):
    return jax.nn.silu(x)

def _sigmoid(x):
    return jax.nn.sigmoid(x)

def _layernorm(x, axis=-1, eps=1e-05):
    m = jnp.mean(x, axis=axis, keepdims=True)
    v = jnp.var(x, axis=axis, keepdims=True)
    return (x - m) / jnp.sqrt(v + eps)

def _scatter_add(tgt, idx, src, axis=0):
    return tgt.at[idx].add(src)

def _segment_sum(src, seg, n):
    return jax.ops.segment_sum(src, seg, n)
kernel_name = 'mk_recurrent_d1_jaxref_r8_d59457'

def setup_inputs(seed: int=0):
    np.random.seed(seed)
    _w = jnp.asarray

    def _L0_attn_setup():
        import jax, jax.numpy as jnp
        import numpy as np
        import math
        B, SEQ, DIM, HEADS = (1, 256, 256, 8)
        L_INIT = 0.8 - 0.6 * math.exp(-0.3 * 1)
        EPS = 1e-06
        key = jax.random.key(seed)
        ks = jax.random.split(key, 9)
        x = jax.random.normal(ks[0], (B, SEQ, DIM), jnp.float32)
        l_q1 = jax.random.normal(ks[1], (HEADS,), jnp.float32) * 0.1
        l_k1 = jax.random.normal(ks[2], (HEADS,), jnp.float32) * 0.1
        l_q2 = jax.random.normal(ks[3], (HEADS,), jnp.float32) * 0.1
        l_k2 = jax.random.normal(ks[4], (HEADS,), jnp.float32) * 0.1
        s = 1.0 / math.sqrt(DIM)
        wq = jax.random.normal(ks[5], (2 * DIM, DIM), jnp.float32) * s
        wk = jax.random.normal(ks[6], (2 * DIM, DIM), jnp.float32) * s
        wv = jax.random.normal(ks[7], (DIM, DIM), jnp.float32) * s
        wo = jax.random.normal(ks[8], (DIM, DIM), jnp.float32) * s
        return {'x': x, 'l_q1': l_q1, 'l_k1': l_k1, 'l_q2': l_q2, 'l_k2': l_k2, 'wq': wq, 'wk': wk, 'wv': wv, 'wo': wo}
    _L0_attn_in = _L0_attn_setup()

    def _L0_ffn_setup():
        import jax, jax.numpy as jnp
        import numpy as np
        ALPHA = 1.702
        LIMIT = 7.0
        TOP_K = 2
        E, H, I = (8, 256, 256)
        B, S = (2, 256)
        key = jax.random.key(seed)
        ks = jax.random.split(key, 7)
        return {'hidden_states': jax.random.normal(ks[0], (B, S, H), dtype=jnp.float32), 'router_weight': jax.random.normal(ks[1], (E, H), dtype=jnp.float32) * 0.02, 'router_bias': jax.random.normal(ks[2], (E,), dtype=jnp.float32) * 0.02, 'gate_up_proj': jax.random.normal(ks[3], (E, H, 2 * I), dtype=jnp.float32) * 0.02, 'gate_up_proj_bias': jax.random.normal(ks[4], (E, 2 * I), dtype=jnp.float32) * 0.02, 'down_proj': jax.random.normal(ks[5], (E, I, H), dtype=jnp.float32) * 0.02, 'down_proj_bias': jax.random.normal(ks[6], (E, H), dtype=jnp.float32) * 0.02}
    _L0_ffn_in = _L0_ffn_setup()
    _d = {'L0_attn_x': _L0_attn_in['x'], 'L0_attn_l_q1': _L0_attn_in['l_q1'], 'L0_attn_l_k1': _L0_attn_in['l_k1'], 'L0_attn_l_q2': _L0_attn_in['l_q2'], 'L0_attn_l_k2': _L0_attn_in['l_k2'], 'L0_attn_wq': _L0_attn_in['wq'], 'L0_attn_wk': _L0_attn_in['wk'], 'L0_attn_wv': _L0_attn_in['wv'], 'L0_attn_wo': _L0_attn_in['wo'], 'L0_ffn_router_weight': _L0_ffn_in['router_weight'], 'L0_ffn_router_bias': _L0_ffn_in['router_bias'], 'L0_ffn_gate_up_proj': _L0_ffn_in['gate_up_proj'], 'L0_ffn_gate_up_proj_bias': _L0_ffn_in['gate_up_proj_bias'], 'L0_ffn_down_proj': _L0_ffn_in['down_proj'], 'L0_ffn_down_proj_bias': _L0_ffn_in['down_proj_bias']}
    _x0 = _d['L0_attn_x']
    _d['L0_attn_x'] = jax.random.normal(jax.random.fold_in(jax.random.key(seed), 1), (4, 1024, 256), dtype=_x0.dtype)
    del _x0
    return _d

def reference(L0_attn_x, L0_attn_l_q1, L0_attn_l_k1, L0_attn_l_q2, L0_attn_l_k2, L0_attn_wq, L0_attn_wk, L0_attn_wv, L0_attn_wo, L0_ffn_router_weight, L0_ffn_router_bias, L0_ffn_gate_up_proj, L0_ffn_gate_up_proj_bias, L0_ffn_down_proj, L0_ffn_down_proj_bias):

    def _L0_attn_ref(x, l_q1, l_k1, l_q2, l_k2, wq, wk, wv, wo):
        import jax, jax.numpy as jnp
        import numpy as np
        import math
        B, SEQ, DIM, HEADS = (1, 256, 256, 8)
        L_INIT = 0.8 - 0.6 * math.exp(-0.3 * 1)
        EPS = 1e-06
        b, s, d = x.shape
        nh = HEADS
        lmbda = jnp.exp(jnp.sum(l_q1 * l_k1)) - jnp.exp(jnp.sum(l_q2 * l_k2)) + L_INIT
        q = jnp.einsum('bsd,od->bso', x, wq)
        k = jnp.einsum('bsd,od->bso', x, wk)
        v = jnp.einsum('bsd,od->bso', x, wv)

        def split_heads(t):
            return t.reshape(b, s, nh, -1).transpose(0, 2, 1, 3)
        q, k, v = map(split_heads, (q, k, v))

        def prep(t):
            dh = t.shape[-1] // 2
            t = t.reshape(b, nh, s, 2, dh)
            return t.transpose(0, 1, 3, 2, 4).reshape(b, nh * 2, s, dh)
        q, k = (prep(q), prep(k))
        dh = q.shape[-1]
        scores = jnp.einsum('bhqd,bhkd->bhqk', q, k) / math.sqrt(dh)
        causal = jnp.triu(jnp.full((s, s), -jnp.inf, dtype=scores.dtype), 1)
        attn = jax.nn.softmax((scores + causal[None, None]).astype(jnp.float32), axis=-1).astype(scores.dtype)
        attn = attn[:, :nh] - attn[:, nh:] * lmbda
        out = jnp.einsum('bhqk,bhkd->bhqd', attn, v)
        dv = out.shape[-1]
        o = out.reshape(b, nh, s, nh, dv // nh)
        o32 = o.astype(jnp.float32)
        o = (o32 * jax.lax.rsqrt(jnp.mean(o32 * o32, axis=-1, keepdims=True) + EPS)).astype(o.dtype)
        o = o.reshape(b, nh, s, dv) * (1.0 - L_INIT)
        o = o.transpose(0, 2, 1, 3).reshape(b, s, nh * dv)
        return jnp.einsum('bsd,od->bso', o, wo)

    def _L0_ffn_ref(hidden_states, router_weight, router_bias, gate_up_proj, gate_up_proj_bias, down_proj, down_proj_bias):
        import jax, jax.numpy as jnp
        import numpy as np
        ALPHA = 1.702
        LIMIT = 7.0
        TOP_K = 2
        E, H, I = (8, 256, 256)
        B, S = (2, 256)
        bsz, seq_len, hidden = hidden_states.shape
        h = hidden_states.reshape(-1, hidden)
        T = h.shape[0]
        logits = h @ router_weight.T + router_bias
        top_vals, top_idx = jax.lax.top_k(logits, TOP_K)
        top_w = jax.nn.softmax(top_vals, axis=-1)
        scores = jnp.zeros_like(logits).at[jnp.arange(T)[:, None], top_idx].set(top_w)
        gate_up = jnp.einsum('th,ehj->etj', h, gate_up_proj) + gate_up_proj_bias[:, None, :]
        gate = gate_up[..., ::2]
        up = gate_up[..., 1::2]
        gate = jnp.minimum(gate, LIMIT)
        up = jnp.clip(up, -LIMIT, LIMIT)
        glu = gate * jax.nn.sigmoid(gate * ALPHA)
        act = (up + 1.0) * glu
        expert_out = jnp.einsum('eti,eih->eth', act, down_proj) + down_proj_bias[:, None, :]
        out = jnp.einsum('te,eth->th', scores, expert_out)
        return out.reshape(bsz, seq_len, hidden)
    x = L0_attn_x
    xn = _layernorm(x, axis=-1)
    s = _L0_attn_ref(xn, L0_attn_l_q1, L0_attn_l_k1, L0_attn_l_q2, L0_attn_l_k2, L0_attn_wq, L0_attn_wk, L0_attn_wv, L0_attn_wo)
    g = _silu(_L0_ffn_ref(xn, L0_ffn_router_weight, L0_ffn_router_bias, L0_ffn_gate_up_proj, L0_ffn_gate_up_proj_bias, L0_ffn_down_proj, L0_ffn_down_proj_bias))
    x = x + s * g
    return x

_drawn_inputs = setup_inputs


def setup_inputs(seed=0):
    import zlib

    import numpy as np

    out = dict(_drawn_inputs(seed))
    spreads = {}
    factors = {'L0_attn_l_q1': 8.0,
     'L0_attn_l_k1': 8.0,
     'L0_attn_l_q2': 8.0,
     'L0_attn_l_k2': 8.0,
     'L0_attn_wq': 4.309,
     'L0_attn_wk': 4.312,
     'L0_attn_wv': 4.018,
     'L0_attn_wo': 4.015,
     'L0_ffn_router_weight': 4.6,
     'L0_ffn_router_bias': 8.0,
     'L0_ffn_gate_up_proj': 4.362,
     'L0_ffn_gate_up_proj_bias': 8.0,
     'L0_ffn_down_proj': 4.239,
     'L0_ffn_down_proj_bias': 8.0}
    for name, (base, spread) in spreads.items():
        noise = np.random.default_rng([zlib.crc32(name.encode()), seed]).standard_normal(out[name].shape)
        drawn = base * np.exp(spread * noise) if base else spread * noise
        out[name] = jnp.asarray(drawn.astype(out[name].dtype))
    for name, factor in factors.items():
        out[name] = (out[name] * factor).astype(out[name].dtype)
    return out
```

```python
import math
from contextlib import ExitStack

import concourse.bass as bass
from concourse import mybir

F32 = mybir.dt.float32
F32R = mybir.dt.float32r
BF16 = mybir.dt.bfloat16
U32 = mybir.dt.uint32
I32 = mybir.dt.int32
ALU = mybir.AluOpType
ACT = mybir.ActivationFunctionType
AX = mybir.AxisListType

B, S, D = 4, 1024, 256
NH, DH = 8, 32
T = B * S
E, I, LIMIT, ALPHA = 8, 256, 7.0, 1.702
L_INIT = 0.8 - 0.6 * math.exp(-0.3 * 1)
LN_EPS, RMS_EPS = 1e-5, 1e-6
GROUP = DH // NH
P = 128
HC = D // P
CH = 512
CT = CH // P
NCH = T // CH
QT = S // P
MASKED = -1.0e30

QKT = 2 * 2 * NH * DH // P
NIT = B * NH // 2
STEPS = 2 * 2 * QT
NQ = 2 * QT
TOP_K = 2
SLOT_TILES = T * TOP_K // P + E
KB_UNIT = 4


def credited(it, per, event):
    return (it + 1) * per + event + 1


def units(n):
    head, q = divmod(n, QT)
    first = sum(-(-(i % QT + 1) // KB_UNIT) for i in range(n))
    blocks = list(range(q + 1))
    return [(first + k, blocks[KB_UNIT * k:KB_UNIT * (k + 1)]) for k in range(-(-(q + 1) // KB_UNIT))]


UNITS = units(NQ - 1)[-1][0] + 1


def slot_user(step):
    if step >= 3:
        return step - 3
    return max(s for s in range(STEPS) if s % 3 == step) - STEPS


def build(nc, x, wqk, wv, wo, lam, rw, rb, gu, gub, dn, dnb, out):
    with ExitStack() as ctx:
        def sb(name, shape, dt=F32, where=ctx):
            return where.enter_context(nc.sbuf_tensor(name, shape, dt))

        def sem(name):
            return ctx.enter_context(nc.semaphore(name))

        q_parts = nc.dram_tensor("q_parts", (NIT, 2, P, S), F32, kind="Internal").ap()
        k_parts = nc.dram_tensor("k_parts", (NIT, 2, P, S), F32, kind="Internal").ap()
        xn_dram = nc.dram_tensor("xn_dram", (T, D), F32, kind="Internal").ap()
        xs_dram = nc.dram_tensor("xs_dram", (SLOT_TILES * P, D), F32, kind="Internal").ap()
        ys_dram = nc.dram_tensor("ys_dram", (SLOT_TILES * P, D), F32, kind="Internal").ap()
        o_dram = nc.dram_tensor("o_dram", (B * NH, P, S), F32, kind="Internal").ap()

        bank = [ctx.enter_context(nc.psum_tensor(f"bank{i}", [P, 2 * CH], F32)) for i in range(3)]
        bank6 = ctx.enter_context(nc.psum_tensor("bank6", [P, CH], F32))
        bank7 = ctx.enter_context(nc.psum_tensor("bank7", [P, CH], F32))

        ident = sb("ident", [P, P])
        identb = sb("identb", [P, P], BF16)
        maskb = sb("maskb", [P, P], BF16)
        zerob = sb("zerob", [P, CH], BF16)
        gather4 = sb("gather4", [P, 224])
        group_mean = sb("group_mean", [P, P])
        V_all = sb("V_all", [P, B * QT, D])
        d1_all = sb("d1_all", [P, B * NH, QT])
        lam_in = sb("lam_in", [P, 4, NH])
        lam_w = sb("lam_w", [P, 2, NH])
        lam_s = sb("lam_s", [P, 8])
        neg_lam = lam_s[:, 6:7]
        wo_sb = sb("wo_sb", [P, HC, D])
        gu_sb = sb("gu_sb", [P, HC, E, 2 * I])
        dn_sb = sb("dn_sb", [P, HC, E, D])
        gub_sb = sb("gub_sb", [P, E, 2 * I])
        dnb_sb = sb("dnb_sb", [P, E, D])
        weight = sb("weight", [P, T // P, TOP_K])
        slot_of = sb("slot_of", [P, T // P, TOP_K], U32)
        expert_of = sb("expert_of", [P, SLOT_TILES], I32)

        consts_done = sem("consts_done")
        lam_step = sem("lam_step")
        ew_loaded = sem("ew_loaded")
        const_step = sem("const_step")

        with ExitStack() as ph:
            wqk_sb = sb("wqk_sb", [P, HC, QKT * P], where=ph)
            wv_sb = sb("wv_sb", [P, HC, D + E], where=ph)
            rb_sb = sb("rb_sb", [P, E], where=ph)
            zeros = sb("zeros", [P, 8 * D], where=ph)
            before = sb("before", [P, E, E], where=ph)
            earlier = sb("earlier", [P, P], BF16, where=ph)
            ones = sb("ones", [P, P], BF16, where=ph)
            count_i = sb("count_i", [P, SLOT_TILES], I32, where=ph)
            count_f = sb("count_f", [P, SLOT_TILES], where=ph)
            count_128 = sb("count_128", [P, T // P], where=ph)
            logits = sb("logits", [P, T // P, E], where=ph)
            cmp = sb("cmp", [P, T // P * E * E], where=ph)
            ranks = sb("ranks", [P, 3, T // P, E], where=ph)
            chosen = sb("chosen", [P, TOP_K, T // P, E], where=ph)
            chosen_b = sb("chosen_b", [P, T // P, E], BF16, where=ph)
            top = sb("top", [P, 6, T // P], where=ph)
            run = [sb(f"run{i}", [P, T // P, E], where=ph) for i in range(2)]
            per_e = sb("per_e", [P, 8, E], where=ph)
            X = [sb(f"X{h}", [P, CT, D], where=ph) for h in range(2)]
            XN = [sb(f"XN{h}", [P, CT, D], where=ph) for h in range(2)]
            XNT = [sb(f"XNT{h}", [P, HC, CH], where=ph) for h in range(2)]
            PARTS = [sb(f"PARTS{i}", [P, 2, CH], F32R, where=ph) for i in range(4)]
            stats = sb("stats", [P, CT, 6], where=ph)
            mv = sb("mv", [P, CT, 2], where=ph)
            ve = sb("ve", [P, CT], where=ph)
            sd = sb("sd", [P, CT], where=ph)
            rs = sb("rs", [P, CT], where=ph)
            nt = sb("nt", [P, CT], where=ph)

            w_loaded = sem("w_loaded")
            x_loaded = [sem(f"x_loaded{h}") for h in range(2)]
            ln_step = sem("ln_step")
            stats_seen = sem("stats_seen")
            var_ready = sem("var_ready")
            std_ready = sem("std_ready")
            xn_ready = sem("xn_ready")
            xnT_bank = sem("xnT_bank")
            xnT_ready = sem("xnT_ready")
            qk_bank = sem("qk_bank")
            hi_ready = sem("hi_ready")
            lo_ready = sem("lo_ready")
            v_bank = sem("v_bank")
            v_ready = sem("v_ready")
            parts_stored = [sem(f"parts_stored{i}") for i in range(4)]
            xn_stored = [sem(f"xn_stored{h}") for h in range(2)]
            logits_ready = sem("logits_ready")
            zeros_ready = sem("zeros_ready")
            zeros_stored = sem("zeros_stored")
            route = sem("route")
            chosen_ready = sem("chosen_ready")
            ranks_bank = sem("ranks_bank")
            gap_ready = sem("gap_ready")
            odds_ready = sem("odds_ready")

            tbank = [bank[0][:, 0:CH], bank[0][:, CH:]]
            qkbank = [bank[1][:, 0:CH], bank[1][:, CH:], bank[2][:, 0:CH], bank[2][:, CH:]]
            vbank = [bank6, bank7]
            LN_OPS = 13

            with nc.Block() as block:
                @block.gpsimd
                def _(pool):
                    nc.gpsimd.memset(ident[:], 0.0).then_inc(const_step, 1)
                    nc.gpsimd.memset(maskb[:], 0.0).then_inc(const_step, 1)
                    nc.gpsimd.memset(gather4[:], 0.0).then_inc(const_step, 1)
                    nc.gpsimd.memset(group_mean[:], 1.0 / GROUP).then_inc(const_step, 1)
                    nc.gpsimd.memset(zerob[:], 0.0).then_inc(consts_done, 1)
                    pool.wait_ge(const_step, 4)
                    nc.gpsimd.affine_select(out=ident[:], in_=ident[:], compare_op=ALU.not_equal, fill=1.0,
                                            base=0, pattern=[[-1, P]], channel_multiplier=1).then_inc(const_step, 1)
                    nc.gpsimd.affine_select(out=maskb[:], in_=maskb[:], compare_op=ALU.is_ge, fill=MASKED,
                                            base=0, pattern=[[-1, P]], channel_multiplier=1).then_inc(consts_done, 1)
                    for g in range(4):
                        nc.gpsimd.affine_select(out=gather4[:, 96:128], in_=gather4[:, 96:128],
                                                compare_op=ALU.not_equal, fill=1.0, base=-32 * g,
                                                pattern=[[-1, 32]], channel_multiplier=1).then_inc(const_step, 1)
                        pool.wait_ge(const_step, 6 + g)
                    v = group_mean[:].rearrange("p (a c) -> p a c", c=GROUP)
                    nc.gpsimd.affine_select(out=v, in_=v, compare_op=ALU.is_ge, fill=0.0, base=0,
                                            pattern=[[-GROUP, P // GROUP], [0, GROUP]],
                                            channel_multiplier=1).then_inc(const_step, 1)
                    pool.wait_ge(const_step, 10)
                    nc.gpsimd.affine_select(out=v, in_=v, compare_op=ALU.is_ge, fill=0.0, base=GROUP - 1,
                                            pattern=[[GROUP, P // GROUP], [0, GROUP]],
                                            channel_multiplier=-1).then_inc(consts_done, 1)
                    nc.gpsimd.tensor_copy(identb[:], ident[:]).then_inc(consts_done, 1)
                    nc.gpsimd.memset(zeros[:], 0.0).then_inc(zeros_ready, 1)
                    nc.gpsimd.memset(before[:], 1.0).then_inc(const_step, 1)
                    nc.gpsimd.memset(earlier[:], 1.0).then_inc(const_step, 1)
                    nc.gpsimd.memset(ones[:], 1.0).then_inc(consts_done, 1)
                    nc.gpsimd.iota(count_i[:], pattern=[[1, SLOT_TILES]], base=0, channel_multiplier=0
                                   ).then_inc(const_step, 1)
                    pool.wait_ge(const_step, 13)
                    nc.gpsimd.affine_select(out=before[:], in_=before[:], compare_op=ALU.is_gt, fill=0.0, base=0,
                                            pattern=[[1, E], [-1, E]], channel_multiplier=0
                                            ).then_inc(consts_done, 1)
                    nc.gpsimd.affine_select(out=earlier[:], in_=earlier[:], compare_op=ALU.is_gt, fill=0.0,
                                            base=0, pattern=[[1, P]], channel_multiplier=-1
                                            ).then_inc(consts_done, 1)
                    nc.gpsimd.tensor_copy(count_f[:], count_i[:]).then_inc(const_step, 1)
                    pool.wait_ge(const_step, 14)
                    nc.gpsimd.tensor_scalar(count_128[:], count_f[:, 0:T // P], float(P), None, ALU.mult
                                            ).then_inc(consts_done, 1)

                @block.sync
                def _(sp):
                    sp.dma_start(wqk_sb[:], wqk.rearrange("(c p) n -> p c n", p=P)).then_inc(w_loaded, 16)
                    sp.dma_start(wv_sb[:, :, 0:D], wv.rearrange("(c p) n -> p c n", p=P)).then_inc(w_loaded, 16)
                    sp.dma_start(wv_sb[:, :, D:], rw.rearrange("(c p) n -> p c n", p=P)).then_inc(w_loaded, 16)
                    sp.dma_start(lam_in[:], lam.partition_broadcast(P)).then_inc(w_loaded, 16)
                    sp.dma_start(wo_sb[:], wo.rearrange("(c p) n -> p c n", p=P)).then_inc(w_loaded, 16)
                    sp.dma_start(rb_sb[:], rb.partition_broadcast(P)).then_inc(w_loaded, 16)
                    x_v = x.rearrange("(b h t p) d -> b h p t d", b=B, h=2, p=P)
                    for h in range(2):
                        sp.dma_start(X[h][:], x_v[0, h]).then_inc(x_loaded[h], 16)
                    sp.dma_start(gu_sb[:].rearrange("p c e n -> p c (e n)"),
                                 gu.rearrange("(c p) e n -> p c (e n)", p=P)).then_inc(ew_loaded, 16)
                    sp.dma_start(dn_sb[:].rearrange("p c e n -> p c (e n)"),
                                 dn.rearrange("(c p) e n -> p c (e n)", p=P)).then_inc(ew_loaded, 16)
                    sp.dma_start(gub_sb[:], gub.partition_broadcast(P)).then_inc(ew_loaded, 16)
                    sp.dma_start(dnb_sb[:], dnb.partition_broadcast(P)).then_inc(ew_loaded, 16)
                    sp.wait_ge(zeros_ready, 1)
                    xs_v = xs_dram.rearrange("(n p r) d -> n p (r d)", p=P, r=8)
                    for n in range(SLOT_TILES // 8):
                        sp.dma_start(xs_v[n], zeros[:]).then_inc(zeros_stored, 16)

                    xn_v = xn_dram.rearrange("(c t p) d -> c p t d", c=NCH, p=P)

                    def chunk(b, h):
                        sp.wait_ge(xn_ready, credited(b, 2, h))
                        sp.dma_start(xn_v[b * 2 + h], XN[h][:]).then_inc(xn_stored[h], 16)
                        for i in range(QKT):
                            sp.wait_ge(hi_ready, credited(b, 2 * QKT, h * QKT + i))
                            sp.wait_ge(lo_ready, credited(b, 2 * QKT, h * QKT + i))
                            dst = (q_parts if i < QKT // 2 else k_parts)[
                                b * 4 + i % 4, :, :, h * CH:(h + 1) * CH]
                            sp.dma_start(dst.rearrange("l p n -> p l n"), PARTS[i % 4][:].bitcast(F32)
                                         ).then_inc(parts_stored[i % 4], 16)

                    with sp.Fori(0, B - 1) as b:
                        for h in range(2):
                            sp.wait_ge(xn_ready, credited(b, 2, h))
                            sp.dma_start(X[h][:], x_v[b + 1, h]).then_inc(x_loaded[h], 16)
                            chunk(b, h)
                    for h in range(2):
                        chunk(B - 1, h)
                    for h in range(2):
                        sp.wait_ge(xn_stored[h], 16 * (B + 1))
                    for i in range(4):
                        sp.wait_ge(parts_stored[i], 16 * (4 * B + 1))
                    sp.wait_ge(zeros_stored, 16 * (SLOT_TILES // 8))

                @block.vector
                def _(dve):
                    dve.sem_inc(ln_step, 2 * LN_OPS)
                    dve.sem_inc(xn_ready, 2)
                    dve.sem_inc(var_ready, 2)
                    dve.sem_inc(lo_ready, 2 * QKT)
                    dve.sem_inc(logits_ready, 8)
                    dve.wait_ge(w_loaded, 96)
                    nc.vector.tensor_tensor(lam_w[:], lam_in[:, 0:4:2, :], lam_in[:, 1:4:2, :], ALU.mult
                                            ).then_inc(lam_step, 1)
                    dve.wait_ge(lam_step, 1)
                    nc.vector.tensor_reduce(lam_s[:, 0:2], lam_w[:], AX.X, ALU.add).then_inc(lam_step, 1)
                    with dve.Fori(0, B) as b:
                        for h in range(2):
                            base = h * LN_OPS
                            dve.wait_ge(x_loaded[h], 16 * (b + 1))
                            for i in range(CT):
                                nc.vector.bn_stats(stats[:, i, :], X[h][:, i, :]).then_inc(ln_step, 1)
                            for i in range(CT):
                                if i == 0:
                                    dve.wait_ge(ln_step, credited(b, 2 * LN_OPS, base + 3))
                                    dve.sem_inc(stats_seen, 1)
                                nc.vector.bn_aggr(mv[:, i, :], stats[:, i, :]).then_inc(ln_step, 1)
                            dve.wait_ge(ln_step, credited(b, 2 * LN_OPS, base + 7))
                            nc.vector.tensor_scalar(ve[:], mv[:, :, 1], LN_EPS, None, ALU.add
                                                    ).then_inc(var_ready, 1)
                            dve.wait_ge(std_ready, credited(b, 2, h))
                            nc.vector.reciprocal(rs[:], sd[:]).then_inc(ln_step, 1)
                            dve.wait_ge(ln_step, credited(b, 2 * LN_OPS, base + 8))
                            nc.vector.tensor_tensor(nt[:], rs[:], rs[:], ALU.mult).then_inc(ln_step, 1)
                            dve.wait_ge(ln_step, credited(b, 2 * LN_OPS, base + 9))
                            nc.vector.tensor_tensor(nt[:], nt[:], ve[:], ALU.mult).then_inc(ln_step, 1)
                            dve.wait_ge(ln_step, credited(b, 2 * LN_OPS, base + 10))
                            nc.vector.tensor_scalar(nt[:], nt[:], -0.5, 1.5, ALU.mult, ALU.add
                                                    ).then_inc(ln_step, 1)
                            dve.wait_ge(ln_step, credited(b, 2 * LN_OPS, base + 11))
                            nc.vector.tensor_tensor(rs[:], rs[:], nt[:], ALU.mult).then_inc(ln_step, 1)
                            dve.wait_ge(ln_step, credited(b, 2 * LN_OPS, base + 12))
                            dve.wait_ge(xn_stored[h], 16 * (b + 1))
                            dve.wait_ge(xnT_bank, credited(b, 4, 2 * h + 1 - 4))
                            for i in range(CT):
                                last = nc.vector.tensor_scalar(XN[h][:, i, :], X[h][:, i, :], mv[:, i, 0:1],
                                                               rs[:, i:i + 1], ALU.subtract, ALU.mult)
                            last.then_inc(xn_ready, 1)
                            for i in range(QKT):
                                dve.wait_ge(hi_ready, credited(b, 2 * QKT, h * QKT + i))
                                scale = 1.0 / math.sqrt(DH) if i < QKT // 2 else 1.0
                                nc.vector.scalar_tensor_tensor(
                                    out=PARTS[i % 4][:, 1, :], in0=qkbank[i % 4], scalar=scale,
                                    in1=PARTS[i % 4][:, 0, :].bitcast(F32), op0=ALU.mult, op1=ALU.subtract
                                ).then_inc(lo_ready, 1)
                            for i in range(CT):
                                dve.wait_ge(v_ready, credited(b, 8, 4 * h + i))
                                nc.vector.tensor_tensor(logits[:, bass.ds(b * QT + h * CT + i, 1), :],
                                                        vbank[i % 2][:, D:D + E].unsqueeze(1),
                                                        rb_sb[:].unsqueeze(1), ALU.add).then_inc(logits_ready, 1)

                    steps = [0]

                    def then(ins):
                        ins.then_inc(route, 1)
                        steps[0] += 1
                        dve.wait_ge(route, steps[0])

                    NT = T // P
                    dve.wait_ge(consts_done, 8)
                    dve.wait_ge(logits_ready, credited(B - 1, 8, 7))
                    own = logits[:].unsqueeze(3).broadcast_to([P, NT, E, E])
                    other = logits[:].unsqueeze(2).broadcast_to([P, NT, E, E])
                    c4 = cmp[:].rearrange("p (t e f) -> p t e f", e=E, f=E)
                    c3 = cmp[:].rearrange("p (t k) -> p t k", t=NT)
                    flat = cmp[:].rearrange("p (n f) -> p n f", f=E)
                    then(nc.vector.tensor_tensor(c4, other, own, ALU.is_equal))
                    then(nc.vector.tensor_tensor(c3, c3, before[:].rearrange("p e f -> p (e f)").unsqueeze(1)
                                                 .broadcast_to([P, NT, E * E]), ALU.mult))
                    then(nc.vector.tensor_reduce(ranks[:, 0].rearrange("p t e -> p (t e)"), flat, AX.X, ALU.add))
                    then(nc.vector.tensor_tensor(c4, other, own, ALU.is_gt))
                    then(nc.vector.tensor_reduce(ranks[:, 1].rearrange("p t e -> p (t e)"), flat, AX.X, ALU.add))
                    then(nc.vector.tensor_tensor(ranks[:, 2], ranks[:, 0], ranks[:, 1], ALU.add))
                    for k in range(TOP_K):
                        then(nc.vector.tensor_scalar(chosen[:, k], ranks[:, 2], float(k), None, ALU.is_equal))
                    nc.vector.tensor_tensor(chosen_b[:], chosen[:, 0], chosen[:, 1], ALU.add
                                            ).then_inc(chosen_ready, 1)
                    ck = cmp[:, 0:TOP_K * NT * E].rearrange("p (k t e) -> p k t e", k=TOP_K, e=E)
                    for k in range(TOP_K):
                        then(nc.vector.tensor_tensor(ck[:, k], chosen[:, k], logits[:], ALU.mult))
                    then(nc.vector.tensor_reduce(top[:, 0:2], ck, AX.X, ALU.add))
                    nc.vector.tensor_tensor(top[:, 2], top[:, 1], top[:, 0], ALU.subtract).then_inc(gap_ready, 1)
                    dve.wait_ge(ranks_bank, 1)
                    pre = bank6[:, 0:NT * E].rearrange("p (t e) -> p t e", e=E)
                    tot = bank7[:, 0:NT * E].rearrange("p (t e) -> p t e", e=E)
                    nc.vector.memset(run[0][:, 0:1, :], 0.0)
                    then(nc.vector.tensor_copy(run[0][:, 1:NT, :], tot[:, 0:NT - 1, :]))
                    src, span = 0, 1
                    while span < NT:
                        nc.vector.tensor_copy(run[1 - src][:, 0:span, :], run[src][:, 0:span, :])
                        then(nc.vector.tensor_tensor(run[1 - src][:, span:, :], run[src][:, span:, :],
                                                     run[src][:, 0:NT - span, :], ALU.add))
                        src, span = 1 - src, 2 * span
                    tokens, tiles, first, end, first_slot = (per_e[:, i] for i in range(5))
                    then(nc.vector.tensor_tensor(tokens, run[src][:, NT - 1, :], tot[:, NT - 1, :], ALU.add))
                    ce = cmp[:, 0:E * NT].rearrange("p (e t) -> p e t", e=E)
                    then(nc.vector.tensor_tensor(ce, tokens.unsqueeze(2).broadcast_to([P, E, NT]),
                                                 count_128[:].unsqueeze(1).broadcast_to([P, E, NT]), ALU.is_gt))
                    then(nc.vector.tensor_reduce(tiles, ce, AX.X, ALU.add))
                    cf = cmp[:, 0:E * E].rearrange("p (e f) -> p e f", e=E)
                    then(nc.vector.tensor_tensor(cf, before[:], tiles.unsqueeze(1).broadcast_to([P, E, E]),
                                                 ALU.mult))
                    then(nc.vector.tensor_reduce(first, cf, AX.X, ALU.add))
                    then(nc.vector.tensor_tensor(end, first, tiles, ALU.add))
                    then(nc.vector.tensor_scalar(first_slot, first, float(P), None, ALU.mult))
                    cs = cmp[:, 0:SLOT_TILES * E].rearrange("p (s e) -> p s e", e=E)
                    then(nc.vector.tensor_tensor(cs, end.unsqueeze(1).broadcast_to([P, SLOT_TILES, E]),
                                                 count_f[:].unsqueeze(2).broadcast_to([P, SLOT_TILES, E]),
                                                 ALU.is_le))
                    then(nc.vector.tensor_reduce(cmp[:, 1024:1024 + SLOT_TILES], cs, AX.X, ALU.add))
                    then(nc.vector.tensor_scalar(expert_of[:], cmp[:, 1024:1024 + SLOT_TILES], float(E - 1), None,
                                                 ALU.min))
                    then(nc.vector.tensor_tensor(run[1 - src][:], run[src][:], pre, ALU.add))
                    then(nc.vector.tensor_tensor(run[src][:], run[1 - src][:],
                                                 first_slot.unsqueeze(1).broadcast_to([P, NT, E]), ALU.add))
                    for k in range(TOP_K):
                        then(nc.vector.tensor_tensor(ck[:, k], chosen[:, k], run[src][:], ALU.mult))
                    then(nc.vector.tensor_reduce(top[:, 3:5], ck, AX.X, ALU.add))
                    then(nc.vector.tensor_copy(slot_of[:].rearrange("p t k -> p k t"), top[:, 3:5]))
                    dve.wait_ge(odds_ready, 1)
                    then(nc.vector.tensor_scalar(top[:, 4], top[:, 5], 1.0, None, ALU.add))
                    then(nc.vector.reciprocal(weight[:, :, 0], top[:, 4]))
                    then(nc.vector.tensor_tensor(weight[:, :, 1], weight[:, :, 0], top[:, 5], ALU.mult))
                    dve.wait_ge(lam_step, 3)
                    nc.vector.tensor_tensor(lam_s[:, 4:5], lam_s[:, 3:4], lam_s[:, 2:3], ALU.subtract
                                            ).then_inc(lam_step, 1)
                    dve.wait_ge(lam_step, 4)
                    nc.vector.tensor_scalar(neg_lam, lam_s[:, 4:5], -L_INIT, None, ALU.add
                                            ).then_inc(lam_step, 1)

                @block.scalar
                def _(act):
                    act.sem_inc(std_ready, 2)
                    act.sem_inc(xnT_ready, 4)
                    act.sem_inc(hi_ready, 2 * QKT)
                    act.sem_inc(v_ready, 8)
                    with act.Fori(0, B) as b:
                        for h in range(2):
                            act.wait_ge(var_ready, credited(b, 2, h))
                            nc.scalar.activation(sd[:], ve[:], ACT.Sqrt).then_inc(std_ready, 1)
                            act.wait_ge(v_bank, credited(b, 8, 4 * h + 3 - 8))
                            for c in range(HC):
                                act.wait_ge(xnT_bank, credited(b, 4, 2 * h + c))
                                nc.scalar.copy(XNT[h][:, c, :], tbank[c]).then_inc(xnT_ready, 1)
                            for i in range(QKT):
                                act.wait_ge(qk_bank, credited(b, 2 * QKT, h * QKT + i))
                                act.wait_ge(parts_stored[i % 4], 16 * (4 * b + 2 * h + i // 4 + 1))
                                scale = 1.0 / math.sqrt(DH) if i < QKT // 2 else 1.0
                                nc.scalar.mul(PARTS[i % 4][:, 0, :], qkbank[i % 4], scale).then_inc(hi_ready, 1)
                            for i in range(CT):
                                act.wait_ge(v_bank, credited(b, 8, 4 * h + i))
                                nc.scalar.copy(V_all[:, bass.ds(b * QT + h * CT + i, 1), :],
                                               vbank[i % 2][:, 0:D].unsqueeze(1)).then_inc(v_ready, 1)
                    act.wait_ge(gap_ready, 1)
                    nc.scalar.activation(top[:, 5], top[:, 2], ACT.Exp).then_inc(odds_ready, 1)
                    act.wait_ge(lam_step, 2)
                    nc.scalar.activation(lam_s[:, 2:4], lam_s[:, 0:2], ACT.Exp).then_inc(lam_step, 1)

                @block.tensor
                def _(pe):
                    pe.sem_inc(xnT_bank, 4)
                    pe.sem_inc(qk_bank, 2 * QKT)
                    pe.sem_inc(v_bank, 8)
                    for h in range(2):
                        pe.sem_inc(xn_stored[h], 16)
                    for i in range(4):
                        pe.sem_inc(parts_stored[i], 16)
                    pe.wait_ge(w_loaded, 96)
                    pe.wait_ge(consts_done, 8)
                    with pe.Fori(0, B) as b:
                        for h in range(2):
                            pe.wait_ge(xn_ready, credited(b, 2, h))
                            for c in range(HC):
                                pe.wait_ge(xnT_ready, credited(b, 4, 2 * h + c - 2))
                                for i in range(CT):
                                    last = nc.tensor.transpose(tbank[c][:, i * P:(i + 1) * P],
                                                               XN[h][:, i, c * P:(c + 1) * P], ident[:])
                                last.then_inc(xnT_bank, 1)
                            pe.wait_ge(xnT_ready, credited(b, 4, 2 * h + 1))
                            for i in range(QKT):
                                pe.wait_ge(lo_ready, credited(b, 2 * QKT, h * QKT + i - 4))
                                for c in range(HC):
                                    last = nc.tensor.matmul(qkbank[i % 4], wqk_sb[:, c, i * P:(i + 1) * P],
                                                            XNT[h][:, c, :], start=(c == 0), stop=(c == HC - 1))
                                last.then_inc(qk_bank, 1)
                            for i in range(CT):
                                pe.wait_ge(logits_ready, credited(b, 8, 4 * h + i - 2))
                                for c in range(HC):
                                    last = nc.tensor.matmul(vbank[i % 2][:, 0:D + E],
                                                            XNT[h][:, c, i * P:(i + 1) * P], wv_sb[:, c, :],
                                                            start=(c == 0), stop=(c == HC - 1))
                                last.then_inc(v_bank, 1)
                    pe.wait_ge(chosen_ready, 1)
                    cb = chosen_b[:].rearrange("p t e -> p (t e)")
                    nc.tensor.matmul(bank6[:, 0:T // P * E], earlier[:], cb, start=True, stop=True)
                    nc.tensor.matmul(bank7[:, 0:T // P * E], ones[:], cb, start=True, stop=True
                                     ).then_inc(ranks_bank, 1)

        with ExitStack() as ph:
            Qs = [sb(f"Qs{u}", [P, 2, S], F32R, where=ph) for u in range(2)]
            Ks = [sb(f"Ks{u}", [P, 2, S], F32R, where=ph) for u in range(2)]
            Vj = [sb(f"Vj{u}", [P, QT, DH], where=ph) for u in range(2)]
            Pr = [sb(f"Pr{i}", [P, 2, S], where=ph) for i in range(4)]
            AT = [sb(f"AT{i}", [P, CH], where=ph) for i in range(4)]
            Ob = [sb(f"Ob{u}", [P, S], where=ph) for u in range(2)]
            dsum = [sb(f"dsum{u}", [P, QT, 2], where=ph) for u in range(2)]
            nmax = sb("nmax", [P, 2 * NQ], where=ph)
            rows = [sb(f"rows{u}", [P, D], where=ph) for u in range(2)]
            row_slot = [sb(f"row_slot{u}", [P, TOP_K], U32, where=ph) for u in range(2)]
            rec = sb("rec", [P, NQ], where=ph)
            coef = sb("coef", [P, NQ], where=ph)

            qk_loaded = [sem(f"qk_loaded{u}") for u in range(2)]
            vj_ready = sem("vj_ready")
            d1_kept = sem("d1_kept")
            rows_loaded = [sem(f"rows_loaded{u}") for u in range(2)]
            row_slot_ready = sem("row_slot_ready")
            scatter_begun = sem("scatter_begun")
            rows_sorted = [sem(f"rows_sorted{u}") for u in range(2)]
            scored = sem("scored")
            maxed = sem("maxed")
            exped = sem("exped")
            rec_done = sem("rec_done")
            coef_done = sem("coef_done")
            combined = sem("combined")
            turned = sem("turned")
            turned_out = sem("turned_out")
            pv_done = sem("pv_done")
            o_out = sem("o_out")
            o_stored = [sem(f"o_stored{u}") for u in range(2)]

            slot = bank
            tb, ob = bank6, bank7

            with nc.Block() as block:
                @block.sync
                def _(sp):

                    def load(it, u):
                        sp.wait_ge(scored, credited(it, STEPS, (STEPS // 2) * (u + 1) - 1 - STEPS))
                        rows = slice(u * 2 * DH, (u + 1) * 2 * DH)
                        for g in range(4):
                            qp = q_parts[it, g % 2, rows, :].rearrange("(m d) t -> d m t", m=2)
                            kp = k_parts[it, g // 2, rows, :].rearrange("(m d) t -> d m t", m=2)
                            sp.dma_start(Qs[u][g * DH:(g + 1) * DH, :, :].bitcast(F32), qp
                                         ).then_inc(qk_loaded[u], 16)
                            sp.dma_start(Ks[u][g * DH:(g + 1) * DH, :, :].bitcast(F32), kp
                                         ).then_inc(qk_loaded[u], 16)

                    def store(it, u):
                        sp.wait_ge(o_out, credited(it, 4, 2 * u + 1))
                        sp.dma_start(o_dram[it * 2 + u], Ob[u][:]).then_inc(o_stored[u], 16)

                    for u in range(2):
                        sp.sem_inc(o_stored[u], 16)
                    for u in range(2):
                        load(0, u)
                    with sp.Fori(0, NIT - 1) as it:
                        for u in range(2):
                            load(it + 1, u)
                            store(it, u)
                    for u in range(2):
                        store(NIT - 1, u)
                    for u in range(2):
                        sp.wait_ge(o_stored[u], 16 * (NIT + 1))

                @block.gpsimd
                def _(pool):
                    pool.sem_inc(vj_ready, 2)
                    pool.sem_inc(d1_kept, 2)
                    xn_v = xn_dram.rearrange("(t p) d -> t p d", p=P)
                    with pool.Fori(0, B) as b:
                        with pool.Fori(0, NH // 2) as jj:
                            it = b * (NH // 2) + jj
                            for u in range(2):
                                pool.wait_ge(pv_done, credited(it, NQ, QT * (u + 1) - 1 - NQ))
                                nc.gpsimd.tensor_copy(
                                    Vj[u][:], V_all[:, bass.ds(b * QT, QT), bass.ds(jj * 2 * DH + u * DH, DH)]
                                ).then_inc(vj_ready, 1)
                            for u in range(2):
                                pool.dma_start(rows[u][:], xn_v[it * 2 + u]).then_inc(rows_loaded[u], 16)
                                nc.gpsimd.tensor_copy(row_slot[u][:].unsqueeze(1),
                                                      slot_of[:, bass.ds(it * 2 + u, 1), :]
                                                      ).then_inc(row_slot_ready, 1)
                            for u in range(2):
                                pool.wait_ge(rows_loaded[u], 16 * (it + 1))
                                pool.wait_ge(row_slot_ready, 2 * it + u + 1)
                                pool.sem_inc(scatter_begun, 1)
                                for k in range(TOP_K):
                                    pool.indirect_dma_start(
                                        xs_dram, bass.IndirectOffsetOnAxis(row_slot[u][:, k:k + 1], 0),
                                        rows[u][:], None).then_inc(rows_sorted[u], 16)
                            for u in range(2):
                                pool.wait_ge(exped, credited(it, STEPS, (STEPS // 2) * (u + 1) - 1))
                                nc.gpsimd.tensor_copy(d1_all[:, bass.ds(it * 2 + u, 1), :],
                                                      dsum[u][:, :, 0].unsqueeze(1)).then_inc(d1_kept, 1)
                            for u in range(2):
                                pool.wait_ge(rows_sorted[u], 32 * (it + 1))

                def score(it, n, m):
                    head, q = divmod(n % NQ, QT)
                    step = 2 * (n % NQ) + m
                    it = it + n // NQ
                    if q == 0 and m == 0:
                        nc.tensor.wait_ge(qk_loaded[head], 16 * 8 * (it + 1))
                    nc.tensor.wait_ge(exped, credited(it, STEPS, slot_user(step)))
                    N = (q + 1) * P
                    for c0 in range(0, N, CH):
                        c1 = min(c0 + CH, N)
                        nc.tensor.matmul(slot[step % 3][:, c0:c1], Qs[head][:, m, q * P:(q + 1) * P],
                                         Ks[head][:, m, c0:c1], start=True, stop=(c1 < N))
                    nc.tensor.matmul(slot[step % 3][:, N - P:N], identb[:], maskb[:], start=False,
                                     stop=True).then_inc(scored, 1)

                def turn(it, n, k):
                    un = units(n)
                    if k >= len(un):
                        return
                    unit, blocks = un[k]
                    if k == 0:
                        nc.tensor.wait_ge(combined, credited(it, NQ, n))
                    nc.tensor.wait_ge(turned_out, credited(it, UNITS, unit - 1))
                    for i, kb in enumerate(blocks):
                        last = nc.tensor.transpose(tb[:, i * P:(i + 1) * P],
                                                   Pr[n % 4][:, 0, kb * P:(kb + 1) * P], ident[:])
                    last.then_inc(turned, 1)

                def values(it, n):
                    head, q = divmod(n, QT)
                    if q == 0:
                        nc.tensor.wait_ge(vj_ready, credited(it, 2, head))
                    if q % 4 == 0:
                        nc.tensor.wait_ge(o_out, credited(it, 4, n // 4 - 1))
                        nc.tensor.matmul(ob[:], zerob[:, 0:P], zerob[:], start=True, stop=False,
                                         skip_group_check=True)
                    for unit, blocks in units(n):
                        nc.tensor.wait_ge(turned_out, credited(it, UNITS, unit))
                        for i, kb in enumerate(blocks):
                            g = kb % 4
                            last = nc.tensor.matmul(
                                ob[DH * g:DH * (g + 1), (q % 4) * P:(q % 4 + 1) * P], Vj[head][:, kb, :],
                                AT[unit % 4][:, i * P:(i + 1) * P], start=False, stop=True,
                                tile_position=(0, DH * g), skip_group_check=True)
                    last.then_inc(pv_done, 1)

                def pe_tile(it, n, ahead=True):
                    turn(it, n, 0)
                    if ahead:
                        score(it, n + 3, 0)
                    turn(it, n, 1)
                    if ahead:
                        score(it, n + 3, 1)
                    values(it, n)

                @block.tensor
                def _(pe):
                    pe.sem_inc(scored, STEPS)
                    pe.sem_inc(turned, UNITS)
                    pe.sem_inc(pv_done, NQ)
                    for n in range(3):
                        for m in range(2):
                            score(0, n, m)
                    with pe.Fori(0, NIT - 1) as it:
                        for n in range(NQ):
                            pe_tile(it, n)
                    for n in range(NQ):
                        pe_tile(NIT - 1, n, ahead=(n + 3 < NQ))

                def exponential(it, n, m):
                    it, n = it + n // NQ, n % NQ
                    head, q = divmod(n, QT)
                    step = 2 * n + m
                    N = (q + 1) * P
                    nc.scalar.wait_ge(maxed, credited(it, STEPS, step))
                    if m == 0:
                        nc.scalar.wait_ge(turned, credited(it, UNITS, units(n - 4)[-1][0] if n >= 4 else
                                                           units(NQ + n - 4)[-1][0] - UNITS))
                        if q == 0:
                            nc.scalar.wait_ge(d1_kept, credited(it, 2, head - 2))
                    nc.scalar.activation(Pr[n % 4][:, m, 0:N], slot[step % 3][:, 0:N], ACT.Exp,
                                         bias=nmax[:, step:step + 1], scale=1.0,
                                         accum_out=dsum[head][:, q, m:m + 1]).then_inc(exped, 1)

                def turn_out(it, n, k):
                    un = units(n)
                    if k >= len(un):
                        return
                    unit, blocks = un[k]
                    nc.scalar.wait_ge(turned, credited(it, UNITS, unit))
                    user = [m for m in range(2 * NQ) if any(
                        (u + (m // NQ) * UNITS) == unit - 4 + UNITS for u, _ in units(m % NQ))][0]
                    nc.scalar.wait_ge(pv_done, credited(it, NQ, user - NQ))
                    w = len(blocks) * P
                    nc.scalar.copy(AT[unit % 4][:, 0:w], tb[:, 0:w]).then_inc(turned_out, 1)

                def out_tile(it, n):
                    head, q = divmod(n, QT)
                    if q % 4 != 3:
                        return
                    nc.scalar.wait_ge(pv_done, credited(it, NQ, n))
                    if q == 3:
                        nc.scalar.wait_ge(o_stored[head], 16 * (it + 1))
                    nc.scalar.copy(Ob[head][:, (q // 4) * CH:(q // 4 + 1) * CH], ob[:]).then_inc(o_out, 1)

                def act_tile(it, n, ahead=True):
                    turn_out(it, n, 0)
                    if ahead:
                        exponential(it, n + 2, 0)
                    turn_out(it, n, 1)
                    if ahead:
                        exponential(it, n + 2, 1)
                    out_tile(it, n)

                @block.scalar
                def _(act):
                    act.sem_inc(exped, STEPS)
                    act.sem_inc(turned_out, UNITS)
                    act.sem_inc(o_out, 4)
                    for n in range(2):
                        for m in range(2):
                            exponential(0, n, m)
                    with act.Fori(0, NIT - 1) as it:
                        for n in range(NQ):
                            act_tile(it, n)
                    for n in range(NQ):
                        act_tile(NIT - 1, n, ahead=(n + 2 < NQ))

                def maximum(it, n, m):
                    it, n = it + n // NQ, n % NQ
                    q = n % QT
                    step = 2 * n + m
                    nc.vector.wait_ge(scored, credited(it, STEPS, step))
                    nc.vector.tensor_reduce(nmax[:, step:step + 1], slot[step % 3][:, 0:(q + 1) * P], AX.X,
                                            ALU.max, negate=True).then_inc(maxed, 1)

                def combine(it, n):
                    it, n = it + n // NQ, n % NQ
                    head, q = divmod(n, QT)
                    N = (q + 1) * P
                    nc.vector.wait_ge(exped, credited(it, STEPS, 2 * n + 1))
                    nc.vector.reciprocal(rec[:, n:n + 1], dsum[head][:, q, 1:2]).then_inc(rec_done, 1)
                    nc.vector.wait_ge(rec_done, credited(it, NQ, n))
                    nc.vector.tensor_scalar(coef[:, n:n + 1], rec[:, n:n + 1], neg_lam,
                                            dsum[head][:, q, 0:1], ALU.mult, ALU.mult).then_inc(coef_done, 1)
                    nc.vector.wait_ge(coef_done, credited(it, NQ, n))
                    nc.vector.scalar_tensor_tensor(
                        out=Pr[n % 4][:, 0, 0:N], in0=Pr[n % 4][:, 1, 0:N], scalar=coef[:, n:n + 1],
                        in1=Pr[n % 4][:, 0, 0:N], op0=ALU.mult, op1=ALU.add).then_inc(combined, 1)

                @block.vector
                def _(dve):
                    dve.sem_inc(maxed, STEPS)
                    dve.sem_inc(rec_done, NQ)
                    dve.sem_inc(coef_done, NQ)
                    dve.sem_inc(combined, NQ)
                    for n in range(2):
                        for m in range(2):
                            maximum(0, n, m)
                    combine(0, 0)
                    with dve.Fori(0, NIT - 1) as it:
                        for n in range(NQ):
                            maximum(it, n + 2, 0)
                            maximum(it, n + 2, 1)
                            combine(it, n + 1)
                    for n in range(NQ):
                        if n + 2 < NQ:
                            maximum(NIT - 1, n + 2, 0)
                            maximum(NIT - 1, n + 2, 1)
                        if n + 1 < NQ:
                            combine(NIT - 1, n + 1)


        with ExitStack() as ph:
            xs = [sb(f"xs{u}", [P, D], where=ph) for u in range(2)]
            xsT = [sb(f"xsT{u}", [P, HC, P], where=ph) for u in range(2)]
            hid = [sb(f"hid{u}", [P, 2 * I], where=ph) for u in range(2)]
            gate_tanh = [sb(f"gate_tanh{u}", [P, I], where=ph) for u in range(2)]
            glu = [sb(f"glu{u}", [P, I], where=ph) for u in range(2)]
            up = [sb(f"up{u}", [P, I], where=ph) for u in range(2)]
            act_in = [sb(f"act_in{u}", [P, I], where=ph) for u in range(2)]
            act_T = [sb(f"act_T{u}", [P, HC, P], where=ph) for u in range(2)]
            ys = [sb(f"ys{u}", [P, D], where=ph) for u in range(2)]

            xs_loaded = [sem(f"xs_loaded{u}") for u in range(2)]
            xs_turned = sem("xs_turned")
            xsT_ready = sem("xsT_ready")
            hid_bank = sem("hid_bank")
            hid_ready = sem("hid_ready")
            gate_ready = sem("gate_ready")
            tanh_ready = sem("tanh_ready")
            glu_ready = sem("glu_ready")
            up_ready = sem("up_ready")
            act_ready = sem("act_ready")
            act_turned = sem("act_turned")
            act_T_ready = sem("act_T_ready")
            y_bank = sem("y_bank")
            y_ready = sem("y_ready")
            y_stored = [sem(f"y_stored{u}") for u in range(2)]

            hbank = [bank[0][:, 0:CH], bank[0][:, CH:]]
            xbank = [bank[1][:, 0:CH], bank[1][:, CH:]]
            abank = [bank[2][:, 0:CH], bank[2][:, CH:]]
            ybank = [bank6, bank7]
            NIT3 = SLOT_TILES // 2

            def seen(it, u):
                return credited(it, 2, u)

            with nc.Block() as block:
                xs_v = xs_dram.rearrange("(n u p) d -> n u p d", u=2, p=P)
                ys_v = ys_dram.rearrange("(n u p) d -> n u p d", u=2, p=P)

                @block.sync
                def _(sp):
                    def load(it, u):
                        sp.wait_ge(xs_turned, seen(it, u - 2))
                        sp.dma_start(xs[u][:], xs_v[it, u]).then_inc(xs_loaded[u], 16)

                    with sp.Fori(0, NIT3) as it:
                        for u in range(2):
                            load(it, u)

                def expert(eng, it, u):
                    return eng.value_load(expert_of[0:1, bass.ds(it * 2 + u, 1)], min_val=0, max_val=E - 1)

                def there(it, n):
                    return not isinstance(it, int) or 0 <= 2 * it + n < SLOT_TILES

                def run_steps(eng, step):
                    step(0, 0)
                    with eng.Fori(0, NIT3 - 2) as it:
                        step(it, 1)
                        step(it, 2)
                    for n in (1, 2, 3, 4):
                        step(NIT3 - 2, n)

                def turn_rows(it, n):
                    if not there(it, n):
                        return
                    it, u = it + n // 2, n % 2
                    nc.tensor.wait_ge(xs_loaded[u], 16 * (it + 1))
                    nc.tensor.wait_ge(xsT_ready, seen(it, u - 2))
                    for c in range(HC):
                        last = nc.tensor.transpose(xbank[u][:, c * P:(c + 1) * P], xs[u][:, c * P:(c + 1) * P],
                                                   ident[:])
                    last.then_inc(xs_turned, 1)

                def gate_and_up(it, n):
                    if not there(it, n):
                        return
                    it, u = it + n // 2, n % 2
                    e = expert(nc.tensor, it, u)
                    nc.tensor.wait_ge(xsT_ready, seen(it, u))
                    nc.tensor.wait_ge(hid_ready, seen(it, u - 2))
                    for c in range(HC):
                        last = nc.tensor.matmul(hbank[u], xsT[u][:, c, :],
                                                gu_sb[:, c, bass.ds(e, 1), :].rearrange("p o n -> p (o n)"),
                                                start=(c == 0), stop=(c == HC - 1))
                    last.then_inc(hid_bank, 1)

                def turn_act(it, n):
                    if not there(it, n):
                        return
                    it, u = it + n // 2, n % 2
                    nc.tensor.wait_ge(act_ready, seen(it, u))
                    nc.tensor.wait_ge(act_T_ready, seen(it, u - 2))
                    for c in range(HC):
                        last = nc.tensor.transpose(abank[u][:, c * P:(c + 1) * P],
                                                   act_in[u][:, c * P:(c + 1) * P], ident[:])
                    last.then_inc(act_turned, 1)

                def down(it, n):
                    if not there(it, n):
                        return
                    it, u = it + n // 2, n % 2
                    e = expert(nc.tensor, it, u)
                    nc.tensor.wait_ge(act_T_ready, seen(it, u))
                    nc.tensor.wait_ge(y_ready, seen(it, u - 2))
                    for c in range(HC):
                        last = nc.tensor.matmul(ybank[u][:, 0:D], act_T[u][:, c, :],
                                                dn_sb[:, c, bass.ds(e, 1), :].rearrange("p o n -> p (o n)"),
                                                start=(c == 0), stop=(c == HC - 1))
                    last.then_inc(y_bank, 1)

                @block.tensor
                def _(pe):
                    for s in (xs_turned, hid_bank, act_turned, y_bank):
                        pe.sem_inc(s, 2)
                    pe.wait_ge(ew_loaded, 64)
                    turn_rows(0, 0)
                    turn_rows(0, 1)
                    gate_and_up(0, 0)

                    def step(it, n):
                        turn_rows(it, n + 2)
                        gate_and_up(it, n + 1)
                        down(it, n - 1)
                        turn_act(it, n)

                    run_steps(pe, step)

                def rows_out(it, n):
                    if not there(it, n):
                        return
                    it, u = it + n // 2, n % 2
                    nc.scalar.wait_ge(xs_turned, seen(it, u))
                    nc.scalar.wait_ge(hid_bank, seen(it, u - 2))
                    nc.scalar.copy(xsT[u][:].rearrange("p c n -> p (c n)"), xbank[u][:, 0:HC * P]
                                   ).then_inc(xsT_ready, 1)

                def gate_curve(it, n):
                    if not there(it, n):
                        return
                    it, u = it + n // 2, n % 2
                    nc.scalar.wait_ge(gate_ready, seen(it, u))
                    nc.scalar.wait_ge(glu_ready, seen(it, u - 2))
                    nc.scalar.activation(gate_tanh[u][:], hid[u][:, 0:I], ACT.Tanh, scale=ALPHA / 2
                                         ).then_inc(tanh_ready, 1)

                def act_out(it, n):
                    if not there(it, n):
                        return
                    it, u = it + n // 2, n % 2
                    nc.scalar.wait_ge(act_turned, seen(it, u))
                    nc.scalar.wait_ge(y_bank, seen(it, u - 2))
                    nc.scalar.copy(act_T[u][:].rearrange("p c n -> p (c n)"), abank[u][:, 0:HC * P]
                                   ).then_inc(act_T_ready, 1)

                def store(it, n):
                    if not there(it, n):
                        return
                    it, u = it + n // 2, n % 2
                    nc.scalar.wait_ge(y_ready, seen(it, u))
                    nc.scalar.dma_start(ys_v[it, u], ys[u][:]).then_inc(y_stored[u], 16)

                @block.scalar
                def _(act):
                    for u in range(2):
                        act.sem_inc(y_stored[u], 16)
                    for s in (xsT_ready, tanh_ready, act_T_ready):
                        act.sem_inc(s, 2)
                    rows_out(0, 0)
                    rows_out(0, 1)
                    gate_curve(0, 0)

                    def step(it, n):
                        rows_out(it, n + 2)
                        gate_curve(it, n + 1)
                        store(it, n - 1)
                        act_out(it, n)

                    run_steps(act, step)
                    for u in range(2):
                        act.wait_ge(y_stored[u], 16 * (NIT3 + 1))

                def hidden(it, n):
                    if not there(it, n):
                        return
                    it, u = it + n // 2, n % 2
                    e = expert(nc.vector, it, u)
                    nc.vector.wait_ge(hid_bank, seen(it, u))
                    nc.vector.tensor_tensor(hid[u][:], hbank[u],
                                            gub_sb[:, bass.ds(e, 1), :].rearrange("p o n -> p (o n)"), ALU.add
                                            ).then_inc(hid_ready, 1)

                def gate(it, n):
                    if not there(it, n):
                        return
                    it, u = it + n // 2, n % 2
                    nc.vector.wait_ge(hid_ready, seen(it, u))
                    nc.vector.tensor_scalar(hid[u][:, 0:I], hid[u][:, 0:I], LIMIT, None, ALU.min
                                            ).then_inc(gate_ready, 1)

                def activate(it, n):
                    if not there(it, n):
                        return
                    it, u = it + n // 2, n % 2
                    nc.vector.wait_ge(tanh_ready, seen(it, u))
                    nc.vector.scalar_tensor_tensor(out=glu[u][:], in0=gate_tanh[u][:], scalar=1.0,
                                                   in1=hid[u][:, 0:I], op0=ALU.add, op1=ALU.mult
                                                   ).then_inc(glu_ready, 1)
                    nc.vector.tensor_scalar(up[u][:], hid[u][:, I:], LIMIT, -LIMIT, ALU.min, ALU.max
                                            ).then_inc(up_ready, 1)
                    nc.vector.wait_ge(glu_ready, seen(it, u))
                    nc.vector.wait_ge(up_ready, seen(it, u))
                    nc.vector.wait_ge(act_turned, seen(it, u - 2))
                    nc.vector.scalar_tensor_tensor(out=act_in[u][:], in0=up[u][:], scalar=1.0, in1=glu[u][:],
                                                   op0=ALU.add, op1=ALU.mult).then_inc(act_ready, 1)

                def output(it, n):
                    if not there(it, n):
                        return
                    it, u = it + n // 2, n % 2
                    e = expert(nc.vector, it, u)
                    nc.vector.wait_ge(y_bank, seen(it, u))
                    nc.vector.wait_ge(y_stored[u], 16 * (it + 1))
                    nc.vector.scalar_tensor_tensor(out=ys[u][:], in0=ybank[u][:, 0:D], scalar=0.5,
                                                   in1=dnb_sb[:, bass.ds(e, 1), :].rearrange("p o n -> p (o n)"),
                                                   op0=ALU.mult, op1=ALU.add).then_inc(y_ready, 1)

                @block.vector
                def _(dve):
                    for s in (hid_ready, gate_ready, glu_ready, up_ready, act_ready, y_ready):
                        dve.sem_inc(s, 2)
                    hidden(0, 0)
                    gate(0, 0)

                    def step(it, n):
                        activate(it, n)
                        hidden(it, n + 1)
                        output(it, n - 1)
                        gate(it, n + 1)

                    run_steps(dve, step)

        with ExitStack() as ph:
            Oq = [sb(f"Oq{h}", [P, NH, CH], where=ph) for h in range(2)]
            xr = [sb(f"xr{h}", [P, CT, D], where=ph) for h in range(2)]
            yg = [sb(f"yg{h}", [P, CT, TOP_K, D], where=ph) for h in range(2)]
            yslot = [sb(f"yslot{h}", [P, CT, TOP_K], U32, where=ph) for h in range(2)]
            yw = [sb(f"yw{h}", [P, CT, TOP_K], where=ph) for h in range(2)]
            d1x = sb("d1x", [P, NH, CT], where=ph)
            d1e = sb("d1e", [P, CT, NH], where=ph)
            d1b = sb("d1b", [P, CT, NH, DH], where=ph)
            Oc = sb("Oc", [P, HC, CH], where=ph)
            sq = sb("sq", [P, HC, CH], where=ph)
            root = sb("root", [P, HC, CH], where=ph)
            On = sb("On", [P, HC, CH], where=ph)
            att = sb("att", [P, CT, D], where=ph)
            ff = sb("ff", [P, CT, D], where=ph)
            ft = sb("ft", [P, CT, D], where=ph)
            res = [sb(f"res{h}", [P, CT, D], where=ph) for h in range(2)]

            c_loaded = [sem(f"c_loaded{h}") for h in range(2)]
            picked = sem("picked")
            gather_begun = sem("gather_begun")
            y_gathered = [sem(f"y_gathered{h}") for h in range(2)]
            oc_bank = sem("oc_bank")
            oc_ready = sem("oc_ready")
            ms_bank = sem("ms_bank")
            root_ready = sem("root_ready")
            recip_ready = sem("recip_ready")
            on_ready = sem("on_ready")
            att_bank = sem("att_bank")
            att_ready = sem("att_ready")
            d1_step = sem("d1_step")
            d1_ready = sem("d1_ready")
            ff_half = sem("ff_half")
            ff_ready = sem("ff_ready")
            ft_ready = sem("ft_ready")
            tail = sem("tail")
            res_ready = sem("res_ready")
            stored = [sem(f"stored{h}") for h in range(2)]
            obank = [bank[0][:, 0:CH], bank[0][:, CH:]]
            mbank = [bank[1][:, 0:CH], bank[1][:, CH:]]
            wbank = [bank[2][:, 0:CH], bank[2][:, CH:]]

            with nc.Block() as block:
                @block.sync
                def _(sp):
                    x_v = x.rearrange("(b h t p) d -> b h p t d", b=B, h=2, p=P)
                    o_v = o_dram.rearrange("(b j) p (h n) -> b h p j n", b=B, h=2)
                    out_v = out.rearrange("(b h t p) d -> b h p t d", b=B, h=2, p=P)

                    def load(b, h):
                        sp.dma_start(Oq[h][:], o_v[b, h]).then_inc(c_loaded[h], 16)
                        sp.dma_start(xr[h][:], x_v[b, h]).then_inc(c_loaded[h], 16)

                    def store(b, h):
                        sp.wait_ge(res_ready, credited(b, 2, h))
                        sp.dma_start(out_v[b, h], res[h][:]).then_inc(stored[h], 16)

                    for h in range(2):
                        sp.sem_inc(stored[h], 16)
                        load(0, h)
                    with sp.Fori(0, B - 1) as b:
                        for h in range(2):
                            store(b, h)
                            load(b + 1, h)
                    for h in range(2):
                        store(B - 1, h)
                    for h in range(2):
                        sp.wait_ge(stored[h], 16 * (B + 1))

                @block.gpsimd
                def _(pool):
                    pool.sem_inc(picked, 4)
                    with pool.Fori(0, B) as b:
                        for h in range(2):
                            pool.wait_ge(res_ready, credited(b, 2, h - 2))
                            c = b * QT + h * CT
                            nc.gpsimd.tensor_copy(yslot[h][:], slot_of[:, bass.ds(c, CT), :]).then_inc(picked, 1)
                            nc.gpsimd.tensor_copy(yw[h][:], weight[:, bass.ds(c, CT), :]).then_inc(picked, 1)
                            pool.wait_ge(picked, credited(b, 4, 2 * h + 1))
                            pool.sem_inc(gather_begun, 1)
                            for i in range(CT):
                                for k in range(TOP_K):
                                    pool.indirect_dma_start(
                                        yg[h][:, i, k, :], None, ys_dram,
                                        bass.IndirectOffsetOnAxis(yslot[h][:, i, k:k + 1], 0)
                                    ).then_inc(y_gathered[h], 16)

                @block.tensor
                def _(pe):
                    for s in (oc_bank, ms_bank, att_bank):
                        pe.sem_inc(s, 4)
                    with pe.Fori(0, B) as b:
                        for h in range(2):
                            pe.wait_ge(c_loaded[h], 32 * (b + 1))
                            for t in range(HC):
                                pe.wait_ge(oc_ready, credited(b, 4, 2 * h + t - 2))
                                for j in range(4):
                                    last = nc.tensor.matmul(obank[t], gather4[:, 96 - DH * j:224 - DH * j],
                                                            Oq[h][:, 4 * t + j, :], start=(j == 0), stop=(j == 3))
                                last.then_inc(oc_bank, 1)
                            pe.wait_ge(d1_ready, credited(b, 2, h))
                            for t in range(HC):
                                pe.wait_ge(oc_ready, credited(b, 4, 2 * h + t))
                                pe.wait_ge(root_ready, credited(b, 4, 2 * h + t - 2))
                                nc.tensor.matmul(mbank[t], group_mean[:], sq[:, t, :], start=True, stop=False)
                                for i in range(CT):
                                    last = nc.tensor.matmul(
                                        mbank[t][:, i * P:(i + 1) * P],
                                        d1b[:, i, 4 * t:4 * t + 4, :].rearrange("p j d -> p (j d)"), ident[:],
                                        start=False, stop=(i == CT - 1))
                                last.then_inc(ms_bank, 1)
                            pe.wait_ge(on_ready, credited(b, 4, 2 * h + 1))
                            for k in range(2):
                                pe.wait_ge(att_ready, credited(b, 4, 2 * h + k - 2))
                                for t in range(2):
                                    i = 2 * k + t
                                    for c in range(HC):
                                        last = nc.tensor.matmul(wbank[k][:, t * D:(t + 1) * D],
                                                                On[:, c, i * P:(i + 1) * P], wo_sb[:, c, :],
                                                                start=(c == 0), stop=(c == HC - 1))
                                last.then_inc(att_bank, 1)

                @block.scalar
                def _(act):
                    for s in (oc_ready, root_ready, att_ready):
                        act.sem_inc(s, 4)
                    act.sem_inc(ft_ready, 2)
                    with act.Fori(0, B) as b:
                        for h in range(2):
                            for t in range(HC):
                                act.wait_ge(oc_bank, credited(b, 4, 2 * h + t))
                                act.wait_ge(on_ready, credited(b, 4, 2 * h + t - 2))
                                nc.scalar.copy(Oc[:, t, :], obank[t])
                                nc.scalar.activation(sq[:, t, :], obank[t], ACT.Square).then_inc(oc_ready, 1)
                            for t in range(HC):
                                act.wait_ge(ms_bank, credited(b, 4, 2 * h + t))
                                nc.scalar.activation(root[:, t, :], mbank[t], ACT.Sqrt).then_inc(root_ready, 1)
                            act.wait_ge(res_ready, credited(b, 2, h - 1))
                            for k in range(2):
                                act.wait_ge(att_bank, credited(b, 4, 2 * h + k))
                                nc.scalar.copy(att[:, 2 * k:2 * k + 2, :],
                                               wbank[k].rearrange("p (t d) -> p t d", t=2)).then_inc(att_ready, 1)
                            act.wait_ge(ff_ready, credited(b, 2, h))
                            nc.scalar.activation(ft[:], ff[:], ACT.Tanh, scale=0.5).then_inc(ft_ready, 1)

                @block.vector
                def _(dve):
                    for s in (d1_step, recip_ready, on_ready, tail):
                        dve.sem_inc(s, 4)
                    for s in (d1_ready, ff_half, ff_ready, res_ready):
                        dve.sem_inc(s, 2)
                    with dve.Fori(0, B) as b:
                        for h in range(2):
                            nc.vector.tensor_copy(d1x[:], d1_all[:, bass.ds(b * NH, NH), h * CT:(h + 1) * CT]
                                                  ).then_inc(d1_step, 1)
                            dve.wait_ge(d1_step, credited(b, 4, 2 * h))
                            nc.vector.scalar_tensor_tensor(out=d1e[:].rearrange("p i j -> p j i"), in0=d1x[:],
                                                           scalar=RMS_EPS, in1=d1x[:], op0=ALU.mult, op1=ALU.mult
                                                           ).then_inc(d1_step, 1)
                            dve.wait_ge(d1_step, credited(b, 4, 2 * h + 1))
                            dve.wait_ge(ms_bank, credited(b, 4, 2 * h - 1))
                            nc.vector.tensor_copy(
                                d1b[:].rearrange("p i j d -> p (i j) d"),
                                d1e[:].rearrange("p i j -> p (i j)").unsqueeze(2).broadcast_to([P, CT * NH, DH])
                            ).then_inc(d1_ready, 1)
                            dve.wait_ge(y_gathered[h], 16 * CT * TOP_K * (b + 1))
                            dve.wait_ge(picked, credited(b, 4, 2 * h + 1))
                            for i in range(CT):
                                last = nc.vector.tensor_scalar(ff[:, i, :], yg[h][:, i, 0, :], yw[h][:, i, 0:1], None,
                                                               ALU.mult)
                            last.then_inc(ff_half, 1)
                            dve.wait_ge(ff_half, credited(b, 2, h))
                            for i in range(CT):
                                last = nc.vector.scalar_tensor_tensor(
                                    out=ff[:, i, :], in0=yg[h][:, i, 1, :], scalar=yw[h][:, i, 1:2],
                                    in1=ff[:, i, :], op0=ALU.mult, op1=ALU.add)
                            last.then_inc(ff_ready, 1)
                            for t in range(HC):
                                dve.wait_ge(root_ready, credited(b, 4, 2 * h + t))
                                nc.vector.reciprocal(root[:, t, :], root[:, t, :]).then_inc(recip_ready, 1)
                                dve.wait_ge(recip_ready, credited(b, 4, 2 * h + t))
                                dve.wait_ge(att_bank, credited(b, 4, 2 * h - 1))
                                nc.vector.scalar_tensor_tensor(out=On[:, t, :], in0=Oc[:, t, :],
                                                               scalar=1.0 - L_INIT, in1=root[:, t, :],
                                                               op0=ALU.mult, op1=ALU.mult).then_inc(on_ready, 1)
                            dve.wait_ge(ft_ready, credited(b, 2, h))
                            nc.vector.scalar_tensor_tensor(out=ft[:], in0=ft[:], scalar=1.0, in1=ff[:],
                                                           op0=ALU.add, op1=ALU.mult).then_inc(tail, 1)
                            dve.wait_ge(tail, credited(b, 4, 2 * h))
                            dve.wait_ge(att_ready, credited(b, 4, 2 * h + 1))
                            nc.vector.tensor_tensor(ft[:], ft[:], att[:], ALU.mult).then_inc(tail, 1)
                            dve.wait_ge(tail, credited(b, 4, 2 * h + 1))
                            dve.wait_ge(c_loaded[h], 32 * (b + 1))
                            dve.wait_ge(stored[h], 16 * (b + 1))
                            nc.vector.scalar_tensor_tensor(out=res[h][:], in0=ft[:], scalar=0.5, in1=xr[h][:],
                                                           op0=ALU.mult, op1=ALU.add).then_inc(res_ready, 1)


def kernel(L0_attn_x, L0_attn_l_q1, L0_attn_l_k1, L0_attn_l_q2, L0_attn_l_k2, L0_attn_wq, L0_attn_wk, L0_attn_wv,
           L0_attn_wo, L0_ffn_router_weight, L0_ffn_router_bias, L0_ffn_gate_up_proj, L0_ffn_gate_up_proj_bias,
           L0_ffn_down_proj, L0_ffn_down_proj_bias):
    import numpy as np
    import concourse.bacc as bacc
    from concourse.bass_utils import run_bass_kernel_spmd

    def heads(w):
        return np.asarray(w).reshape(2, NH, DH, D).transpose(3, 1, 0, 2).reshape(D, 2 * NH * DH)

    arrays = {
        "x": np.asarray(L0_attn_x).reshape(T, D),
        "wqk": np.concatenate([heads(L0_attn_wq), heads(L0_attn_wk)], axis=1),
        "wv": np.asarray(L0_attn_wv).T,
        "wo": np.asarray(L0_attn_wo).T,
        "lam": np.stack([np.asarray(a) for a in (L0_attn_l_q1, L0_attn_l_k1, L0_attn_l_q2, L0_attn_l_k2)]),
        "rw": np.asarray(L0_ffn_router_weight).T,
        "rb": np.asarray(L0_ffn_router_bias),
        "gu": np.asarray(L0_ffn_gate_up_proj).reshape(E, D, I, 2).transpose(1, 0, 3, 2).reshape(D, E, 2 * I),
        "gub": np.asarray(L0_ffn_gate_up_proj_bias).reshape(E, I, 2).transpose(0, 2, 1).reshape(E, 2 * I),
        "dn": np.asarray(L0_ffn_down_proj).transpose(1, 0, 2),
        "dnb": np.asarray(L0_ffn_down_proj_bias),
    }
    arrays = {name: np.ascontiguousarray(a) for name, a in arrays.items()}
    nc = bacc.Bacc("TRN2", target_bir_lowering=False, num_devices=1)
    args = [nc.dram_tensor(name, a.shape, mybir.dt.from_np(a.dtype), kind="ExternalInput").ap()
            for name, a in arrays.items()]
    out = nc.dram_tensor("out", (T, D), F32, kind="ExternalOutput").ap()
    build(nc, *args, out)
    r = run_bass_kernel_spmd(nc, [arrays], core_ids=[0])
    return r.results[0]["out"].reshape(B, S, D)
```

```python
import math
from contextlib import ExitStack

import concourse.bass as bass
from concourse import mybir

F32 = mybir.dt.float32
F32R = mybir.dt.float32r
BF16 = mybir.dt.bfloat16
U32 = mybir.dt.uint32
I32 = mybir.dt.int32
ALU = mybir.AluOpType
ACT = mybir.ActivationFunctionType
AX = mybir.AxisListType

B, S, D = 4, 1024, 256
NH, DH = 8, 32
T = B * S
E, I, LIMIT, ALPHA = 8, 256, 7.0, 1.702
L_INIT = 0.8 - 0.6 * math.exp(-0.3 * 1)
LN_EPS, RMS_EPS = 1e-5, 1e-6
GROUP = DH // NH
P = 128
HC = D // P
CH = 512
CT = CH // P
NCH = T // CH
QT = S // P
MASKED = -1.0e30

QKT = 2 * 2 * NH * DH // P
NIT = B * NH // 2
STEPS = 2 * 2 * QT
NQ = 2 * QT
TOP_K = 2
SLOT_TILES = T * TOP_K // P + E
KB_UNIT = 4


def credited(it, per, event):
    return (it + 1) * per + event + 1


ORDER = [q for pair in zip(range(QT // 2, QT), range(QT // 2)) for q in pair]
USES = 2 * 3 * QT // 2
SLOTS = 3


def query(n):
    return n % NQ // QT, ORDER[n % QT]


def uses(n):
    first = 3 * (n // 2)
    return [(first, [0]), (first + 1, [1])] if n % 2 == 0 else [(first + 2, [0, 1])]


def last_step(use):
    pair, k = divmod(use, 3)
    return 4 * pair + [0, 1, 3][k]


def gathers(n):
    return [(n - 5) // 4] if n % 4 == 1 else []


def units(n):
    count = sum(-(-(query(i)[1] + 1) // KB_UNIT) for i in range(n))
    first = count + sum(len(gathers(i)) for i in range(n))
    blocks = list(range(query(n)[1] + 1))
    return [(first + k, count + k, blocks[KB_UNIT * k:KB_UNIT * (k + 1)])
            for k in range(-(-len(blocks) // KB_UNIT))]


UNITS = units(NQ - 1)[-1][1] + 1
FILLS = UNITS + 4


def build(nc, x, wqk, wv, wo, lam, rw, rb, gu, gub, dn, dnb, out):
    with ExitStack() as ctx:
        def sb(name, shape, dt=F32, where=ctx):
            return where.enter_context(nc.sbuf_tensor(name, shape, dt))

        def sem(name):
            return ctx.enter_context(nc.semaphore(name))

        q_parts = nc.dram_tensor("q_parts", (NIT, 2, P, S), F32, kind="Internal").ap()
        k_parts = nc.dram_tensor("k_parts", (NIT, 2, P, S), F32, kind="Internal").ap()
        xn_dram = nc.dram_tensor("xn_dram", (T, D), F32, kind="Internal").ap()
        xs_dram = nc.dram_tensor("xs_dram", (SLOT_TILES * P, D), F32, kind="Internal").ap()
        ys_dram = nc.dram_tensor("ys_dram", (SLOT_TILES * P, D), F32, kind="Internal").ap()

        bank = [ctx.enter_context(nc.psum_tensor(f"bank{i}", [P, 2 * CH], F32)) for i in range(3)]
        bank6 = ctx.enter_context(nc.psum_tensor("bank6", [P, CH], F32))
        bank7 = ctx.enter_context(nc.psum_tensor("bank7", [P, CH], F32))

        ident = sb("ident", [P, P])
        identb = sb("identb", [P, P], BF16)
        maskb = sb("maskb", [P, P], BF16)
        zerob = sb("zerob", [P, CH], BF16)
        gather4 = sb("gather4", [P, DH])
        VO = sb("VO", [P, NIT, QT, 2 * DH])
        d1_all = sb("d1_all", [P, B * NH, QT])
        lam_in = sb("lam_in", [P, 4, NH])
        lam_w = sb("lam_w", [P, 2, NH])
        lam_s = sb("lam_s", [P, 8])
        neg_lam = lam_s[:, 6:7]
        wo_sb = sb("wo_sb", [P, HC, D])
        gu_sb = sb("gu_sb", [P, HC, E, 2 * I])
        dn_sb = sb("dn_sb", [P, HC, E, D])
        gub_sb = sb("gub_sb", [P, E, 2 * I])
        dnb_sb = sb("dnb_sb", [P, E, D])
        weight = sb("weight", [P, T // P, TOP_K])
        slot_of = sb("slot_of", [P, T // P, TOP_K], U32)
        expert_rows = sb("expert_rows", [P, SLOT_TILES // 2, 4], I32)

        consts_done = sem("consts_done")
        lam_step = sem("lam_step")
        ew_loaded = sem("ew_loaded")
        const_step = sem("const_step")

        with ExitStack() as ph:
            wqk_sb = sb("wqk_sb", [P, HC, QKT * P], where=ph)
            wv_sb = sb("wv_sb", [P, HC, D + E], where=ph)
            rb_sb = sb("rb_sb", [P, E], where=ph)
            zeros = sb("zeros", [P, SLOT_TILES // NCH * D], where=ph)
            before = sb("before", [P, E, E], where=ph)
            earlier = sb("earlier", [P, P], BF16, where=ph)
            ones = sb("ones", [P, P], BF16, where=ph)
            count_i = sb("count_i", [P, SLOT_TILES], I32, where=ph)
            count_f = sb("count_f", [P, SLOT_TILES], where=ph)
            count_128 = sb("count_128", [P, T // P], where=ph)
            logits = sb("logits", [P, T // P, E], where=ph)
            cmp = sb("cmp", [P, T // P * E * TOP_K + 2 * SLOT_TILES * E], where=ph)
            ranks = sb("ranks", [P, 3, QT, E], where=ph)
            chosen = sb("chosen", [P, TOP_K, T // P, E], where=ph)
            chosen_b = sb("chosen_b", [P, T // P, E], BF16, where=ph)
            top = sb("top", [P, 6, T // P], where=ph)
            run = [sb(f"run{i}", [P, T // P, E], where=ph) for i in range(2)]
            per_e = sb("per_e", [P, 8, E], where=ph)
            X = [sb(f"X{h}", [P, CT, D], where=ph) for h in range(2)]
            XN = [sb(f"XN{h}", [P, CT, D], where=ph) for h in range(2)]
            XNT = [sb(f"XNT{h}", [P, HC, CH], where=ph) for h in range(2)]
            PARTS = [sb(f"PARTS{i}", [P, 2, CH], F32R, where=ph) for i in range(4)]
            stats = sb("stats", [P, CT, 6], where=ph)
            mv = sb("mv", [P, CT, 2], where=ph)
            ve = sb("ve", [P, CT], where=ph)
            sd = sb("sd", [P, CT], where=ph)
            rs = sb("rs", [P, CT], where=ph)
            nt = sb("nt", [P, CT], where=ph)

            w_loaded = sem("w_loaded")
            x_loaded = [sem(f"x_loaded{h}") for h in range(2)]
            ln_step = sem("ln_step")
            stats_seen = sem("stats_seen")
            var_ready = sem("var_ready")
            std_ready = sem("std_ready")
            xn_ready = sem("xn_ready")
            xnT_bank = sem("xnT_bank")
            xnT_ready = sem("xnT_ready")
            qk_bank = sem("qk_bank")
            hi_ready = sem("hi_ready")
            lo_ready = sem("lo_ready")
            v_bank = sem("v_bank")
            v_ready = sem("v_ready")
            parts_stored = [sem(f"parts_stored{i}") for i in range(4)]
            xn_stored = [sem(f"xn_stored{h}") for h in range(2)]
            logits_ready = sem("logits_ready")
            zeros_ready = sem("zeros_ready")
            zeros_stored = sem("zeros_stored")
            rank_step = sem("rank_step")
            route = sem("route")
            chosen_ready = sem("chosen_ready")
            ranks_bank = sem("ranks_bank")
            gap_ready = sem("gap_ready")
            odds_ready = sem("odds_ready")

            tbank = [bank[0][:, 0:CH], bank[0][:, CH:]]
            qkbank = [bank[1][:, 0:CH], bank[1][:, CH:], bank[2][:, 0:CH], bank[2][:, CH:]]
            vbank = [bank6, bank7]
            LN_OPS = 13
            RANK_OPS = 11

            with nc.Block() as block:
                @block.gpsimd
                def _(pool):
                    nc.gpsimd.memset(ident[:], 0.0).then_inc(const_step, 1)
                    nc.gpsimd.memset(maskb[:], 0.0).then_inc(const_step, 1)
                    nc.gpsimd.memset(gather4[:], 0.0).then_inc(const_step, 1)
                    nc.gpsimd.memset(zerob[:], 0.0).then_inc(consts_done, 1)
                    pool.wait_ge(const_step, 3)
                    nc.gpsimd.affine_select(out=ident[:], in_=ident[:], compare_op=ALU.not_equal, fill=1.0,
                                            base=0, pattern=[[-1, P]], channel_multiplier=1).then_inc(const_step, 1)
                    nc.gpsimd.affine_select(out=maskb[:], in_=maskb[:], compare_op=ALU.is_ge, fill=MASKED,
                                            base=0, pattern=[[-1, P]], channel_multiplier=1).then_inc(consts_done, 1)
                    for g in range(4):
                        nc.gpsimd.affine_select(out=gather4[:], in_=gather4[:],
                                                compare_op=ALU.not_equal, fill=1.0, base=-32 * g,
                                                pattern=[[-1, 32]], channel_multiplier=1).then_inc(const_step, 1)
                        pool.wait_ge(const_step, 5 + g)
                    nc.gpsimd.tensor_copy(identb[:], ident[:]).then_inc(consts_done, 1)
                    nc.gpsimd.memset(zeros[:], 0.0).then_inc(zeros_ready, 1)
                    nc.gpsimd.memset(before[:], 1.0).then_inc(const_step, 1)
                    nc.gpsimd.memset(earlier[:], 1.0).then_inc(const_step, 1)
                    nc.gpsimd.memset(ones[:], 1.0).then_inc(consts_done, 1)
                    nc.gpsimd.iota(count_i[:], pattern=[[1, SLOT_TILES]], base=0, channel_multiplier=0
                                   ).then_inc(const_step, 1)
                    pool.wait_ge(const_step, 11)
                    nc.gpsimd.affine_select(out=before[:], in_=before[:], compare_op=ALU.is_gt, fill=0.0, base=0,
                                            pattern=[[1, E], [-1, E]], channel_multiplier=0
                                            ).then_inc(consts_done, 1)
                    nc.gpsimd.affine_select(out=earlier[:], in_=earlier[:], compare_op=ALU.is_gt, fill=0.0,
                                            base=0, pattern=[[1, P]], channel_multiplier=-1
                                            ).then_inc(consts_done, 1)
                    nc.gpsimd.tensor_copy(count_f[:], count_i[:]).then_inc(const_step, 1)
                    pool.wait_ge(const_step, 12)
                    nc.gpsimd.tensor_scalar(count_128[:], count_f[:, 0:T // P], float(P), None, ALU.mult
                                            ).then_inc(consts_done, 1)

                @block.sync
                def _(sp):
                    x_v = x.rearrange("(b h t p) d -> b h p t d", b=B, h=2, p=P)
                    sp.dma_start(X[0][:], x_v[0, 0]).then_inc(x_loaded[0], 16)
                    sp.dma_start(wqk_sb[:], wqk.rearrange("(c p) n -> p c n", p=P)).then_inc(w_loaded, 16)
                    sp.dma_start(X[1][:], x_v[0, 1]).then_inc(x_loaded[1], 16)
                    sp.dma_start(wv_sb[:, :, 0:D], wv.rearrange("(c p) n -> p c n", p=P)).then_inc(w_loaded, 16)
                    sp.dma_start(wv_sb[:, :, D:], rw.rearrange("(c p) n -> p c n", p=P)).then_inc(w_loaded, 16)
                    sp.dma_start(rb_sb[:], rb.partition_broadcast(P)).then_inc(w_loaded, 16)
                    sp.dma_start(lam_in[:], lam.partition_broadcast(P)).then_inc(w_loaded, 16)
                    sp.dma_start(wo_sb[:], wo.rearrange("(c p) n -> p c n", p=P)).then_inc(w_loaded, 16)

                    xn_v = xn_dram.rearrange("(c t p) d -> c p t d", c=NCH, p=P)

                    sp.wait_ge(zeros_ready, 1)
                    xs_v = xs_dram.rearrange("(n p r) d -> n p (r d)", p=P, r=SLOT_TILES // NCH)

                    def chunk(b, h):
                        sp.dma_start(xs_v[b * 2 + h], zeros[:]).then_inc(zeros_stored, 16)
                        sp.wait_ge(xn_ready, credited(b, 2, h))
                        sp.dma_start(xn_v[b * 2 + h], XN[h][:]).then_inc(xn_stored[h], 16)
                        for i in range(QKT):
                            sp.wait_ge(hi_ready, credited(b, 2 * QKT, h * QKT + i))
                            sp.wait_ge(lo_ready, credited(b, 2 * QKT, h * QKT + i))
                            dst = (q_parts if i < QKT // 2 else k_parts)[
                                b * 4 + i % 4, :, :, h * CH:(h + 1) * CH]
                            sp.dma_start(dst.rearrange("l p n -> p l n"), PARTS[i % 4][:].bitcast(F32)
                                         ).then_inc(parts_stored[i % 4], 16)

                    with sp.Fori(0, B - 1) as b:
                        for h in range(2):
                            sp.wait_ge(xn_ready, credited(b, 2, h))
                            sp.dma_start(X[h][:], x_v[b + 1, h]).then_inc(x_loaded[h], 16)
                            chunk(b, h)
                    for h in range(2):
                        chunk(B - 1, h)
                    for h in range(2):
                        sp.wait_ge(xn_stored[h], 16 * (B + 1))
                    for i in range(4):
                        sp.wait_ge(parts_stored[i], 16 * (4 * B + 1))
                    sp.wait_ge(zeros_stored, 16 * NCH)

                @block.vector
                def _(dve):
                    dve.sem_inc(ln_step, 2 * LN_OPS)
                    dve.sem_inc(xn_ready, 2)
                    dve.sem_inc(var_ready, 2)
                    dve.sem_inc(lo_ready, 2 * QKT)
                    dve.sem_inc(logits_ready, 8)

                    def normalise(b, h):
                        b, h = b + h // 2, h % 2
                        base = h * LN_OPS
                        dve.wait_ge(x_loaded[h], 16 * (b + 1))
                        for i in range(CT):
                            nc.vector.bn_stats(stats[:, i, :], X[h][:, i, :]).then_inc(ln_step, 1)
                        for i in range(CT):
                            if i == 0:
                                dve.wait_ge(ln_step, credited(b, 2 * LN_OPS, base + 3))
                                dve.sem_inc(stats_seen, 1)
                            nc.vector.bn_aggr(mv[:, i, :], stats[:, i, :]).then_inc(ln_step, 1)
                        dve.wait_ge(ln_step, credited(b, 2 * LN_OPS, base + 7))
                        nc.vector.tensor_scalar(ve[:], mv[:, :, 1], LN_EPS, None, ALU.add).then_inc(var_ready, 1)
                        dve.wait_ge(std_ready, credited(b, 2, h))
                        nc.vector.reciprocal(rs[:], sd[:]).then_inc(ln_step, 1)
                        dve.wait_ge(ln_step, credited(b, 2 * LN_OPS, base + 8))
                        nc.vector.tensor_tensor(nt[:], rs[:], rs[:], ALU.mult).then_inc(ln_step, 1)
                        dve.wait_ge(ln_step, credited(b, 2 * LN_OPS, base + 9))
                        nc.vector.tensor_tensor(nt[:], nt[:], ve[:], ALU.mult).then_inc(ln_step, 1)
                        dve.wait_ge(ln_step, credited(b, 2 * LN_OPS, base + 10))
                        nc.vector.tensor_scalar(nt[:], nt[:], -0.5, 1.5, ALU.mult, ALU.add).then_inc(ln_step, 1)
                        dve.wait_ge(ln_step, credited(b, 2 * LN_OPS, base + 11))
                        nc.vector.tensor_tensor(rs[:], rs[:], nt[:], ALU.mult).then_inc(ln_step, 1)
                        dve.wait_ge(ln_step, credited(b, 2 * LN_OPS, base + 12))
                        dve.wait_ge(xn_stored[h], 16 * (b + 1))
                        dve.wait_ge(xnT_bank, credited(b, 4, 2 * h + 1 - 4))
                        for i in range(CT):
                            last = nc.vector.tensor_scalar(XN[h][:, i, :], X[h][:, i, :], mv[:, i, 0:1],
                                                           rs[:, i:i + 1], ALU.subtract, ALU.mult)
                        last.then_inc(xn_ready, 1)

                    def rank(b):
                        done = [0]

                        def then(ins):
                            ins.then_inc(rank_step, 1)
                            done[0] += 1
                            dve.wait_ge(rank_step, b * RANK_OPS + done[0])

                        tiles = bass.ds(b * QT, QT)
                        dve.wait_ge(logits_ready, credited(b, 8, 7))
                        own = logits[:, tiles, :].unsqueeze(3).broadcast_to([P, QT, E, E])
                        other = logits[:, tiles, :].unsqueeze(2).broadcast_to([P, QT, E, E])
                        c4 = cmp[:, 0:QT * E * E].rearrange("p (t e f) -> p t e f", e=E, f=E)
                        c3 = cmp[:, 0:QT * E * E].rearrange("p (t k) -> p t k", t=QT)
                        then(nc.vector.tensor_tensor(c4, other, own, ALU.is_equal))
                        then(nc.vector.tensor_tensor(c3, c3, before[:].rearrange("p e f -> p (e f)").unsqueeze(1)
                                                     .broadcast_to([P, QT, E * E]), ALU.mult))
                        then(nc.vector.tensor_reduce(ranks[:, 0], c4, AX.X, ALU.add))
                        then(nc.vector.tensor_tensor(c4, other, own, ALU.is_gt))
                        then(nc.vector.tensor_reduce(ranks[:, 1], c4, AX.X, ALU.add))
                        then(nc.vector.tensor_tensor(ranks[:, 2], ranks[:, 0], ranks[:, 1], ALU.add))
                        for k in range(TOP_K):
                            then(nc.vector.tensor_scalar(chosen[:, k, tiles, :], ranks[:, 2], float(k), None,
                                                         ALU.is_equal))
                        nc.vector.tensor_tensor(chosen_b[:, tiles, :], chosen[:, 0, tiles, :],
                                                chosen[:, 1, tiles, :], ALU.add).then_inc(chosen_ready, 1)
                        ck = cmp[:, 0:TOP_K * QT * E].rearrange("p (k t e) -> p k t e", k=TOP_K, e=E)
                        for k in range(TOP_K):
                            then(nc.vector.tensor_tensor(ck[:, k], chosen[:, k, tiles, :], logits[:, tiles, :],
                                                         ALU.mult))
                        then(nc.vector.tensor_reduce(top[:, 0:2, tiles], ck, AX.X, ALU.add))

                    def batch(b, more):
                        for h in range(2):
                            for i in range(QKT):
                                dve.wait_ge(hi_ready, credited(b, 2 * QKT, h * QKT + i))
                                scale = 1.0 / math.sqrt(DH) if i < QKT // 2 else 1.0
                                nc.vector.scalar_tensor_tensor(
                                    out=PARTS[i % 4][:, 1, :], in0=qkbank[i % 4], scalar=scale,
                                    in1=PARTS[i % 4][:, 0, :].bitcast(F32), op0=ALU.mult, op1=ALU.subtract
                                ).then_inc(lo_ready, 1)
                                if i == 2 and (more or h == 0):
                                    normalise(b, h + 1)
                            for i in range(CT):
                                dve.wait_ge(v_ready, credited(b, 8, 4 * h + i))
                                nc.vector.tensor_tensor(logits[:, bass.ds(b * QT + h * CT + i, 1), :],
                                                        vbank[i % 2][:, D:D + E].unsqueeze(1),
                                                        rb_sb[:].unsqueeze(1), ALU.add).then_inc(logits_ready, 1)
                        rank(b)

                    normalise(0, 0)
                    dve.wait_ge(consts_done, 7)
                    dve.wait_ge(w_loaded, 96)
                    nc.vector.tensor_tensor(lam_w[:], lam_in[:, 0:4:2, :], lam_in[:, 1:4:2, :], ALU.mult
                                            ).then_inc(lam_step, 1)
                    dve.wait_ge(lam_step, 1)
                    nc.vector.tensor_reduce(lam_s[:, 0:2], lam_w[:], AX.X, ALU.add).then_inc(lam_step, 1)
                    with dve.Fori(0, B - 1) as b:
                        batch(b, True)
                    batch(B - 1, False)

                    steps = [0]

                    def then(ins):
                        ins.then_inc(route, 1)
                        steps[0] += 1
                        dve.wait_ge(route, steps[0])

                    NT = T // P
                    ck = cmp[:, 0:TOP_K * NT * E].rearrange("p (k t e) -> p k t e", k=TOP_K, e=E)
                    nc.vector.tensor_tensor(top[:, 2], top[:, 1], top[:, 0], ALU.subtract).then_inc(gap_ready, 1)
                    dve.wait_ge(ranks_bank, 1)
                    pre = bank6[:, 0:NT * E].rearrange("p (t e) -> p t e", e=E)
                    tot = bank7[:, 0:NT * E].rearrange("p (t e) -> p t e", e=E)
                    nc.vector.memset(run[0][:, 0:1, :], 0.0)
                    then(nc.vector.tensor_copy(run[0][:, 1:NT, :], tot[:, 0:NT - 1, :]))
                    src, span = 0, 1
                    while span < NT:
                        nc.vector.tensor_copy(run[1 - src][:, 0:span, :], run[src][:, 0:span, :])
                        then(nc.vector.tensor_tensor(run[1 - src][:, span:, :], run[src][:, span:, :],
                                                     run[src][:, 0:NT - span, :], ALU.add))
                        src, span = 1 - src, 2 * span
                    tokens, tiles, first, end, first_slot = (per_e[:, i] for i in range(5))
                    then(nc.vector.tensor_tensor(tokens, run[src][:, NT - 1, :], tot[:, NT - 1, :], ALU.add))
                    ce = cmp[:, 0:E * NT].rearrange("p (e t) -> p e t", e=E)
                    then(nc.vector.tensor_tensor(ce, tokens.unsqueeze(2).broadcast_to([P, E, NT]),
                                                 count_128[:].unsqueeze(1).broadcast_to([P, E, NT]), ALU.is_gt))
                    then(nc.vector.tensor_reduce(tiles, ce, AX.X, ALU.add))
                    cf = cmp[:, 0:E * E].rearrange("p (e f) -> p e f", e=E)
                    then(nc.vector.tensor_tensor(cf, before[:], tiles.unsqueeze(1).broadcast_to([P, E, E]),
                                                 ALU.mult))
                    then(nc.vector.tensor_reduce(first, cf, AX.X, ALU.add))
                    then(nc.vector.tensor_tensor(end, first, tiles, ALU.add))
                    then(nc.vector.tensor_scalar(first_slot, first, float(P), None, ALU.mult))
                    cs = cmp[:, 0:SLOT_TILES * E].rearrange("p (s e) -> p s e", e=E)
                    then(nc.vector.tensor_tensor(cs, end.unsqueeze(1).broadcast_to([P, SLOT_TILES, E]),
                                                 count_f[:].unsqueeze(2).broadcast_to([P, SLOT_TILES, E]),
                                                 ALU.is_le))
                    then(nc.vector.tensor_reduce(cmp[:, SLOT_TILES * E:SLOT_TILES * (E + 1)], cs, AX.X, ALU.add))
                    pairs = cmp[:, SLOT_TILES * E:SLOT_TILES * (E + 1)].rearrange("p (i u) -> p i u", u=2)
                    NR = SLOT_TILES // 2
                    nc.vector.tensor_scalar(expert_rows[:, :, 0:2], pairs, float(E - 1), None, ALU.min)
                    nc.vector.tensor_scalar(expert_rows[:, 0:NR - 1, 2:4], pairs[:, 1:], float(E - 1), None, ALU.min)
                    then(nc.vector.memset(expert_rows[:, NR - 1:NR, 2:4], 0))
                    then(nc.vector.tensor_tensor(run[1 - src][:], run[src][:], pre, ALU.add))
                    then(nc.vector.tensor_tensor(run[src][:], run[1 - src][:],
                                                 first_slot.unsqueeze(1).broadcast_to([P, NT, E]), ALU.add))
                    for k in range(TOP_K):
                        then(nc.vector.tensor_tensor(ck[:, k], chosen[:, k], run[src][:], ALU.mult))
                    then(nc.vector.tensor_reduce(top[:, 3:5], ck, AX.X, ALU.add))
                    then(nc.vector.tensor_copy(slot_of[:].rearrange("p t k -> p k t"), top[:, 3:5]))
                    dve.wait_ge(odds_ready, 1)
                    then(nc.vector.tensor_scalar(top[:, 4], top[:, 5], 1.0, None, ALU.add))
                    then(nc.vector.reciprocal(weight[:, :, 0], top[:, 4]))
                    then(nc.vector.tensor_tensor(weight[:, :, 1], weight[:, :, 0], top[:, 5], ALU.mult))
                    dve.wait_ge(lam_step, 3)
                    nc.vector.tensor_tensor(lam_s[:, 4:5], lam_s[:, 3:4], lam_s[:, 2:3], ALU.subtract
                                            ).then_inc(lam_step, 1)
                    dve.wait_ge(lam_step, 4)
                    nc.vector.tensor_scalar(neg_lam, lam_s[:, 4:5], -L_INIT, None, ALU.add
                                            ).then_inc(lam_step, 1)

                @block.scalar
                def _(act):
                    act.sem_inc(std_ready, 2)
                    act.sem_inc(xnT_ready, 4)
                    act.sem_inc(hi_ready, 2 * QKT)
                    act.sem_inc(v_ready, 8)

                    def deviation(b, h):
                        b, h = b + h // 2, h % 2
                        act.wait_ge(var_ready, credited(b, 2, h))
                        nc.scalar.activation(sd[:], ve[:], ACT.Sqrt).then_inc(std_ready, 1)

                    def turned_rows(b, h):
                        b, h = b + h // 2, h % 2
                        act.wait_ge(v_bank, credited(b, 8, 4 * h + 3 - 8))
                        for c in range(HC):
                            act.wait_ge(xnT_bank, credited(b, 4, 2 * h + c))
                            nc.scalar.copy(XNT[h][:, c, :], tbank[c]).then_inc(xnT_ready, 1)

                    def batch(b, more):
                        for h in range(2):
                            for i in range(QKT):
                                act.wait_ge(qk_bank, credited(b, 2 * QKT, h * QKT + i))
                                act.wait_ge(parts_stored[i % 4], 16 * (4 * b + 2 * h + i // 4 + 1))
                                scale = 1.0 / math.sqrt(DH) if i < QKT // 2 else 1.0
                                nc.scalar.mul(PARTS[i % 4][:, 0, :], qkbank[i % 4], scale).then_inc(hi_ready, 1)
                                if i == 2 and (more or h == 0):
                                    deviation(b, h + 1)
                            if more or h == 0:
                                turned_rows(b, h + 1)
                            for i in range(CT):
                                act.wait_ge(v_bank, credited(b, 8, 4 * h + i))
                                nc.scalar.copy(VO[:, bass.ds(b * (NH // 2), NH // 2), h * CT + i, :],
                                               vbank[i % 2][:, 0:D].rearrange("p (j d) -> p j d", d=2 * DH)
                                               ).then_inc(v_ready, 1)

                    deviation(0, 0)
                    turned_rows(0, 0)
                    with act.Fori(0, B - 1) as b:
                        batch(b, True)
                    batch(B - 1, False)
                    act.wait_ge(gap_ready, 1)
                    nc.scalar.activation(top[:, 5], top[:, 2], ACT.Exp).then_inc(odds_ready, 1)
                    act.wait_ge(lam_step, 2)
                    nc.scalar.activation(lam_s[:, 2:4], lam_s[:, 0:2], ACT.Exp).then_inc(lam_step, 1)

                @block.tensor
                def _(pe):
                    pe.sem_inc(xnT_bank, 4)
                    pe.sem_inc(qk_bank, 2 * QKT)
                    pe.sem_inc(v_bank, 8)
                    for h in range(2):
                        pe.sem_inc(xn_stored[h], 16)
                    for i in range(4):
                        pe.sem_inc(parts_stored[i], 16)
                    pe.wait_ge(consts_done, 7)

                    def turn_rows(b, h):
                        b, h = b + h // 2, h % 2
                        pe.wait_ge(xn_ready, credited(b, 2, h))
                        for c in range(HC):
                            pe.wait_ge(xnT_ready, credited(b, 4, 2 * h + c - 2))
                            for i in range(CT):
                                last = nc.tensor.transpose(tbank[c][:, i * P:(i + 1) * P],
                                                           XN[h][:, i, c * P:(c + 1) * P], ident[:])
                            last.then_inc(xnT_bank, 1)

                    def batch(b, more):
                        for h in range(2):
                            pe.wait_ge(xnT_ready, credited(b, 4, 2 * h + 1))
                            for i in range(QKT):
                                pe.wait_ge(lo_ready, credited(b, 2 * QKT, h * QKT + i - 4))
                                for c in range(HC):
                                    last = nc.tensor.matmul(qkbank[i % 4], wqk_sb[:, c, i * P:(i + 1) * P],
                                                            XNT[h][:, c, :], start=(c == 0), stop=(c == HC - 1))
                                last.then_inc(qk_bank, 1)
                            if more or h == 0:
                                turn_rows(b, h + 1)
                            for i in range(CT):
                                pe.wait_ge(logits_ready, credited(b, 8, 4 * h + i - 2))
                                for c in range(HC):
                                    last = nc.tensor.matmul(vbank[i % 2][:, 0:D + E],
                                                            XNT[h][:, c, i * P:(i + 1) * P], wv_sb[:, c, :],
                                                            start=(c == 0), stop=(c == HC - 1))
                                last.then_inc(v_bank, 1)

                    turn_rows(0, 0)
                    pe.wait_ge(w_loaded, 96)
                    with pe.Fori(0, B - 1) as b:
                        batch(b, True)
                    batch(B - 1, False)
                    pe.wait_ge(chosen_ready, B)
                    cb = chosen_b[:].rearrange("p t e -> p (t e)")
                    nc.tensor.matmul(bank6[:, 0:T // P * E], earlier[:], cb, start=True, stop=True)
                    nc.tensor.matmul(bank7[:, 0:T // P * E], ones[:], cb, start=True, stop=True
                                     ).then_inc(ranks_bank, 1)

        with ExitStack() as ph:
            Qs = [sb(f"Qs{u}", [P, 2, S], F32R, where=ph) for u in range(2)]
            Ks = [sb(f"Ks{u}", [P, 2, S], F32R, where=ph) for u in range(2)]
            Vj = [sb(f"Vj{u}", [P, QT, DH], where=ph) for u in range(2)]
            Pr = [sb(f"Pr{i}", [P, 2, S], where=ph) for i in range(4)]
            AT = [sb(f"AT{i}", [P, CH], where=ph) for i in range(4)]
            Ob = [sb(f"Ob{i}", [P, CH], where=ph) for i in range(2)]
            dsum = [sb(f"dsum{u}", [P, QT, 2], where=ph) for u in range(2)]
            nmax = sb("nmax", [P, 2 * NQ], where=ph)
            rows = [sb(f"rows{u}", [P, D], where=ph) for u in range(2)]
            row_slot = [sb(f"row_slot{u}", [P, TOP_K], U32, where=ph) for u in range(2)]
            rec = sb("rec", [P, NQ], where=ph)
            coef = sb("coef", [P, NQ], where=ph)

            qk_loaded = [sem(f"qk_loaded{u}") for u in range(2)]
            vj_ready = sem("vj_ready")
            d1_kept = sem("d1_kept")
            rows_loaded = [sem(f"rows_loaded{u}") for u in range(2)]
            row_slot_ready = sem("row_slot_ready")
            scatter_begun = sem("scatter_begun")
            rows_sorted = [sem(f"rows_sorted{u}") for u in range(2)]
            scored = sem("scored")
            maxed = sem("maxed")
            exped = sem("exped")
            rec_done = sem("rec_done")
            coef_done = sem("coef_done")
            combined = sem("combined")
            turned = sem("turned")
            turned_out = sem("turned_out")
            pv_done = sem("pv_done")
            o_out = sem("o_out")

            slot = bank
            tb, ob = bank6, bank7

            with nc.Block() as block:
                @block.sync
                def _(sp):

                    def load(it, u):
                        sp.wait_ge(scored, credited(it, USES, (USES // 2) * (u + 1) - 1 - USES))
                        rows = slice(u * 2 * DH, (u + 1) * 2 * DH)
                        for g in range(4):
                            qp = q_parts[it, g % 2, rows, :].rearrange("(m d) t -> d m t", m=2)
                            kp = k_parts[it, g // 2, rows, :].rearrange("(m d) t -> d m t", m=2)
                            sp.dma_start(Qs[u][g * DH:(g + 1) * DH, :, :].bitcast(F32), qp
                                         ).then_inc(qk_loaded[u], 16)
                            sp.dma_start(Ks[u][g * DH:(g + 1) * DH, :, :].bitcast(F32), kp
                                         ).then_inc(qk_loaded[u], 16)

                    for u in range(2):
                        load(0, u)
                    sp.dma_start(gu_sb[:].rearrange("p c e n -> p c (e n)"),
                                 gu.rearrange("(c p) e n -> p c (e n)", p=P)).then_inc(ew_loaded, 16)
                    sp.dma_start(dn_sb[:].rearrange("p c e n -> p c (e n)"),
                                 dn.rearrange("(c p) e n -> p c (e n)", p=P)).then_inc(ew_loaded, 16)
                    sp.dma_start(gub_sb[:], gub.partition_broadcast(P)).then_inc(ew_loaded, 16)
                    sp.dma_start(dnb_sb[:], dnb.partition_broadcast(P)).then_inc(ew_loaded, 16)
                    with sp.Fori(0, NIT - 1) as it:
                        for u in range(2):
                            load(it + 1, u)

                @block.gpsimd
                def _(pool):
                    pool.sem_inc(vj_ready, 2)
                    pool.sem_inc(d1_kept, 2)
                    xn_v = xn_dram.rearrange("(t p) d -> t p d", p=P)
                    with pool.Fori(0, NIT) as it:
                        for u in range(2):
                            pool.wait_ge(pv_done, credited(it, NQ, QT * (u + 1) - 1 - NQ))
                            nc.gpsimd.tensor_copy(Vj[u][:].unsqueeze(1), VO[:, bass.ds(it, 1), :, u * DH:(u + 1) * DH]
                                                  ).then_inc(vj_ready, 1)
                        for u in range(2):
                            pool.dma_start(rows[u][:], xn_v[it * 2 + u]).then_inc(rows_loaded[u], 16)
                            nc.gpsimd.tensor_copy(row_slot[u][:].unsqueeze(1),
                                                  slot_of[:, bass.ds(it * 2 + u, 1), :]
                                                  ).then_inc(row_slot_ready, 1)
                        for u in range(2):
                            pool.wait_ge(rows_loaded[u], 16 * (it + 1))
                            pool.wait_ge(row_slot_ready, 2 * it + u + 1)
                            pool.sem_inc(scatter_begun, 1)
                            for k in range(TOP_K):
                                pool.indirect_dma_start(
                                    xs_dram, bass.IndirectOffsetOnAxis(row_slot[u][:, k:k + 1], 0),
                                    rows[u][:], None).then_inc(rows_sorted[u], 16)
                        for u in range(2):
                            pool.wait_ge(exped, credited(it, STEPS, (STEPS // 2) * (u + 1) - 1))
                            nc.gpsimd.tensor_copy(d1_all[:, bass.ds(it * 2 + u, 1), :],
                                                  dsum[u][:, :, 0].unsqueeze(1)).then_inc(d1_kept, 1)
                        for u in range(2):
                            pool.wait_ge(rows_sorted[u], 32 * (it + 1))

                def gathered_place(half, i):
                    return query(4 * half + i)[1] // (QT // 2) * 2 + i // 2

                def score(it, n, k):
                    it, n = it + n // NQ, n % NQ
                    head, q = query(n)
                    if k >= len(uses(n)):
                        return
                    use, maps = uses(n)[k]
                    if n % QT == 0 and k == 0:
                        nc.tensor.wait_ge(qk_loaded[head], 16 * 8 * (it + 1))
                    nc.tensor.wait_ge(exped, credited(it, STEPS, last_step(use - SLOTS)))
                    N = (q + 1) * P
                    for m in maps:
                        at = slot[use % SLOTS][:, CH:] if len(maps) > 1 and m else slot[use % SLOTS]
                        for c0 in range(0, N, CH):
                            c1 = min(c0 + CH, N)
                            nc.tensor.matmul(at[:, c0:c1], Qs[head][:, m, q * P:(q + 1) * P],
                                             Ks[head][:, m, c0:c1], start=True, stop=(c1 < N))
                        last = nc.tensor.matmul(at[:, N - P:N], identb[:], maskb[:], start=False, stop=True)
                    last.then_inc(scored, 1)

                def turn(it, n, k):
                    un = units(n)
                    if k >= len(un):
                        return
                    fill, _, blocks = un[k]
                    if k == 0:
                        nc.tensor.wait_ge(combined, credited(it, NQ, n))
                    nc.tensor.wait_ge(turned_out, credited(it, FILLS, fill - 1))
                    for i, kb in enumerate(blocks):
                        last = nc.tensor.transpose(tb[:, i * P:(i + 1) * P],
                                                   Pr[n % 4][:, 0, kb * P:(kb + 1) * P], ident[:])
                    last.then_inc(turned, 1)

                def gather(it, n):
                    for half in gathers(n):
                        nc.tensor.wait_ge(o_out, credited(it, 4, half))
                        nc.tensor.wait_ge(turned_out, credited(it, FILLS, units(n)[-1][0]))
                        for i in range(4):
                            at = gathered_place(half, i) * DH
                            last = nc.tensor.matmul(tb[:, at:at + DH], Ob[half % 2][:, i * P:(i + 1) * P],
                                                    gather4[:], start=True, stop=True)
                        last.then_inc(turned, 1)

                def values(it, n):
                    head, q = query(n)
                    if n % QT == 0:
                        nc.tensor.wait_ge(vj_ready, credited(it, 2, head))
                    if n % 4 == 0:
                        nc.tensor.wait_ge(o_out, credited(it, 4, n // 4 - 1))
                        nc.tensor.matmul(ob[:], zerob[:, 0:P], zerob[:], start=True, stop=False,
                                         skip_group_check=True)
                    for fill, unit, blocks in units(n):
                        nc.tensor.wait_ge(turned_out, credited(it, FILLS, fill))
                        for i, kb in enumerate(blocks):
                            g = kb % 4
                            last = nc.tensor.matmul(
                                ob[DH * g:DH * (g + 1), (n % 4) * P:(n % 4 + 1) * P], Vj[head][:, kb, :],
                                AT[unit % 4][:, i * P:(i + 1) * P], start=False, stop=True,
                                tile_position=(0, DH * g), skip_group_check=True)
                    last.then_inc(pv_done, 1)

                def pe_tile(it, n, ahead=True, start=False):
                    turn(it, n, 0)
                    if ahead:
                        score(it, n + 3, 0)
                    turn(it, n, 1)
                    if ahead:
                        score(it, n + 3, 1)
                    if start and n == 1:
                        nc.tensor.wait_ge(turned_out, credited(it, FILLS, units(n)[-1][0]))
                        nc.tensor.sem_inc(turned, 1)
                    else:
                        gather(it, n)
                    values(it, n)

                @block.tensor
                def _(pe):
                    pe.sem_inc(scored, USES)
                    pe.sem_inc(turned, FILLS)
                    pe.sem_inc(pv_done, NQ)
                    for n in range(3):
                        for k in range(2):
                            score(0, n, k)
                    for n in range(NQ):
                        pe_tile(0, n, start=True)
                    with pe.Fori(1, NIT - 1) as it:
                        for n in range(NQ):
                            pe_tile(it, n)
                    for n in range(NQ):
                        pe_tile(NIT - 1, n, ahead=(n + 3 < NQ))
                    nc.tensor.wait_ge(o_out, credited(NIT - 1, 4, 3))
                    for i in range(4):
                        at = gathered_place(3, i) * DH
                        last = nc.tensor.matmul(tb[:, at:at + DH], Ob[1][:, i * P:(i + 1) * P], gather4[:],
                                                start=True, stop=True)
                    last.then_inc(turned, 1)

                def exponential(it, n, m):
                    it, n = it + n // NQ, n % NQ
                    head, q = query(n)
                    step = 2 * n + m
                    N = (q + 1) * P
                    use, maps = [x for x in uses(n) if m in x[1]][0]
                    at = slot[use % SLOTS][:, CH:] if len(maps) > 1 and m else slot[use % SLOTS]
                    if m == maps[0]:
                        nc.scalar.wait_ge(maxed, credited(it, USES, use))
                    if m == 0:
                        nc.scalar.wait_ge(turned, credited(it, FILLS, units(n - 4)[-1][0] if n >= 4 else
                                                           units(NQ + n - 4)[-1][0] - FILLS))
                        if n % QT == 0:
                            nc.scalar.wait_ge(d1_kept, credited(it, 2, head - 2))
                    nc.scalar.activation(Pr[n % 4][:, m, 0:N], at[:, 0:N], ACT.Exp,
                                         bias=nmax[:, step:step + 1], scale=1.0,
                                         accum_out=dsum[head][:, q, m:m + 1]).then_inc(exped, 1)

                def turn_out(it, n, k):
                    un = units(n)
                    if k >= len(un):
                        return
                    fill, unit, blocks = un[k]
                    nc.scalar.wait_ge(turned, credited(it, FILLS, fill))
                    user = [m for m in range(2 * NQ) if any(
                        (u + (m // NQ) * UNITS) == unit - 4 + UNITS for _, u, _ in units(m % NQ))][0]
                    nc.scalar.wait_ge(pv_done, credited(it, NQ, user - NQ))
                    w = len(blocks) * P
                    nc.scalar.copy(AT[unit % 4][:, 0:w], tb[:, 0:w]).then_inc(turned_out, 1)

                def out_tile(it, n):
                    if n % 4 != 3:
                        return
                    nc.scalar.wait_ge(pv_done, credited(it, NQ, n))
                    nc.scalar.copy(Ob[n // 4 % 2][:], ob[:]).then_inc(o_out, 1)

                def gathered_out(it, half, fill):
                    nc.scalar.wait_ge(turned, credited(it, FILLS, fill))
                    if half < 0:
                        it, half = it - 1, half + 4
                    head, first = half // 2, half % 2 * 2
                    to = VO[:, bass.ds(it, 1), :, head * DH:(head + 1) * DH].rearrange(
                        "p o (a t) d -> p (o a) t d", a=2)[:, :, first:first + 2, :]
                    nc.scalar.copy(to, tb[:, 0:4 * DH].rearrange("p (a t d) -> p a t d", a=2, t=2)
                                   ).then_inc(turned_out, 1)

                def act_tile(it, n, ahead=True, start=False):
                    turn_out(it, n, 0)
                    if ahead:
                        exponential(it, n + 2, 0)
                    turn_out(it, n, 1)
                    if ahead:
                        exponential(it, n + 2, 1)
                    for half in gathers(n):
                        if start and half < 0:
                            nc.scalar.wait_ge(turned, credited(it, FILLS, units(n)[-1][0] + 1))
                            nc.scalar.sem_inc(turned_out, 1)
                        else:
                            gathered_out(it, half, units(n)[-1][0] + 1)
                    out_tile(it, n)

                @block.scalar
                def _(act):
                    act.sem_inc(exped, STEPS)
                    act.sem_inc(turned_out, FILLS)
                    act.sem_inc(o_out, 4)
                    for n in range(2):
                        for m in range(2):
                            exponential(0, n, m)
                    for n in range(NQ):
                        act_tile(0, n, start=True)
                    with act.Fori(1, NIT - 1) as it:
                        for n in range(NQ):
                            act_tile(it, n)
                    for n in range(NQ):
                        act_tile(NIT - 1, n, ahead=(n + 2 < NQ))
                    gathered_out(NIT - 1, 3, FILLS)

                def maximum(it, n, k):
                    it, n = it + n // NQ, n % NQ
                    if k >= len(uses(n)):
                        return
                    use, maps = uses(n)[k]
                    N = (query(n)[1] + 1) * P
                    step = 2 * n + maps[0]
                    src = slot[use % SLOTS][:, 0:N]
                    if len(maps) > 1:
                        src = slot[use % SLOTS][:].rearrange("p (m n) -> p m n", m=2)[:, :, 0:N]
                    nc.vector.wait_ge(scored, credited(it, USES, use))
                    nc.vector.tensor_reduce(nmax[:, step:step + len(maps)], src, AX.X, ALU.max, negate=True
                                            ).then_inc(maxed, 1)

                def inverse(it, n):
                    it, n = it + n // NQ, n % NQ
                    head, q = query(n)
                    nc.vector.wait_ge(exped, credited(it, STEPS, 2 * n + 1))
                    nc.vector.reciprocal(rec[:, n:n + 1], dsum[head][:, q, 1:2]).then_inc(rec_done, 1)

                def ratio(it, n):
                    it, n = it + n // NQ, n % NQ
                    head, q = query(n)
                    nc.vector.wait_ge(rec_done, credited(it, NQ, n))
                    nc.vector.scalar_tensor_tensor(out=coef[:, n:n + 1], in0=dsum[head][:, q, 0:1],
                                                   scalar=neg_lam, in1=rec[:, n:n + 1], op0=ALU.mult,
                                                   op1=ALU.mult).then_inc(coef_done, 1)

                def combine(it, n):
                    it, n = it + n // NQ, n % NQ
                    N = (query(n)[1] + 1) * P
                    nc.vector.wait_ge(coef_done, credited(it, NQ, n))
                    nc.vector.scalar_tensor_tensor(
                        out=Pr[n % 4][:, 0, 0:N], in0=Pr[n % 4][:, 1, 0:N], scalar=coef[:, n:n + 1],
                        in1=Pr[n % 4][:, 0, 0:N], op0=ALU.mult, op1=ALU.add).then_inc(combined, 1)

                def dve_tile(it, n, ahead=True, ahead2=True):
                    if ahead:
                        inverse(it, n + 1)
                    if ahead2:
                        maximum(it, n + 2, 0)
                    if ahead:
                        ratio(it, n + 1)
                    if ahead2:
                        maximum(it, n + 2, 1)
                    if ahead:
                        combine(it, n + 1)

                @block.vector
                def _(dve):
                    dve.sem_inc(maxed, USES)
                    dve.sem_inc(rec_done, NQ)
                    dve.sem_inc(coef_done, NQ)
                    dve.sem_inc(combined, NQ)
                    for n in range(2):
                        for k in range(2):
                            maximum(0, n, k)
                    inverse(0, 0)
                    ratio(0, 0)
                    combine(0, 0)
                    with dve.Fori(0, NIT - 1) as it:
                        for n in range(NQ):
                            dve_tile(it, n)
                    for n in range(NQ):
                        dve_tile(NIT - 1, n, ahead=(n + 1 < NQ), ahead2=(n + 2 < NQ))

        with ExitStack() as ph:
            xs = [sb(f"xs{u}", [P, D], where=ph) for u in range(2)]
            xsT = [sb(f"xsT{u}", [P, HC, P], where=ph) for u in range(2)]
            hid = [sb(f"hid{u}", [P, 2 * I], where=ph) for u in range(2)]
            gate_tanh = [sb(f"gate_tanh{u}", [P, I], where=ph) for u in range(2)]
            glu = [sb(f"glu{u}", [P, I], where=ph) for u in range(2)]
            up = [sb(f"up{u}", [P, I], where=ph) for u in range(2)]
            act_in = [sb(f"act_in{u}", [P, I], where=ph) for u in range(2)]
            act_T = [sb(f"act_T{u}", [P, HC, P], where=ph) for u in range(2)]
            ys = [sb(f"ys{u}", [P, D], where=ph) for u in range(2)]

            xs_loaded = [sem(f"xs_loaded{u}") for u in range(2)]
            xs_turned = sem("xs_turned")
            xsT_ready = sem("xsT_ready")
            hid_bank = sem("hid_bank")
            hid_ready = sem("hid_ready")
            gate_ready = sem("gate_ready")
            tanh_ready = sem("tanh_ready")
            glu_ready = sem("glu_ready")
            up_ready = sem("up_ready")
            act_ready = sem("act_ready")
            act_turned = sem("act_turned")
            act_T_ready = sem("act_T_ready")
            y_bank = sem("y_bank")
            y_ready = sem("y_ready")
            y_stored = [sem(f"y_stored{u}") for u in range(2)]

            hbank = [bank[0][:, 0:CH], bank[0][:, CH:]]
            xbank = [bank[1][:, 0:CH], bank[1][:, CH:]]
            abank = [bank[2][:, 0:CH], bank[2][:, CH:]]
            ybank = [bank6, bank7]
            NIT3 = SLOT_TILES // 2

            def seen(it, u):
                return credited(it, 2, u)

            with nc.Block() as block:
                xs_v = xs_dram.rearrange("(n u p) d -> n u p d", u=2, p=P)
                ys_v = ys_dram.rearrange("(n u p) d -> n u p d", u=2, p=P)

                @block.sync
                def _(sp):
                    def load(it, u):
                        sp.wait_ge(xs_turned, seen(it, u - 2))
                        sp.dma_start(xs[u][:], xs_v[it, u]).then_inc(xs_loaded[u], 16)

                    with sp.Fori(0, NIT3) as it:
                        for u in range(2):
                            load(it, u)

                def expert_loader(eng):
                    registers = [eng.alloc_register(f"expert{n}") for n in range(4)]

                    def load(i):
                        eng.load(registers, expert_rows[0:1, bass.ds(i, 1), :].rearrange("p o n -> p (o n)"))
                        return [bass.RuntimeValue.of_register_unchecked(r, min_val=0, max_val=E - 1)
                                for r in registers]

                    return load

                def there(it, n):
                    return not isinstance(it, int) or 0 <= 2 * it + n < SLOT_TILES

                def run_steps(eng, step, load=None):
                    load = load or (lambda it: None)
                    step(0, 0, load(0))
                    with eng.Fori(0, NIT3 - 2) as it:
                        e = load(it)
                        step(it, 1, e)
                        step(it, 2, e)
                    e = load(NIT3 - 2)
                    for n in (1, 2, 3, 4):
                        step(NIT3 - 2, n, e)

                def turn_rows(it, n):
                    if not there(it, n):
                        return
                    it, u = it + n // 2, n % 2
                    nc.tensor.wait_ge(xs_loaded[u], 16 * (it + 1))
                    nc.tensor.wait_ge(xsT_ready, seen(it, u - 2))
                    for c in range(HC):
                        last = nc.tensor.transpose(xbank[u][:, c * P:(c + 1) * P], xs[u][:, c * P:(c + 1) * P],
                                                   ident[:])
                    last.then_inc(xs_turned, 1)

                def gate_and_up(it, n, experts_of):
                    if not there(it, n):
                        return
                    e = experts_of[n]
                    it, u = it + n // 2, n % 2
                    nc.tensor.wait_ge(xsT_ready, seen(it, u))
                    nc.tensor.wait_ge(hid_ready, seen(it, u - 2))
                    for c in range(HC):
                        last = nc.tensor.matmul(hbank[u], xsT[u][:, c, :],
                                                gu_sb[:, c, bass.ds(e, 1), :].rearrange("p o n -> p (o n)"),
                                                start=(c == 0), stop=(c == HC - 1))
                    last.then_inc(hid_bank, 1)

                def turn_act(it, n):
                    if not there(it, n):
                        return
                    it, u = it + n // 2, n % 2
                    nc.tensor.wait_ge(act_ready, seen(it, u))
                    nc.tensor.wait_ge(act_T_ready, seen(it, u - 2))
                    for c in range(HC):
                        last = nc.tensor.transpose(abank[u][:, c * P:(c + 1) * P],
                                                   act_in[u][:, c * P:(c + 1) * P], ident[:])
                    last.then_inc(act_turned, 1)

                def down(it, n, experts_of):
                    if not there(it, n):
                        return
                    e = experts_of[n]
                    it, u = it + n // 2, n % 2
                    nc.tensor.wait_ge(act_T_ready, seen(it, u))
                    nc.tensor.wait_ge(y_ready, seen(it, u - 2))
                    for c in range(HC):
                        last = nc.tensor.matmul(ybank[u][:, 0:D], act_T[u][:, c, :],
                                                dn_sb[:, c, bass.ds(e, 1), :].rearrange("p o n -> p (o n)"),
                                                start=(c == 0), stop=(c == HC - 1))
                    last.then_inc(y_bank, 1)

                @block.tensor
                def _(pe):
                    for s in (xs_turned, hid_bank, act_turned, y_bank):
                        pe.sem_inc(s, 2)
                    pe.wait_ge(ew_loaded, 64)
                    turn_rows(0, 0)
                    turn_rows(0, 1)
                    load = expert_loader(pe)
                    gate_and_up(0, 0, load(0))

                    def step(it, n, e):
                        turn_rows(it, n + 2)
                        gate_and_up(it, n + 1, e)
                        down(it, n - 1, e)
                        turn_act(it, n)

                    run_steps(pe, step, load)

                def rows_out(it, n):
                    if not there(it, n):
                        return
                    it, u = it + n // 2, n % 2
                    nc.scalar.wait_ge(xs_turned, seen(it, u))
                    nc.scalar.wait_ge(hid_bank, seen(it, u - 2))
                    nc.scalar.copy(xsT[u][:].rearrange("p c n -> p (c n)"), xbank[u][:, 0:HC * P]
                                   ).then_inc(xsT_ready, 1)

                def gate_curve(it, n):
                    if not there(it, n):
                        return
                    it, u = it + n // 2, n % 2
                    nc.scalar.wait_ge(gate_ready, seen(it, u))
                    nc.scalar.wait_ge(glu_ready, seen(it, u - 2))
                    nc.scalar.activation(gate_tanh[u][:], hid[u][:, 0:I], ACT.Tanh, scale=ALPHA / 2
                                         ).then_inc(tanh_ready, 1)

                def act_out(it, n):
                    if not there(it, n):
                        return
                    it, u = it + n // 2, n % 2
                    nc.scalar.wait_ge(act_turned, seen(it, u))
                    nc.scalar.wait_ge(y_bank, seen(it, u - 2))
                    nc.scalar.copy(act_T[u][:].rearrange("p c n -> p (c n)"), abank[u][:, 0:HC * P]
                                   ).then_inc(act_T_ready, 1)

                def store(it, n):
                    if not there(it, n):
                        return
                    it, u = it + n // 2, n % 2
                    nc.scalar.wait_ge(y_ready, seen(it, u))
                    nc.scalar.dma_start(ys_v[it, u], ys[u][:]).then_inc(y_stored[u], 16)

                @block.scalar
                def _(act):
                    for u in range(2):
                        act.sem_inc(y_stored[u], 16)
                    for s in (xsT_ready, tanh_ready, act_T_ready):
                        act.sem_inc(s, 2)
                    rows_out(0, 0)
                    rows_out(0, 1)
                    gate_curve(0, 0)

                    def step(it, n, e):
                        rows_out(it, n + 2)
                        gate_curve(it, n + 1)
                        store(it, n - 1)
                        act_out(it, n)

                    run_steps(act, step)
                    for u in range(2):
                        act.wait_ge(y_stored[u], 16 * (NIT3 + 1))

                def hidden(it, n, experts_of):
                    if not there(it, n):
                        return
                    e = experts_of[n]
                    it, u = it + n // 2, n % 2
                    nc.vector.wait_ge(hid_bank, seen(it, u))
                    nc.vector.tensor_tensor(hid[u][:], hbank[u],
                                            gub_sb[:, bass.ds(e, 1), :].rearrange("p o n -> p (o n)"), ALU.add
                                            ).then_inc(hid_ready, 1)

                def gate(it, n):
                    if not there(it, n):
                        return
                    it, u = it + n // 2, n % 2
                    nc.vector.wait_ge(hid_ready, seen(it, u))
                    nc.vector.tensor_scalar(hid[u][:, 0:I], hid[u][:, 0:I], LIMIT, None, ALU.min
                                            ).then_inc(gate_ready, 1)

                def activate(it, n):
                    if not there(it, n):
                        return
                    it, u = it + n // 2, n % 2
                    nc.vector.wait_ge(tanh_ready, seen(it, u))
                    nc.vector.scalar_tensor_tensor(out=glu[u][:], in0=gate_tanh[u][:], scalar=1.0,
                                                   in1=hid[u][:, 0:I], op0=ALU.add, op1=ALU.mult
                                                   ).then_inc(glu_ready, 1)
                    nc.vector.tensor_scalar(up[u][:], hid[u][:, I:], LIMIT, -LIMIT, ALU.min, ALU.max
                                            ).then_inc(up_ready, 1)
                    nc.vector.wait_ge(glu_ready, seen(it, u))
                    nc.vector.wait_ge(up_ready, seen(it, u))
                    nc.vector.wait_ge(act_turned, seen(it, u - 2))
                    nc.vector.scalar_tensor_tensor(out=act_in[u][:], in0=up[u][:], scalar=1.0, in1=glu[u][:],
                                                   op0=ALU.add, op1=ALU.mult).then_inc(act_ready, 1)

                def output(it, n, experts_of):
                    if not there(it, n):
                        return
                    e = experts_of[n]
                    it, u = it + n // 2, n % 2
                    nc.vector.wait_ge(y_bank, seen(it, u))
                    nc.vector.wait_ge(y_stored[u], 16 * (it + 1))
                    nc.vector.scalar_tensor_tensor(out=ys[u][:], in0=ybank[u][:, 0:D], scalar=0.5,
                                                   in1=dnb_sb[:, bass.ds(e, 1), :].rearrange("p o n -> p (o n)"),
                                                   op0=ALU.mult, op1=ALU.add).then_inc(y_ready, 1)

                @block.vector
                def _(dve):
                    for s in (hid_ready, gate_ready, glu_ready, up_ready, act_ready, y_ready):
                        dve.sem_inc(s, 2)
                    load = expert_loader(dve)
                    hidden(0, 0, load(0))
                    gate(0, 0)

                    def step(it, n, e):
                        activate(it, n)
                        hidden(it, n + 1, e)
                        output(it, n - 1, e)
                        gate(it, n + 1)

                    run_steps(dve, step, load)

        with ExitStack() as ph:
            xr = [sb(f"xr{h}", [P, CT, D], where=ph) for h in range(2)]
            yg = [sb(f"yg{h}", [P, CT, TOP_K, D], where=ph) for h in range(2)]
            yslot = [sb(f"yslot{h}", [P, CT, TOP_K], U32, where=ph) for h in range(2)]
            yw = [sb(f"yw{h}", [P, CT, TOP_K], where=ph) for h in range(2)]
            d1x = sb("d1x", [P, NH, CT], where=ph)
            d1e = sb("d1e", [P, NH // 2, CT, 2], where=ph)
            sq = sb("sq", [P, NH // 2, CT * 2 * DH], where=ph)
            square_sum = sb("square_sum", [P, NH // 2, CT * 2 * DH // GROUP], where=ph)
            root = sb("root", [P, NH // 2, CT * 2 * DH // GROUP], where=ph)
            On = sb("On", [P, CT, D], where=ph)
            OnT = sb("OnT", [P, CT, HC, P], where=ph)
            ff = [sb(f"ff{h}", [P, CT, D], where=ph) for h in range(2)]
            ft = [sb(f"ft{h}", [P, CT, D], where=ph) for h in range(2)]

            xr_loaded = [sem(f"xr_loaded{h}") for h in range(2)]
            picked = sem("picked")
            gather_begun = sem("gather_begun")
            y_gathered = [sem(f"y_gathered{h}") for h in range(2)]
            sq_ready = sem("sq_ready")
            d1_step = sem("d1_step")
            summed = sem("summed")
            ms_ready = sem("ms_ready")
            root_ready = sem("root_ready")
            recip_ready = sem("recip_ready")
            on_ready = sem("on_ready")
            on_turned = sem("on_turned")
            onT_ready = sem("onT_ready")
            att_bank = sem("att_bank")
            ff_half = sem("ff_half")
            ff_ready = sem("ff_ready")
            ft_ready = sem("ft_ready")
            silu_ready = sem("silu_ready")
            gated = sem("gated")
            res_ready = sem("res_ready")
            stored = [sem(f"stored{h}") for h in range(2)]
            tbank = [bank[2][:, 0:CH], bank[2][:, CH:]]
            wbank = [bank6, bank7]
            HT = CT // 2
            half_gain = math.sqrt(GROUP) * (1.0 - L_INIT) / 2

            with nc.Block() as block:
                @block.sync
                def _(sp):
                    x_v = x.rearrange("(b h t p) d -> b h p t d", b=B, h=2, p=P)
                    out_v = out.rearrange("(b h t p) d -> b h p t d", b=B, h=2, p=P)

                    def load_x(b, h):
                        sp.dma_start(xr[h][:], x_v[b, h]).then_inc(xr_loaded[h], 16)

                    def store(b, h):
                        sp.wait_ge(res_ready, credited(b, 2, h))
                        sp.dma_start(out_v[b, h], ff[h][:]).then_inc(stored[h], 16)

                    for h in range(2):
                        sp.sem_inc(stored[h], 16)
                        load_x(0, h)
                    with sp.Fori(0, B - 1) as b:
                        for h in range(2):
                            store(b, h)
                            load_x(b + 1, h)
                    for h in range(2):
                        store(B - 1, h)
                    for h in range(2):
                        sp.wait_ge(stored[h], 16 * (B + 1))

                @block.gpsimd
                def _(pool):
                    pool.sem_inc(picked, 4)
                    with pool.Fori(0, B) as b:
                        for h in range(2):
                            pool.wait_ge(ff_ready, credited(b, 2, h - 2))
                            c = b * QT + h * CT
                            nc.gpsimd.tensor_copy(yslot[h][:], slot_of[:, bass.ds(c, CT), :]).then_inc(picked, 1)
                            nc.gpsimd.tensor_copy(yw[h][:], weight[:, bass.ds(c, CT), :]).then_inc(picked, 1)
                            pool.wait_ge(picked, credited(b, 4, 2 * h + 1))
                            pool.sem_inc(gather_begun, 1)
                            for i in range(CT):
                                for k in range(TOP_K):
                                    pool.indirect_dma_start(
                                        yg[h][:, i, k, :], None, ys_dram,
                                        bass.IndirectOffsetOnAxis(yslot[h][:, i, k:k + 1], 0)
                                    ).then_inc(y_gathered[h], 16)

                def outputs(b, h):
                    return VO[:, bass.ds(b * (NH // 2), NH // 2), h * CT:(h + 1) * CT, :].rearrange(
                        "p j t d -> p j (t d)")

                def run_chunks(eng, first, second):
                    def batch(b, more):
                        for h in range(2):
                            if more or h == 0:
                                first(b + (h + 1) // 2, (h + 1) % 2)
                            second(b, h)

                    first(0, 0)
                    with eng.Fori(0, B - 1) as b:
                        batch(b, True)
                    batch(B - 1, False)

                @block.tensor
                def _(pe):
                    for s in (on_turned, att_bank):
                        pe.sem_inc(s, 4)

                    def project(b, h):
                        pe.wait_ge(on_ready, credited(b, 4, 2 * h + 1))
                        for k in range(2):
                            pe.wait_ge(onT_ready, credited(b, 4, 2 * h + k - 2))
                            for t in range(HT):
                                for c in range(HC):
                                    n = t * HC + c
                                    last = nc.tensor.transpose(tbank[k][:, n * P:(n + 1) * P],
                                                               On[:, k * HT + t, c * P:(c + 1) * P], ident[:])
                            last.then_inc(on_turned, 1)
                        pe.wait_ge(gated, credited(b, 2, h - 1))
                        for k in range(2):
                            pe.wait_ge(onT_ready, credited(b, 4, 2 * h + k))
                            for t in range(HT):
                                for c in range(HC):
                                    last = nc.tensor.matmul(wbank[k][:, t * D:(t + 1) * D],
                                                            OnT[:, k * HT + t, c, :], wo_sb[:, c, :],
                                                            start=(c == 0), stop=(c == HC - 1))
                            last.then_inc(att_bank, 1)

                    with pe.Fori(0, B) as b:
                        for h in range(2):
                            project(b, h)

                @block.scalar
                def _(act):
                    act.sem_inc(onT_ready, 4)
                    for s in (sq_ready, root_ready, ft_ready):
                        act.sem_inc(s, 2)

                    def squares(b, h):
                        act.wait_ge(ms_ready, credited(b, 2, h - 1))
                        nc.scalar.activation(sq[:], outputs(b, h), ACT.Square).then_inc(sq_ready, 1)

                    def curves(b, h):
                        act.wait_ge(on_ready, credited(b, 4, 2 * h - 1))
                        act.wait_ge(ms_ready, credited(b, 2, h))
                        nc.scalar.activation(root[:], square_sum[:], ACT.Sqrt, scale=1.0 / half_gain ** 2
                                             ).then_inc(root_ready, 1)
                        act.wait_ge(res_ready, credited(b, 2, h - 2))
                        act.wait_ge(ff_ready, credited(b, 2, h))
                        nc.scalar.activation(ft[h][:], ff[h][:], ACT.Tanh, scale=0.5).then_inc(ft_ready, 1)

                    def turned_out(b, h):
                        act.wait_ge(att_bank, credited(b, 4, 2 * h - 1))
                        for k in range(2):
                            act.wait_ge(on_turned, credited(b, 4, 2 * h + k))
                            nc.scalar.copy(OnT[:, k * HT:(k + 1) * HT, :, :].rearrange("p t c n -> p (t c n)"),
                                           tbank[k]).then_inc(onT_ready, 1)

                    squares(0, 0)
                    curves(0, 0)

                    def batch(b, more):
                        for h in range(2):
                            after = (b + (h + 1) // 2, (h + 1) % 2)
                            if more or h == 0:
                                squares(*after)
                            turned_out(b, h)
                            if more or h == 0:
                                curves(*after)

                    with act.Fori(0, B - 1) as b:
                        batch(b, True)
                    batch(B - 1, False)

                @block.vector
                def _(dve):
                    for s in (on_ready, d1_step):
                        dve.sem_inc(s, 4)
                    for s in (summed, ms_ready, recip_ready, ff_half, ff_ready, silu_ready, gated, res_ready):
                        dve.sem_inc(s, 2)

                    def normalise(b, h):
                        nc.vector.tensor_copy(d1x[:], d1_all[:, bass.ds(b * NH, NH), h * CT:(h + 1) * CT]
                                              ).then_inc(d1_step, 1)
                        dve.wait_ge(d1_step, credited(b, 4, 2 * h))
                        d1p = d1x[:].rearrange("p (j u) t -> p j u t", u=2)
                        nc.vector.tensor_tensor(d1e[:].rearrange("p j t u -> p j u t"), d1p, d1p, ALU.mult
                                                ).then_inc(d1_step, 1)
                        dve.wait_ge(sq_ready, credited(b, 2, h))
                        dve.wait_ge(root_ready, credited(b, 2, h - 1))
                        nc.vector.tensor_reduce(square_sum[:], sq[:].rearrange("p j (a c) -> p j a c", c=GROUP), AX.X,
                                                ALU.add).then_inc(summed, 1)
                        dve.wait_ge(d1_step, credited(b, 4, 2 * h + 1))
                        dve.wait_ge(summed, credited(b, 2, h))
                        per_head = square_sum[:].rearrange("p j (n a) -> p (j n) a", a=DH // GROUP)
                        nc.vector.scalar_tensor_tensor(
                            out=per_head, in0=d1e[:].rearrange("p j t u -> p (j t u)").unsqueeze(2)
                            .broadcast_to([P, CT * NH, DH // GROUP]), scalar=GROUP * RMS_EPS, in1=per_head,
                            op0=ALU.mult, op1=ALU.add).then_inc(ms_ready, 1)
                        dve.wait_ge(y_gathered[h], 16 * CT * TOP_K * (b + 1))
                        dve.wait_ge(picked, credited(b, 4, 2 * h + 1))
                        dve.wait_ge(stored[h], 16 * (b + 1))
                        for i in range(CT):
                            last = nc.vector.tensor_scalar(ff[h][:, i, :], yg[h][:, i, 0, :], yw[h][:, i, 0:1],
                                                           None, ALU.mult)
                        last.then_inc(ff_half, 1)
                        dve.wait_ge(ff_half, credited(b, 2, h))
                        for i in range(CT):
                            last = nc.vector.scalar_tensor_tensor(
                                out=ff[h][:, i, :], in0=yg[h][:, i, 1, :], scalar=yw[h][:, i, 1:2],
                                in1=ff[h][:, i, :], op0=ALU.mult, op1=ALU.add)
                        last.then_inc(ff_ready, 1)
                        dve.wait_ge(root_ready, credited(b, 2, h))
                        nc.vector.reciprocal(root[:], root[:]).then_inc(recip_ready, 1)
                        dve.wait_ge(recip_ready, credited(b, 2, h))
                        dve.wait_ge(on_turned, credited(b, 4, 2 * h - 1))
                        for k in range(2):
                            for j in range(2 * k, 2 * k + 2):
                                to = On[:, :, j * 2 * DH:(j + 1) * 2 * DH].rearrange(
                                    "p t (a c) -> p t a c", c=GROUP)
                                o4 = VO[:, bass.ds(b * (NH // 2) + j, 1), h * CT:(h + 1) * CT, :].rearrange(
                                    "p o t (a c) -> p (o t) a c", c=GROUP)
                                r4 = root[:, j, :].rearrange("p (t a) -> p t a", t=CT).unsqueeze(3).broadcast_to(
                                    [P, CT, 2 * DH // GROUP, GROUP])
                                last = nc.vector.tensor_tensor(to, o4, r4, ALU.mult)
                            last.then_inc(on_ready, 1)

                    def finish(b, h):
                        dve.wait_ge(ft_ready, credited(b, 2, h))
                        nc.vector.scalar_tensor_tensor(out=ft[h][:], in0=ft[h][:], scalar=1.0, in1=ff[h][:],
                                                       op0=ALU.add, op1=ALU.mult).then_inc(silu_ready, 1)
                        dve.wait_ge(silu_ready, credited(b, 2, h))
                        for k in range(2):
                            dve.wait_ge(att_bank, credited(b, 4, 2 * h + k))
                            part = ft[h][:, k * HT:(k + 1) * HT, :].rearrange("p t d -> p (t d)")
                            last = nc.vector.tensor_tensor(part, part, wbank[k][:], ALU.mult)
                        last.then_inc(gated, 1)
                        dve.wait_ge(gated, credited(b, 2, h))
                        dve.wait_ge(xr_loaded[h], 16 * (b + 1))
                        nc.vector.tensor_tensor(ff[h][:], ft[h][:], xr[h][:], ALU.add).then_inc(res_ready, 1)

                    run_chunks(dve, normalise, finish)


def kernel(L0_attn_x, L0_attn_l_q1, L0_attn_l_k1, L0_attn_l_q2, L0_attn_l_k2, L0_attn_wq, L0_attn_wk, L0_attn_wv,
           L0_attn_wo, L0_ffn_router_weight, L0_ffn_router_bias, L0_ffn_gate_up_proj, L0_ffn_gate_up_proj_bias,
           L0_ffn_down_proj, L0_ffn_down_proj_bias):
    import numpy as np
    import concourse.bacc as bacc
    from concourse.bass_utils import run_bass_kernel_spmd

    def heads(w):
        return np.asarray(w).reshape(2, NH, DH, D).transpose(3, 1, 0, 2).reshape(D, 2 * NH * DH)

    arrays = {
        "x": np.asarray(L0_attn_x).reshape(T, D),
        "wqk": np.concatenate([heads(L0_attn_wq), heads(L0_attn_wk)], axis=1),
        "wv": np.asarray(L0_attn_wv).T,
        "wo": np.asarray(L0_attn_wo).T,
        "lam": np.stack([np.asarray(a) for a in (L0_attn_l_q1, L0_attn_l_k1, L0_attn_l_q2, L0_attn_l_k2)]),
        "rw": np.asarray(L0_ffn_router_weight).T,
        "rb": np.asarray(L0_ffn_router_bias),
        "gu": np.asarray(L0_ffn_gate_up_proj).reshape(E, D, I, 2).transpose(1, 0, 3, 2).reshape(D, E, 2 * I),
        "gub": np.asarray(L0_ffn_gate_up_proj_bias).reshape(E, I, 2).transpose(0, 2, 1).reshape(E, 2 * I),
        "dn": np.asarray(L0_ffn_down_proj).transpose(1, 0, 2),
        "dnb": np.asarray(L0_ffn_down_proj_bias),
    }
    arrays = {name: np.ascontiguousarray(a) for name, a in arrays.items()}
    nc = bacc.Bacc("TRN2", target_bir_lowering=False, num_devices=1)
    args = [nc.dram_tensor(name, a.shape, mybir.dt.from_np(a.dtype), kind="ExternalInput").ap()
            for name, a in arrays.items()]
    out = nc.dram_tensor("out", (T, D), F32, kind="ExternalOutput").ap()
    build(nc, *args, out)
    r = run_bass_kernel_spmd(nc, [arrays], core_ids=[0])
    return r.results[0]["out"].reshape(B, S, D)
```

```python
import math
from contextlib import ExitStack

import concourse.bass as bass
from concourse import mybir

F32 = mybir.dt.float32
F32R = mybir.dt.float32r
BF16 = mybir.dt.bfloat16
U32 = mybir.dt.uint32
I32 = mybir.dt.int32
ALU = mybir.AluOpType
ACT = mybir.ActivationFunctionType
AX = mybir.AxisListType

B, S, D = 4, 1024, 256
NH, DH = 8, 32
T = B * S
E, I, LIMIT, ALPHA = 8, 256, 7.0, 1.702
L_INIT = 0.8 - 0.6 * math.exp(-0.3 * 1)
LN_EPS, RMS_EPS = 1e-5, 1e-6
GROUP = DH // NH
P = 128
HC = D // P
CH = 512
CT = CH // P
NCH = T // CH
QT = S // P
MASKED = -1.0e30

QKT = 2 * 2 * NH * DH // P
NIT = B * NH // 2
STEPS = 2 * 2 * QT
NQ = 2 * QT
TOP_K = 2
SLOT_TILES = T * TOP_K // P + E
KB_UNIT = 4


def credited(it, per, event):
    return (it + 1) * per + event + 1


ORDER = [q for pair in zip(range(QT // 2, QT), range(QT // 2)) for q in pair]
USES = 2 * 3 * QT // 2
SLOTS = 3


def query(n):
    return n % NQ // QT, ORDER[n % QT]


def uses(n):
    first = 3 * (n // 2)
    return [(first, [0]), (first + 1, [1])] if n % 2 == 0 else [(first + 2, [0, 1])]


def last_step(use):
    pair, k = divmod(use, 3)
    return 4 * pair + [0, 1, 3][k]


def gathers(n):
    return [(n - 5) // 4] if n % 4 == 1 else []


def units(n):
    count = sum(-(-(query(i)[1] + 1) // KB_UNIT) for i in range(n))
    first = count + sum(len(gathers(i)) for i in range(n))
    blocks = list(range(query(n)[1] + 1))
    return [(first + k, count + k, blocks[KB_UNIT * k:KB_UNIT * (k + 1)])
            for k in range(-(-len(blocks) // KB_UNIT))]


UNITS = units(NQ - 1)[-1][1] + 1
SORT_AT = {4: (0, 0), 6: (0, 1), 10: (1, 0), 12: (1, 1)}
FILLS = UNITS + 4
LONG_PR, SHORT_PR = 4, 4


def place(it, n):
    return it + n // NQ, n % NQ


def absent(it, n):
    return isinstance(it, int) and (it == 0 and n < 0 or it == NIT - 1 and n >= NQ)


def build(nc, x, wqk, wv, wo, lam, rw, rb, gu, gub, dn, dnb, out):
    with ExitStack() as ctx:
        def sb(name, shape, dt=F32, where=ctx):
            return where.enter_context(nc.sbuf_tensor(name, shape, dt))

        def sem(name):
            return ctx.enter_context(nc.semaphore(name))

        q_parts = nc.dram_tensor("q_parts", (NIT, 2, P, S), F32, kind="Internal").ap()
        k_parts = nc.dram_tensor("k_parts", (NIT, 2, P, S), F32, kind="Internal").ap()
        xn_dram = nc.dram_tensor("xn_dram", (T, D), F32, kind="Internal").ap()
        xs_dram = nc.dram_tensor("xs_dram", (SLOT_TILES * P, D), F32, kind="Internal").ap()
        ys_dram = nc.dram_tensor("ys_dram", (SLOT_TILES * P, D), F32, kind="Internal").ap()

        bank = [ctx.enter_context(nc.psum_tensor(f"bank{i}", [P, 2 * CH], F32)) for i in range(3)]
        bank6 = ctx.enter_context(nc.psum_tensor("bank6", [P, CH], F32))
        bank7 = ctx.enter_context(nc.psum_tensor("bank7", [P, CH], F32))

        ident = sb("ident", [P, P])
        identb = sb("identb", [P, P], BF16)
        maskb = sb("maskb", [P, P], BF16)
        zerob = sb("zerob", [P, CH], BF16)
        gather4 = sb("gather4", [P, DH])
        VO = sb("VO", [P, NIT, QT, 2 * DH])
        d1_all = sb("d1_all", [P, B * NH, QT])
        lam_in = sb("lam_in", [P, 4, NH])
        lam_w = sb("lam_w", [P, 2, NH])
        lam_s = sb("lam_s", [P, 8])
        neg_lam = lam_s[:, 6:7]
        wo_sb = sb("wo_sb", [P, HC, D])
        weight = sb("weight", [P, T // P, TOP_K])
        slot_of = sb("slot_of", [P, T // P, TOP_K], U32)
        expert_rows = sb("expert_rows", [P, SLOT_TILES // 2, 4], I32)

        Qs_first = sb("Qs_first", [P, 2, S], F32R)
        Ks_first = sb("Ks_first", [P, 2, S], F32R)
        qk_loaded = [sem(f"qk_loaded{u}") for u in range(2)]

        def load_head(sp, it, u, Q, K):
            rows = slice(u * 2 * DH, (u + 1) * 2 * DH)
            for g in range(4):
                qp = q_parts[it, g % 2, rows, :].rearrange("(m d) t -> d m t", m=2)
                kp = k_parts[it, g // 2, rows, :].rearrange("(m d) t -> d m t", m=2)
                sp.dma_start(Q[g * DH:(g + 1) * DH, :, :].bitcast(F32), qp).then_inc(qk_loaded[u], 16)
                sp.dma_start(K[g * DH:(g + 1) * DH, :, :].bitcast(F32), kp).then_inc(qk_loaded[u], 16)

        consts_done = sem("consts_done")
        lam_step = sem("lam_step")
        ew_loaded = sem("ew_loaded")
        const_step = sem("const_step")

        with ExitStack() as ph:
            wqk_sb = sb("wqk_sb", [P, HC, QKT * P], where=ph)
            wv_sb = sb("wv_sb", [P, HC, D + E], where=ph)
            rb_sb = sb("rb_sb", [P, E], where=ph)
            zeros = sb("zeros", [P, SLOT_TILES // NCH * D], where=ph)
            before = sb("before", [P, E, E], where=ph)
            earlier = sb("earlier", [P, P], BF16, where=ph)
            ones = sb("ones", [P, P], BF16, where=ph)
            count_i = sb("count_i", [P, SLOT_TILES], I32, where=ph)
            count_f = sb("count_f", [P, SLOT_TILES], where=ph)
            count_128 = sb("count_128", [P, T // P], where=ph)
            logits = sb("logits", [P, T // P, E], where=ph)
            cmp = sb("cmp", [P, T // P * E * TOP_K + 2 * SLOT_TILES * E], where=ph)
            ranks = sb("ranks", [P, 3, QT, E], where=ph)
            chosen = sb("chosen", [P, TOP_K, T // P, E], where=ph)
            chosen_b = sb("chosen_b", [P, T // P, E], BF16, where=ph)
            top = sb("top", [P, 6, T // P], where=ph)
            run = [sb(f"run{i}", [P, T // P, E], where=ph) for i in range(2)]
            per_e = sb("per_e", [P, 8, E], where=ph)
            wqk_parts = sb("wqk_parts", [P, 2, HC, QKT * P], F32R, where=ph)
            XNT_parts = sb("XNT_parts", [P, 2, HC, CH], F32R, where=ph)
            X = [sb(f"X{h}", [P, CT, D], where=ph) for h in range(2)]
            XN = [sb(f"XN{h}", [P, CT, D], where=ph) for h in range(2)]
            XNT = [sb(f"XNT{h}", [P, HC, CH], where=ph) for h in range(2)]
            PARTS = [sb(f"PARTS{i}", [P, 2, CH], F32R, where=ph) for i in range(4)]
            stats = sb("stats", [P, CT, 6], where=ph)
            mv = sb("mv", [P, CT, 2], where=ph)
            ve = sb("ve", [P, CT], where=ph)
            sd = sb("sd", [P, CT], where=ph)
            rs = sb("rs", [P, CT], where=ph)
            nt = sb("nt", [P, CT], where=ph)

            w_loaded = sem("w_loaded")
            x_loaded = [sem(f"x_loaded{h}") for h in range(2)]
            ln_step = sem("ln_step")
            stats_seen = sem("stats_seen")
            var_ready = sem("var_ready")
            std_ready = sem("std_ready")
            xn_ready = sem("xn_ready")
            xnT_bank = sem("xnT_bank")
            xnT_ready = sem("xnT_ready")
            xnT_hi = sem("xnT_hi")
            xnT_lo = sem("xnT_lo")
            w_hi = sem("w_hi")
            w_lo = sem("w_lo")
            wqk_loaded = sem("wqk_loaded")
            qk_bank = sem("qk_bank")
            hi_ready = sem("hi_ready")
            lo_ready = sem("lo_ready")
            v_bank = sem("v_bank")
            v_ready = sem("v_ready")
            parts_stored = [sem(f"parts_stored{i}") for i in range(4)]
            xn_stored = [sem(f"xn_stored{h}") for h in range(2)]
            logits_ready = sem("logits_ready")
            zeros_ready = sem("zeros_ready")
            zeros_stored = sem("zeros_stored")
            rank_step = sem("rank_step")
            route = sem("route")
            chosen_ready = sem("chosen_ready")
            ranks_bank = sem("ranks_bank")
            gap_ready = sem("gap_ready")
            odds_ready = sem("odds_ready")

            tbank = [bank[0][:, 0:CH], bank[0][:, CH:]]
            qkbank = [bank[1][:, 0:CH], bank[1][:, CH:], bank[2][:, 0:CH], bank[2][:, CH:]]
            vbank = [bank6, bank7]
            LN_OPS = 13
            NORMALISE_AFTER = (1, 3, 5)
            RANK_OPS = 11

            with nc.Block() as block:
                @block.gpsimd
                def _(pool):
                    nc.gpsimd.memset(ident[:], 0.0).then_inc(const_step, 1)
                    nc.gpsimd.memset(maskb[:], 0.0).then_inc(const_step, 1)
                    nc.gpsimd.memset(gather4[:], 0.0).then_inc(const_step, 1)
                    nc.gpsimd.memset(zerob[:], 0.0).then_inc(consts_done, 1)
                    pool.wait_ge(const_step, 3)
                    nc.gpsimd.affine_select(out=ident[:], in_=ident[:], compare_op=ALU.not_equal, fill=1.0,
                                            base=0, pattern=[[-1, P]], channel_multiplier=1).then_inc(const_step, 1)
                    nc.gpsimd.affine_select(out=maskb[:], in_=maskb[:], compare_op=ALU.is_ge, fill=MASKED,
                                            base=0, pattern=[[-1, P]], channel_multiplier=1).then_inc(consts_done, 1)
                    for g in range(4):
                        nc.gpsimd.affine_select(out=gather4[:], in_=gather4[:],
                                                compare_op=ALU.not_equal, fill=1.0, base=-32 * g,
                                                pattern=[[-1, 32]], channel_multiplier=1).then_inc(const_step, 1)
                        pool.wait_ge(const_step, 5 + g)
                    nc.gpsimd.tensor_copy(identb[:], ident[:]).then_inc(consts_done, 1)
                    nc.gpsimd.memset(zeros[:], 0.0).then_inc(zeros_ready, 1)
                    nc.gpsimd.memset(before[:], 1.0).then_inc(const_step, 1)
                    nc.gpsimd.memset(earlier[:], 1.0).then_inc(const_step, 1)
                    nc.gpsimd.memset(ones[:], 1.0).then_inc(consts_done, 1)
                    nc.gpsimd.iota(count_i[:], pattern=[[1, SLOT_TILES]], base=0, channel_multiplier=0
                                   ).then_inc(const_step, 1)
                    pool.wait_ge(const_step, 11)
                    nc.gpsimd.affine_select(out=before[:], in_=before[:], compare_op=ALU.is_gt, fill=0.0, base=0,
                                            pattern=[[1, E], [-1, E]], channel_multiplier=0
                                            ).then_inc(consts_done, 1)
                    nc.gpsimd.affine_select(out=earlier[:], in_=earlier[:], compare_op=ALU.is_gt, fill=0.0,
                                            base=0, pattern=[[1, P]], channel_multiplier=-1
                                            ).then_inc(consts_done, 1)
                    nc.gpsimd.tensor_copy(count_f[:], count_i[:]).then_inc(const_step, 1)
                    pool.wait_ge(const_step, 12)
                    nc.gpsimd.tensor_scalar(count_128[:], count_f[:, 0:T // P], float(P), None, ALU.mult
                                            ).then_inc(consts_done, 1)

                @block.sync
                def _(sp):
                    x_v = x.rearrange("(b h t p) d -> b h p t d", b=B, h=2, p=P)
                    sp.dma_start(X[0][:], x_v[0, 0]).then_inc(x_loaded[0], 16)
                    sp.dma_start(wqk_sb[:], wqk.rearrange("(c p) n -> p c n", p=P)).then_inc(wqk_loaded, 16)
                    sp.dma_start(X[1][:], x_v[0, 1]).then_inc(x_loaded[1], 16)
                    sp.dma_start(wv_sb[:, :, 0:D], wv.rearrange("(c p) n -> p c n", p=P)).then_inc(w_loaded, 16)
                    sp.dma_start(wv_sb[:, :, D:], rw.rearrange("(c p) n -> p c n", p=P)).then_inc(w_loaded, 16)
                    sp.dma_start(rb_sb[:], rb.partition_broadcast(P)).then_inc(w_loaded, 16)
                    sp.dma_start(lam_in[:], lam.partition_broadcast(P)).then_inc(w_loaded, 16)
                    sp.dma_start(wo_sb[:], wo.rearrange("(c p) n -> p c n", p=P)).then_inc(w_loaded, 16)

                    xn_v = xn_dram.rearrange("(c t p) d -> c p t d", c=NCH, p=P)

                    sp.wait_ge(zeros_ready, 1)
                    xs_v = xs_dram.rearrange("(n p r) d -> n p (r d)", p=P, r=SLOT_TILES // NCH)

                    def chunk(b, h):
                        sp.dma_start(xs_v[b * 2 + h], zeros[:]).then_inc(zeros_stored, 16)
                        sp.wait_ge(xn_ready, credited(b, 2, h))
                        sp.dma_start(xn_v[b * 2 + h], XN[h][:]).then_inc(xn_stored[h], 16)
                        for i in range(QKT):
                            sp.wait_ge(hi_ready, credited(b, 2 * QKT, h * QKT + i))
                            sp.wait_ge(lo_ready, credited(b, 2 * QKT, h * QKT + i))
                            dst = (q_parts if i < QKT // 2 else k_parts)[
                                b * 4 + i % 4, :, :, h * CH:(h + 1) * CH]
                            sp.dma_start(dst.rearrange("l p n -> p l n"), PARTS[i % 4][:].bitcast(F32)
                                         ).then_inc(parts_stored[i % 4], 16)

                    with sp.Fori(0, B - 1) as b:
                        for h in range(2):
                            sp.wait_ge(xn_ready, credited(b, 2, h))
                            sp.dma_start(X[h][:], x_v[b + 1, h]).then_inc(x_loaded[h], 16)
                            chunk(b, h)
                    sp.wait_ge(parts_stored[0], 16 * 5)
                    load_head(sp, 0, 0, Qs_first, Ks_first)
                    for h in range(2):
                        chunk(B - 1, h)
                    for h in range(2):
                        sp.wait_ge(xn_stored[h], 16 * (B + 1))
                    for i in range(4):
                        sp.wait_ge(parts_stored[i], 16 * (4 * B + 1))
                    sp.wait_ge(zeros_stored, 16 * NCH)

                @block.vector
                def _(dve):
                    dve.sem_inc(ln_step, 2 * LN_OPS)
                    dve.sem_inc(xn_ready, 2)
                    dve.sem_inc(xnT_lo, 4)
                    dve.sem_inc(var_ready, 2)
                    dve.sem_inc(lo_ready, 2 * QKT)
                    dve.sem_inc(logits_ready, 8)

                    def variance(b, h):
                        b, h = b + h // 2, h % 2
                        base = h * LN_OPS
                        dve.wait_ge(x_loaded[h], 16 * (b + 1))
                        for i in range(CT):
                            nc.vector.bn_stats(stats[:, i, :], X[h][:, i, :]).then_inc(ln_step, 1)
                        for i in range(CT):
                            if i == 0:
                                dve.wait_ge(ln_step, credited(b, 2 * LN_OPS, base + 3))
                                dve.sem_inc(stats_seen, 1)
                            nc.vector.bn_aggr(mv[:, i, :], stats[:, i, :]).then_inc(ln_step, 1)
                        dve.wait_ge(ln_step, credited(b, 2 * LN_OPS, base + 7))
                        nc.vector.tensor_scalar(ve[:], mv[:, :, 1], LN_EPS, None, ALU.add).then_inc(var_ready, 1)

                    def inverse_deviation(b, h):
                        b, h = b + h // 2, h % 2
                        base = h * LN_OPS
                        dve.wait_ge(std_ready, credited(b, 2, h))
                        nc.vector.reciprocal(rs[:], sd[:]).then_inc(ln_step, 1)
                        dve.wait_ge(ln_step, credited(b, 2 * LN_OPS, base + 8))
                        nc.vector.tensor_tensor(nt[:], rs[:], rs[:], ALU.mult).then_inc(ln_step, 1)
                        dve.wait_ge(ln_step, credited(b, 2 * LN_OPS, base + 9))
                        nc.vector.tensor_tensor(nt[:], nt[:], ve[:], ALU.mult).then_inc(ln_step, 1)
                        dve.wait_ge(ln_step, credited(b, 2 * LN_OPS, base + 10))
                        nc.vector.tensor_scalar(nt[:], nt[:], -0.5, 1.5, ALU.mult, ALU.add).then_inc(ln_step, 1)
                        dve.wait_ge(ln_step, credited(b, 2 * LN_OPS, base + 11))
                        nc.vector.tensor_tensor(rs[:], rs[:], nt[:], ALU.mult).then_inc(ln_step, 1)

                    def normalise(b, h):
                        b, h = b + h // 2, h % 2
                        dve.wait_ge(ln_step, credited(b, 2 * LN_OPS, h * LN_OPS + 12))
                        dve.wait_ge(xn_stored[h], 16 * (b + 1))
                        dve.wait_ge(xnT_bank, credited(b, 4, 2 * h + 1 - 4))
                        for i in range(CT):
                            last = nc.vector.tensor_scalar(XN[h][:, i, :], X[h][:, i, :], mv[:, i, 0:1],
                                                           rs[:, i:i + 1], ALU.subtract, ALU.mult)
                        last.then_inc(xn_ready, 1)

                    def low_rows(b, h):
                        b, h = b + h // 2, h % 2
                        for c in range(HC):
                            dve.wait_ge(xnT_hi, credited(b, 4, 2 * h + c))
                            nc.vector.tensor_tensor(XNT_parts[:, 1, c, :], tbank[c],
                                                    XNT_parts[:, 0, c, :].bitcast(F32), ALU.subtract
                                                    ).then_inc(xnT_lo, 1)

                    def rank(b):
                        done = [0]

                        def then(ins):
                            ins.then_inc(rank_step, 1)
                            done[0] += 1
                            dve.wait_ge(rank_step, b * RANK_OPS + done[0])

                        tiles = bass.ds(b * QT, QT)
                        dve.wait_ge(logits_ready, credited(b, 8, 7))
                        own = logits[:, tiles, :].unsqueeze(3).broadcast_to([P, QT, E, E])
                        other = logits[:, tiles, :].unsqueeze(2).broadcast_to([P, QT, E, E])
                        c4 = cmp[:, 0:QT * E * E].rearrange("p (t e f) -> p t e f", e=E, f=E)
                        c3 = cmp[:, 0:QT * E * E].rearrange("p (t k) -> p t k", t=QT)
                        then(nc.vector.tensor_tensor(c4, other, own, ALU.is_equal))
                        then(nc.vector.tensor_tensor(c3, c3, before[:].rearrange("p e f -> p (e f)").unsqueeze(1)
                                                     .broadcast_to([P, QT, E * E]), ALU.mult))
                        then(nc.vector.tensor_reduce(ranks[:, 0], c4, AX.X, ALU.add))
                        then(nc.vector.tensor_tensor(c4, other, own, ALU.is_gt))
                        then(nc.vector.tensor_reduce(ranks[:, 1], c4, AX.X, ALU.add))
                        then(nc.vector.tensor_tensor(ranks[:, 2], ranks[:, 0], ranks[:, 1], ALU.add))
                        for k in range(TOP_K):
                            then(nc.vector.tensor_scalar(chosen[:, k, tiles, :], ranks[:, 2], float(k), None,
                                                         ALU.is_equal))
                        nc.vector.tensor_tensor(chosen_b[:, tiles, :], chosen[:, 0, tiles, :],
                                                chosen[:, 1, tiles, :], ALU.add).then_inc(chosen_ready, 1)
                        ck = cmp[:, 0:TOP_K * QT * E].rearrange("p (k t e) -> p k t e", k=TOP_K, e=E)
                        for k in range(TOP_K):
                            then(nc.vector.tensor_tensor(ck[:, k], chosen[:, k, tiles, :], logits[:, tiles, :],
                                                         ALU.mult))
                        then(nc.vector.tensor_reduce(top[:, 0:2, tiles], ck, AX.X, ALU.add))

                    def low_parts(b, h, tiles, then_normalise=False):
                        for i in tiles:
                            dve.wait_ge(hi_ready, credited(b, 2 * QKT, h * QKT + i))
                            scale = 1.0 / math.sqrt(DH) if i < QKT // 2 else 1.0
                            nc.vector.scalar_tensor_tensor(
                                out=PARTS[i % 4][:, 1, :], in0=qkbank[i % 4], scalar=scale,
                                in1=PARTS[i % 4][:, 0, :].bitcast(F32), op0=ALU.mult, op1=ALU.subtract
                            ).then_inc(lo_ready, 1)
                            if then_normalise and i in NORMALISE_AFTER:
                                (variance, inverse_deviation, normalise)[NORMALISE_AFTER.index(i)](b, h + 1)

                    def add_bias(b, h):
                        for i in range(CT):
                            dve.wait_ge(v_ready, credited(b, 8, 4 * h + i))
                            nc.vector.tensor_tensor(logits[:, bass.ds(b * QT + h * CT + i, 1), :],
                                                    vbank[i % 2][:, D:D + E].unsqueeze(1),
                                                    rb_sb[:].unsqueeze(1), ALU.add).then_inc(logits_ready, 1)

                    variance(0, 0)
                    inverse_deviation(0, 0)
                    normalise(0, 0)
                    dve.wait_ge(w_hi, 1)
                    nc.vector.tensor_tensor(wqk_parts[:, 1], wqk_sb[:], wqk_parts[:, 0].bitcast(F32), ALU.subtract
                                            ).then_inc(w_lo, 1)
                    low_rows(0, 0)
                    dve.wait_ge(consts_done, 7)
                    dve.wait_ge(w_loaded, 80)
                    nc.vector.tensor_tensor(lam_w[:], lam_in[:, 0:4:2, :], lam_in[:, 1:4:2, :], ALU.mult
                                            ).then_inc(lam_step, 1)
                    dve.wait_ge(lam_step, 1)
                    nc.vector.tensor_reduce(lam_s[:, 0:2], lam_w[:], AX.X, ALU.add).then_inc(lam_step, 1)
                    with dve.Fori(0, B - 1) as b:
                        for h in range(2):
                            low_parts(b, h, range(QKT), then_normalise=True)
                            low_rows(b, h + 1)
                            add_bias(b, h)
                        rank(b)
                    low_parts(B - 1, 0, range(QKT), then_normalise=True)
                    low_rows(B - 1, 1)
                    add_bias(B - 1, 0)
                    add_bias(B - 1, 1)
                    rank(B - 1)
                    low_parts(B - 1, 1, range(QKT // 2))

                    steps = [0]

                    def then(ins):
                        ins.then_inc(route, 1)
                        steps[0] += 1
                        dve.wait_ge(route, steps[0])

                    NT = T // P
                    ck = cmp[:, 0:TOP_K * NT * E].rearrange("p (k t e) -> p k t e", k=TOP_K, e=E)
                    nc.vector.tensor_tensor(top[:, 2], top[:, 1], top[:, 0], ALU.subtract).then_inc(gap_ready, 1)
                    dve.wait_ge(ranks_bank, 1)
                    pre = bank6[:, 0:NT * E].rearrange("p (t e) -> p t e", e=E)
                    tot = bank7[:, 0:NT * E].rearrange("p (t e) -> p t e", e=E)
                    nc.vector.memset(run[0][:, 0:1, :], 0.0)
                    then(nc.vector.tensor_copy(run[0][:, 1:NT, :], tot[:, 0:NT - 1, :]))
                    src, span = 0, 1
                    while span < NT:
                        nc.vector.tensor_copy(run[1 - src][:, 0:span, :], run[src][:, 0:span, :])
                        then(nc.vector.tensor_tensor(run[1 - src][:, span:, :], run[src][:, span:, :],
                                                     run[src][:, 0:NT - span, :], ALU.add))
                        src, span = 1 - src, 2 * span
                    low_parts(B - 1, 1, range(QKT // 2, QKT // 2 + 2))
                    tokens, tiles, first, end, first_slot = (per_e[:, i] for i in range(5))
                    then(nc.vector.tensor_tensor(tokens, run[src][:, NT - 1, :], tot[:, NT - 1, :], ALU.add))
                    ce = cmp[:, 0:E * NT].rearrange("p (e t) -> p e t", e=E)
                    then(nc.vector.tensor_tensor(ce, tokens.unsqueeze(2).broadcast_to([P, E, NT]),
                                                 count_128[:].unsqueeze(1).broadcast_to([P, E, NT]), ALU.is_gt))
                    then(nc.vector.tensor_reduce(tiles, ce, AX.X, ALU.add))
                    cf = cmp[:, 0:E * E].rearrange("p (e f) -> p e f", e=E)
                    then(nc.vector.tensor_tensor(cf, before[:], tiles.unsqueeze(1).broadcast_to([P, E, E]),
                                                 ALU.mult))
                    then(nc.vector.tensor_reduce(first, cf, AX.X, ALU.add))
                    then(nc.vector.tensor_tensor(end, first, tiles, ALU.add))
                    then(nc.vector.tensor_scalar(first_slot, first, float(P), None, ALU.mult))
                    cs = cmp[:, 0:SLOT_TILES * E].rearrange("p (s e) -> p s e", e=E)
                    then(nc.vector.tensor_tensor(cs, end.unsqueeze(1).broadcast_to([P, SLOT_TILES, E]),
                                                 count_f[:].unsqueeze(2).broadcast_to([P, SLOT_TILES, E]),
                                                 ALU.is_le))
                    then(nc.vector.tensor_reduce(cmp[:, SLOT_TILES * E:SLOT_TILES * (E + 1)], cs, AX.X, ALU.add))
                    pairs = cmp[:, SLOT_TILES * E:SLOT_TILES * (E + 1)].rearrange("p (i u) -> p i u", u=2)
                    NR = SLOT_TILES // 2
                    nc.vector.tensor_scalar(expert_rows[:, :, 0:2], pairs, float(E - 1), None, ALU.min)
                    nc.vector.tensor_scalar(expert_rows[:, 0:NR - 1, 2:4], pairs[:, 1:], float(E - 1), None, ALU.min)
                    then(nc.vector.memset(expert_rows[:, NR - 1:NR, 2:4], 0))
                    low_parts(B - 1, 1, range(QKT // 2 + 2, QKT))
                    then(nc.vector.tensor_tensor(run[1 - src][:], run[src][:], pre, ALU.add))
                    then(nc.vector.tensor_tensor(run[src][:], run[1 - src][:],
                                                 first_slot.unsqueeze(1).broadcast_to([P, NT, E]), ALU.add))
                    for k in range(TOP_K):
                        then(nc.vector.tensor_tensor(ck[:, k], chosen[:, k], run[src][:], ALU.mult))
                    then(nc.vector.tensor_reduce(top[:, 3:5], ck, AX.X, ALU.add))
                    then(nc.vector.tensor_copy(slot_of[:].rearrange("p t k -> p k t"), top[:, 3:5]))
                    dve.wait_ge(odds_ready, 1)
                    then(nc.vector.tensor_scalar(top[:, 4], top[:, 5], 1.0, None, ALU.add))
                    then(nc.vector.reciprocal(weight[:, :, 0], top[:, 4]))
                    then(nc.vector.tensor_tensor(weight[:, :, 1], weight[:, :, 0], top[:, 5], ALU.mult))
                    dve.wait_ge(lam_step, 3)
                    nc.vector.tensor_tensor(lam_s[:, 4:5], lam_s[:, 3:4], lam_s[:, 2:3], ALU.subtract
                                            ).then_inc(lam_step, 1)
                    dve.wait_ge(lam_step, 4)
                    nc.vector.tensor_scalar(neg_lam, lam_s[:, 4:5], -L_INIT, None, ALU.add
                                            ).then_inc(lam_step, 1)

                @block.scalar
                def _(act):
                    act.sem_inc(std_ready, 2)
                    act.sem_inc(xnT_ready, 4)
                    act.sem_inc(xnT_hi, 4)
                    act.sem_inc(hi_ready, 2 * QKT)
                    act.sem_inc(v_ready, 8)

                    def deviation(b, h):
                        b, h = b + h // 2, h % 2
                        act.wait_ge(var_ready, credited(b, 2, h))
                        nc.scalar.activation(sd[:], ve[:], ACT.Sqrt).then_inc(std_ready, 1)

                    def turned_rows(b, h):
                        b, h = b + h // 2, h % 2
                        act.wait_ge(v_bank, credited(b, 8, 4 * h + 3 - 8))
                        act.wait_ge(qk_bank, credited(b, 2 * QKT, h * QKT - 1))
                        for c in range(HC):
                            act.wait_ge(xnT_bank, credited(b, 4, 2 * h + c))
                            nc.scalar.copy(XNT_parts[:, 0, c, :], tbank[c]).then_inc(xnT_hi, 1)
                        for c in range(HC):
                            act.wait_ge(xnT_lo, credited(b, 4, 2 * h + c))
                            nc.scalar.copy(XNT[h][:, c, :], tbank[c]).then_inc(xnT_ready, 1)

                    def high_parts(b, h, tiles, more=False):
                        for i in tiles:
                            act.wait_ge(qk_bank, credited(b, 2 * QKT, h * QKT + i))
                            act.wait_ge(parts_stored[i % 4], 16 * (4 * b + 2 * h + i // 4 + 1))
                            scale = 1.0 / math.sqrt(DH) if i < QKT // 2 else 1.0
                            nc.scalar.mul(PARTS[i % 4][:, 0, :], qkbank[i % 4], scale).then_inc(hi_ready, 1)
                            if i == NORMALISE_AFTER[1] and more:
                                deviation(b, h + 1)

                    def values_out(b, h):
                        for i in range(CT):
                            act.wait_ge(v_bank, credited(b, 8, 4 * h + i))
                            nc.scalar.copy(VO[:, bass.ds(b * (NH // 2), NH // 2), h * CT + i, :],
                                           vbank[i % 2][:, 0:D].rearrange("p (j d) -> p j d", d=2 * DH)
                                           ).then_inc(v_ready, 1)

                    def chunk(b, h):
                        high_parts(b, h, range(QKT), more=True)
                        turned_rows(b, h + 1)
                        values_out(b, h)

                    deviation(0, 0)
                    act.wait_ge(wqk_loaded, 16)
                    nc.scalar.copy(wqk_parts[:, 0], wqk_sb[:]).then_inc(w_hi, 1)
                    turned_rows(0, 0)
                    with act.Fori(0, B - 1) as b:
                        for h in range(2):
                            chunk(b, h)
                    chunk(B - 1, 0)
                    values_out(B - 1, 1)
                    high_parts(B - 1, 1, range(QKT))
                    act.wait_ge(gap_ready, 1)
                    nc.scalar.activation(top[:, 5], top[:, 2], ACT.Exp).then_inc(odds_ready, 1)
                    act.wait_ge(lam_step, 2)
                    nc.scalar.activation(lam_s[:, 2:4], lam_s[:, 0:2], ACT.Exp).then_inc(lam_step, 1)

                @block.tensor
                def _(pe):
                    pe.sem_inc(xnT_bank, 4)
                    pe.sem_inc(qk_bank, 2 * QKT)
                    pe.sem_inc(v_bank, 8)
                    for h in range(2):
                        pe.sem_inc(xn_stored[h], 16)
                    for i in range(4):
                        pe.sem_inc(parts_stored[i], 16)
                    pe.wait_ge(consts_done, 7)

                    def turn_rows(b, h):
                        b, h = b + h // 2, h % 2
                        pe.wait_ge(xn_ready, credited(b, 2, h))
                        for c in range(HC):
                            pe.wait_ge(xnT_ready, credited(b, 4, 2 * h + c - 2))
                            for i in range(CT):
                                last = nc.tensor.transpose(tbank[c][:, i * P:(i + 1) * P],
                                                           XN[h][:, i, c * P:(c + 1) * P], ident[:])
                            last.then_inc(xnT_bank, 1)

                    def project(b, h, tiles):
                        pe.wait_ge(xnT_lo, credited(b, 4, 2 * h + 1))
                        pe.wait_ge(w_lo, 1)
                        for i in tiles:
                            pe.wait_ge(lo_ready, credited(b, 2 * QKT, h * QKT + i - 4))
                            products = [(c, w, r) for c in range(HC) for w, r in ((0, 0), (0, 1), (1, 0))]
                            for c, w, r in products:
                                last = nc.tensor.matmul(qkbank[i % 4], wqk_parts[:, w, c, i * P:(i + 1) * P],
                                                        XNT_parts[:, r, c, :], start=((c, w, r) == products[0]),
                                                        stop=((c, w, r) == products[-1]))
                            last.then_inc(qk_bank, 1)

                    def values(b, h):
                        pe.wait_ge(xnT_ready, credited(b, 4, 2 * h + 1))
                        for i in range(CT):
                            pe.wait_ge(logits_ready, credited(b, 8, 4 * h + i - 2))
                            for c in range(HC):
                                last = nc.tensor.matmul(vbank[i % 2][:, 0:D + E],
                                                        XNT[h][:, c, i * P:(i + 1) * P], wv_sb[:, c, :],
                                                        start=(c == 0), stop=(c == HC - 1))
                            last.then_inc(v_bank, 1)

                    def chunk(b, h):
                        project(b, h, range(QKT))
                        turn_rows(b, h + 1)
                        values(b, h)

                    turn_rows(0, 0)
                    pe.wait_ge(w_loaded, 80)
                    with pe.Fori(0, B - 1) as b:
                        for h in range(2):
                            chunk(b, h)
                    chunk(B - 1, 0)
                    values(B - 1, 1)
                    project(B - 1, 1, range(QKT // 2))
                    pe.wait_ge(chosen_ready, B)
                    cb = chosen_b[:].rearrange("p t e -> p (t e)")
                    nc.tensor.matmul(bank6[:, 0:T // P * E], earlier[:], cb, start=True, stop=True)
                    nc.tensor.matmul(bank7[:, 0:T // P * E], ones[:], cb, start=True, stop=True
                                     ).then_inc(ranks_bank, 1)
                    project(B - 1, 1, range(QKT // 2, QKT))

        gu_sb = sb("gu_sb", [P, HC, E, 2 * I])
        dn_sb = sb("dn_sb", [P, HC, E, D])
        gub_sb = sb("gub_sb", [P, E, 2 * I])
        dnb_sb = sb("dnb_sb", [P, E, D])

        with ExitStack() as ph:
            Qs = [Qs_first, sb("Qs_second", [P, 2, S], F32R, where=ph)]
            Ks = [Ks_first, sb("Ks_second", [P, 2, S], F32R, where=ph)]
            Vj = [sb(f"Vj{u}", [P, QT, DH], where=ph) for u in range(2)]
            Pr_long = [sb(f"Pr_long{i}", [P, 2, S], where=ph) for i in range(LONG_PR)]
            Pr_short = [sb(f"Pr_short{i}", [P, 2, S // 2], where=ph) for i in range(SHORT_PR)]
            AT = [sb(f"AT{i}", [P, CH], where=ph) for i in range(4)]
            Ob = [sb(f"Ob{i}", [P, CH], where=ph) for i in range(2)]
            dsum = [sb(f"dsum{u}", [P, QT, 2], where=ph) for u in range(2)]
            nmax = sb("nmax", [P, 2 * NQ], where=ph)
            rows = [sb(f"rows{u}", [P, D], where=ph) for u in range(2)]
            row_slot = [sb(f"row_slot{u}", [P, TOP_K], U32, where=ph) for u in range(2)]
            rec = sb("rec", [P, NQ], where=ph)
            coef = sb("coef", [P, NQ], where=ph)

            vj_ready = sem("vj_ready")
            d1_kept = sem("d1_kept")
            rows_loaded = [sem(f"rows_loaded{u}") for u in range(2)]
            row_slot_ready = sem("row_slot_ready")
            scatter_begun = sem("scatter_begun")
            rows_sorted = [sem(f"rows_sorted{u}") for u in range(2)]
            scored = sem("scored")
            maxed = sem("maxed")
            exped = sem("exped")
            rec_done = sem("rec_done")
            coef_done = sem("coef_done")
            combined = sem("combined")
            turned = sem("turned")
            turned_out = sem("turned_out")
            pv_done = sem("pv_done")
            o_out = sem("o_out")

            slot = bank
            tb, ob = bank6, bank7

            def probs(n):
                if n % 2 == 0:
                    return Pr_long[n // 2 % LONG_PR], n - 2 * LONG_PR
                return Pr_short[n // 2 % SHORT_PR], n - 2 * SHORT_PR

            with nc.Block() as block:
                @block.sync
                def _(sp):

                    def load(it, u):
                        sp.wait_ge(scored, credited(it, USES, (USES // 2) * (u + 1) - 1 - USES))
                        load_head(sp, it, u, Qs[u], Ks[u])

                    load(0, 1)
                    sp.dma_start(gu_sb[:].rearrange("p c e n -> p c (e n)"),
                                 gu.rearrange("(c p) e n -> p c (e n)", p=P)).then_inc(ew_loaded, 16)
                    sp.dma_start(dn_sb[:].rearrange("p c e n -> p c (e n)"),
                                 dn.rearrange("(c p) e n -> p c (e n)", p=P)).then_inc(ew_loaded, 16)
                    sp.dma_start(gub_sb[:], gub.partition_broadcast(P)).then_inc(ew_loaded, 16)
                    sp.dma_start(dnb_sb[:], dnb.partition_broadcast(P)).then_inc(ew_loaded, 16)
                    with sp.Fori(0, NIT - 1) as it:
                        for u in range(2):
                            load(it + 1, u)

                @block.gpsimd
                def _(pool):
                    pool.sem_inc(vj_ready, 2)
                    pool.sem_inc(d1_kept, 2)
                    xn_v = xn_dram.rearrange("(t p) d -> t p d", p=P)

                    def copy_v(it, u):
                        pool.wait_ge(pv_done, credited(it, NQ, QT * (u + 1) - 1 - NQ))
                        nc.gpsimd.tensor_copy(Vj[u][:].unsqueeze(1), VO[:, bass.ds(it, 1), :, u * DH:(u + 1) * DH]
                                              ).then_inc(vj_ready, 1)

                    def load_rows(it, u):
                        pool.dma_start(rows[u][:], xn_v[it * 2 + u]).then_inc(rows_loaded[u], 16)
                        nc.gpsimd.tensor_copy(row_slot[u][:].unsqueeze(1),
                                              slot_of[:, bass.ds(it * 2 + u, 1), :]
                                              ).then_inc(row_slot_ready, 1)

                    def sort_rows(it, u, k):
                        if k == 0:
                            pool.wait_ge(rows_loaded[u], 16 * (it + 1))
                            pool.wait_ge(row_slot_ready, 2 * it + u + 1)
                            pool.sem_inc(scatter_begun, 1)
                        pool.indirect_dma_start(xs_dram, bass.IndirectOffsetOnAxis(row_slot[u][:, k:k + 1], 0),
                                                rows[u][:], None).then_inc(rows_sorted[u], 16)

                    def keep_d1(it, u):
                        pool.wait_ge(exped, credited(it, STEPS, (STEPS // 2) * (u + 1) - 1))
                        nc.gpsimd.tensor_copy(d1_all[:, bass.ds(it * 2 + u, 1), :],
                                              dsum[u][:, :, 0].unsqueeze(1)).then_inc(d1_kept, 1)

                    with pool.Fori(0, NIT) as it:
                        for n in range(NQ):
                            if n % QT == 0:
                                copy_v(it, n // QT)
                            if n % QT == QT - 1:
                                keep_d1(it, n // QT)
                            if n == 2:
                                for u in range(2):
                                    load_rows(it, u)
                            if n in SORT_AT:
                                sort_rows(it, *SORT_AT[n])
                        for u in range(2):
                            pool.wait_ge(rows_sorted[u], 32 * (it + 1))

                def gathered_place(half, i):
                    return query(4 * half + i)[1] // (QT // 2) * 2 + i // 2

                def score(it, n, k):
                    if absent(it, n):
                        return
                    it, n = place(it, n)
                    head, q = query(n)
                    if k >= len(uses(n)):
                        return
                    use, maps = uses(n)[k]
                    if n % QT == 0 and k == 0:
                        nc.tensor.wait_ge(qk_loaded[head], 16 * 8 * (it + 1))
                    nc.tensor.wait_ge(exped, credited(it, STEPS, last_step(use - SLOTS)))
                    N = (q + 1) * P
                    for m in maps:
                        at = slot[use % SLOTS][:, CH:] if len(maps) > 1 and m else slot[use % SLOTS]
                        for c0 in range(0, N, CH):
                            c1 = min(c0 + CH, N)
                            nc.tensor.matmul(at[:, c0:c1], Qs[head][:, m, q * P:(q + 1) * P],
                                             Ks[head][:, m, c0:c1], start=True, stop=(c1 < N))
                        last = nc.tensor.matmul(at[:, N - P:N], identb[:], maskb[:], start=False, stop=True)
                    last.then_inc(scored, 1)

                def turn(it, n, k):
                    if absent(it, n):
                        return
                    it, n = place(it, n)
                    un = units(n)
                    if k >= len(un):
                        return
                    fill, _, blocks = un[k]
                    if k == 0:
                        nc.tensor.wait_ge(combined, credited(it, NQ, n))
                    nc.tensor.wait_ge(turned_out, credited(it, FILLS, fill - 1))
                    for i, kb in enumerate(blocks):
                        last = nc.tensor.transpose(tb[:, i * P:(i + 1) * P],
                                                   probs(n)[0][:, 0, kb * P:(kb + 1) * P], ident[:])
                    last.then_inc(turned, 1)

                def gather(it, n):
                    if absent(it, n):
                        return
                    it, n = place(it, n)
                    for half in gathers(n):
                        nc.tensor.wait_ge(turned_out, credited(it, FILLS, units(n)[-1][0]))
                        if isinstance(it, int) and it == 0 and half < 0:
                            nc.tensor.sem_inc(turned, 1)
                            continue
                        nc.tensor.wait_ge(o_out, credited(it, 4, half))
                        for i in range(4):
                            at = gathered_place(half, i) * DH
                            last = nc.tensor.matmul(tb[:, at:at + DH], Ob[half % 2][:, i * P:(i + 1) * P],
                                                    gather4[:], start=True, stop=True)
                        last.then_inc(turned, 1)

                def values(it, n):
                    if absent(it, n):
                        return
                    it, n = place(it, n)
                    head, q = query(n)
                    if n % QT == 0:
                        nc.tensor.wait_ge(vj_ready, credited(it, 2, head))
                    if n % 4 == 0:
                        nc.tensor.wait_ge(o_out, credited(it, 4, n // 4 - 1))
                        nc.tensor.matmul(ob[:], zerob[:, 0:P], zerob[:], start=True, stop=False,
                                         skip_group_check=True)
                    for fill, unit, blocks in units(n):
                        nc.tensor.wait_ge(turned_out, credited(it, FILLS, fill))
                        for i, kb in enumerate(blocks):
                            g = kb % 4
                            last = nc.tensor.matmul(
                                ob[DH * g:DH * (g + 1), (n % 4) * P:(n % 4 + 1) * P], Vj[head][:, kb, :],
                                AT[unit % 4][:, i * P:(i + 1) * P], start=False, stop=True,
                                tile_position=(0, DH * g), skip_group_check=True)
                    last.then_inc(pv_done, 1)

                def run_pairs(eng, ahead, pair):
                    for n in range(-2 * ahead, NQ, 2):
                        pair(0, n)
                    with eng.Fori(1, NIT - 1) as it:
                        for n in range(0, NQ, 2):
                            pair(it, n)
                    for n in range(0, NQ, 2):
                        pair(NIT - 1, n)

                @block.tensor
                def _(pe):
                    pe.sem_inc(scored, USES)
                    pe.sem_inc(turned, FILLS)
                    pe.sem_inc(pv_done, NQ)

                    def pair(it, n):
                        turn(it, n, 0)
                        turn(it, n, 1)
                        score(it, n + 3, 0)
                        values(it, n)
                        turn(it, n + 1, 0)
                        score(it, n + 4, 0)
                        gather(it, n + 1)
                        score(it, n + 4, 1)
                        values(it, n + 1)

                    run_pairs(pe, 2, pair)
                    nc.tensor.wait_ge(o_out, credited(NIT - 1, 4, 3))
                    for i in range(4):
                        at = gathered_place(3, i) * DH
                        last = nc.tensor.matmul(tb[:, at:at + DH], Ob[1][:, i * P:(i + 1) * P], gather4[:],
                                                start=True, stop=True)
                    last.then_inc(turned, 1)

                def exponential(it, n, m):
                    if absent(it, n):
                        return
                    it, n = place(it, n)
                    head, q = query(n)
                    step = 2 * n + m
                    N = (q + 1) * P
                    use, maps = [x for x in uses(n) if m in x[1]][0]
                    at = slot[use % SLOTS][:, CH:] if len(maps) > 1 and m else slot[use % SLOTS]
                    if m == maps[0]:
                        nc.scalar.wait_ge(maxed, credited(it, USES, use))
                    if m == 0:
                        user = probs(n)[1]
                        nc.scalar.wait_ge(turned, credited(it, FILLS, units(user % NQ)[-1][0] + user // NQ * FILLS))
                        if n % QT == 0:
                            nc.scalar.wait_ge(d1_kept, credited(it, 2, head - 2))
                    nc.scalar.activation(probs(n)[0][:, m, 0:N], at[:, 0:N], ACT.Exp,
                                         bias=nmax[:, step:step + 1], scale=1.0,
                                         accum_out=dsum[head][:, q, m:m + 1]).then_inc(exped, 1)

                def turn_out(it, n, k):
                    if absent(it, n):
                        return
                    it, n = place(it, n)
                    un = units(n)
                    if k >= len(un):
                        return
                    fill, unit, blocks = un[k]
                    nc.scalar.wait_ge(turned, credited(it, FILLS, fill))
                    user = [m for m in range(2 * NQ) if any(
                        (u + (m // NQ) * UNITS) == unit - 4 + UNITS for _, u, _ in units(m % NQ))][0]
                    nc.scalar.wait_ge(pv_done, credited(it, NQ, user - NQ))
                    w = len(blocks) * P
                    nc.scalar.copy(AT[unit % 4][:, 0:w], tb[:, 0:w]).then_inc(turned_out, 1)

                def out_tile(it, n):
                    if absent(it, n):
                        return
                    it, n = place(it, n)
                    if n % 4 != 3:
                        return
                    nc.scalar.wait_ge(pv_done, credited(it, NQ, n))
                    nc.scalar.copy(Ob[n // 4 % 2][:], ob[:]).then_inc(o_out, 1)

                def gathered_out(it, n):
                    if absent(it, n):
                        return
                    it, n = place(it, n)
                    for half in gathers(n):
                        nc.scalar.wait_ge(turned, credited(it, FILLS, units(n)[-1][0] + 1))
                        if isinstance(it, int) and it == 0 and half < 0:
                            nc.scalar.sem_inc(turned_out, 1)
                        else:
                            keep_half(it, half)

                def keep_half(it, half):
                    if half < 0:
                        it, half = it - 1, half + 4
                    head, first = half // 2, half % 2 * 2
                    to = VO[:, bass.ds(it, 1), :, head * DH:(head + 1) * DH].rearrange(
                        "p o (a t) d -> p (o a) t d", a=2)[:, :, first:first + 2, :]
                    nc.scalar.copy(to, tb[:, 0:4 * DH].rearrange("p (a t d) -> p a t d", a=2, t=2)
                                   ).then_inc(turned_out, 1)

                @block.scalar
                def _(act):
                    act.sem_inc(exped, STEPS)
                    act.sem_inc(turned_out, FILLS)
                    act.sem_inc(o_out, 4)

                    def pair(it, n):
                        turn_out(it, n, 0)
                        exponential(it, n + 2, 0)
                        turn_out(it, n, 1)
                        exponential(it, n + 2, 1)
                        turn_out(it, n + 1, 0)
                        exponential(it, n + 3, 0)
                        exponential(it, n + 3, 1)
                        out_tile(it, n + 1)
                        gathered_out(it, n + 1)

                    run_pairs(act, 1, pair)
                    act.wait_ge(turned, credited(NIT - 1, FILLS, FILLS))
                    keep_half(NIT - 1, 3)

                def maximum(it, n, k):
                    if absent(it, n):
                        return
                    it, n = place(it, n)
                    if k >= len(uses(n)):
                        return
                    use, maps = uses(n)[k]
                    N = (query(n)[1] + 1) * P
                    step = 2 * n + maps[0]
                    src = slot[use % SLOTS][:, 0:N]
                    if len(maps) > 1:
                        src = slot[use % SLOTS][:].rearrange("p (m n) -> p m n", m=2)[:, :, 0:N]
                    nc.vector.wait_ge(scored, credited(it, USES, use))
                    nc.vector.tensor_reduce(nmax[:, step:step + len(maps)], src, AX.X, ALU.max, negate=True
                                            ).then_inc(maxed, 1)

                def inverse(it, n):
                    if absent(it, n):
                        return
                    it, n = place(it, n)
                    head, q = query(n)
                    nc.vector.wait_ge(exped, credited(it, STEPS, 2 * n + 1))
                    nc.vector.reciprocal(rec[:, n:n + 1], dsum[head][:, q, 1:2]).then_inc(rec_done, 1)

                def ratio(it, n):
                    if absent(it, n):
                        return
                    it, n = place(it, n)
                    head, q = query(n)
                    nc.vector.wait_ge(rec_done, credited(it, NQ, n))
                    nc.vector.scalar_tensor_tensor(out=coef[:, n:n + 1], in0=dsum[head][:, q, 0:1],
                                                   scalar=neg_lam, in1=rec[:, n:n + 1], op0=ALU.mult,
                                                   op1=ALU.mult).then_inc(coef_done, 1)

                def combine(it, n):
                    if absent(it, n):
                        return
                    it, n = place(it, n)
                    N = (query(n)[1] + 1) * P
                    nc.vector.wait_ge(coef_done, credited(it, NQ, n))
                    nc.vector.scalar_tensor_tensor(
                        out=probs(n)[0][:, 0, 0:N], in0=probs(n)[0][:, 1, 0:N], scalar=coef[:, n:n + 1],
                        in1=probs(n)[0][:, 0, 0:N], op0=ALU.mult, op1=ALU.add).then_inc(combined, 1)

                @block.vector
                def _(dve):
                    dve.sem_inc(maxed, USES)
                    dve.sem_inc(rec_done, NQ)
                    dve.sem_inc(coef_done, NQ)
                    dve.sem_inc(combined, NQ)

                    def pair(it, n):
                        maximum(it, n + 1, 0)
                        inverse(it, n)
                        ratio(it, n)
                        combine(it, n)
                        inverse(it, n + 1)
                        maximum(it, n + 2, 0)
                        ratio(it, n + 1)
                        maximum(it, n + 2, 1)
                        combine(it, n + 1)

                    run_pairs(dve, 1, pair)

        with ExitStack() as ph:
            xs = [sb(f"xs{u}", [P, D], where=ph) for u in range(2)]
            xsT = [sb(f"xsT{u}", [P, HC, P], where=ph) for u in range(2)]
            hid = [sb(f"hid{u}", [P, 2 * I], where=ph) for u in range(2)]
            gate_tanh = [sb(f"gate_tanh{u}", [P, I], where=ph) for u in range(2)]
            glu = [sb(f"glu{u}", [P, I], where=ph) for u in range(2)]
            up = [sb(f"up{u}", [P, I], where=ph) for u in range(2)]
            act_in = [sb(f"act_in{u}", [P, I], where=ph) for u in range(2)]
            act_T = [sb(f"act_T{u}", [P, HC, P], where=ph) for u in range(2)]
            ys = [sb(f"ys{u}", [P, D], where=ph) for u in range(2)]

            xs_loaded = [sem(f"xs_loaded{u}") for u in range(2)]
            xs_turned = sem("xs_turned")
            xsT_ready = sem("xsT_ready")
            hid_bank = sem("hid_bank")
            hid_ready = sem("hid_ready")
            gate_ready = sem("gate_ready")
            tanh_ready = sem("tanh_ready")
            glu_ready = sem("glu_ready")
            up_ready = sem("up_ready")
            act_ready = sem("act_ready")
            act_turned = sem("act_turned")
            act_T_ready = sem("act_T_ready")
            y_bank = sem("y_bank")
            y_ready = sem("y_ready")
            y_stored = [sem(f"y_stored{u}") for u in range(2)]

            hbank = [bank[0][:, 0:CH], bank[0][:, CH:]]
            xbank = [bank[1][:, 0:CH], bank[1][:, CH:]]
            abank = [bank[2][:, 0:CH], bank[2][:, CH:]]
            ybank = [bank6, bank7]
            NIT3 = SLOT_TILES // 2

            def seen(it, u):
                return credited(it, 2, u)

            with nc.Block() as block:
                xs_v = xs_dram.rearrange("(n u p) d -> n u p d", u=2, p=P)
                ys_v = ys_dram.rearrange("(n u p) d -> n u p d", u=2, p=P)

                @block.sync
                def _(sp):
                    def load(it, u):
                        sp.wait_ge(xs_turned, seen(it, u - 2))
                        sp.dma_start(xs[u][:], xs_v[it, u]).then_inc(xs_loaded[u], 16)

                    with sp.Fori(0, NIT3) as it:
                        for u in range(2):
                            load(it, u)

                def expert_loader(eng):
                    registers = [eng.alloc_register(f"expert{n}") for n in range(4)]

                    def load(i):
                        eng.load(registers, expert_rows[0:1, bass.ds(i, 1), :].rearrange("p o n -> p (o n)"))
                        return [bass.RuntimeValue.of_register_unchecked(r, min_val=0, max_val=E - 1)
                                for r in registers]

                    return load

                def there(it, n):
                    return not isinstance(it, int) or 0 <= 2 * it + n < SLOT_TILES

                def run_steps(eng, step, load=None):
                    load = load or (lambda it: None)
                    step(0, 0, load(0))
                    with eng.Fori(0, NIT3 - 2) as it:
                        e = load(it)
                        step(it, 1, e)
                        step(it, 2, e)
                    e = load(NIT3 - 2)
                    for n in (1, 2, 3, 4):
                        step(NIT3 - 2, n, e)

                def turn_rows(it, n):
                    if not there(it, n):
                        return
                    it, u = it + n // 2, n % 2
                    nc.tensor.wait_ge(xs_loaded[u], 16 * (it + 1))
                    nc.tensor.wait_ge(xsT_ready, seen(it, u - 2))
                    for c in range(HC):
                        last = nc.tensor.transpose(xbank[u][:, c * P:(c + 1) * P], xs[u][:, c * P:(c + 1) * P],
                                                   ident[:])
                    last.then_inc(xs_turned, 1)

                def gate_and_up(it, n, experts_of):
                    if not there(it, n):
                        return
                    e = experts_of[n]
                    it, u = it + n // 2, n % 2
                    nc.tensor.wait_ge(xsT_ready, seen(it, u))
                    nc.tensor.wait_ge(hid_ready, seen(it, u - 2))
                    for c in range(HC):
                        last = nc.tensor.matmul(hbank[u], xsT[u][:, c, :],
                                                gu_sb[:, c, bass.ds(e, 1), :].rearrange("p o n -> p (o n)"),
                                                start=(c == 0), stop=(c == HC - 1))
                    last.then_inc(hid_bank, 1)

                def turn_act(it, n):
                    if not there(it, n):
                        return
                    it, u = it + n // 2, n % 2
                    nc.tensor.wait_ge(act_ready, seen(it, u))
                    nc.tensor.wait_ge(act_T_ready, seen(it, u - 2))
                    for c in range(HC):
                        last = nc.tensor.transpose(abank[u][:, c * P:(c + 1) * P],
                                                   act_in[u][:, c * P:(c + 1) * P], ident[:])
                    last.then_inc(act_turned, 1)

                def down(it, n, experts_of):
                    if not there(it, n):
                        return
                    e = experts_of[n]
                    it, u = it + n // 2, n % 2
                    nc.tensor.wait_ge(act_T_ready, seen(it, u))
                    nc.tensor.wait_ge(y_ready, seen(it, u - 2))
                    for c in range(HC):
                        last = nc.tensor.matmul(ybank[u][:, 0:D], act_T[u][:, c, :],
                                                dn_sb[:, c, bass.ds(e, 1), :].rearrange("p o n -> p (o n)"),
                                                start=(c == 0), stop=(c == HC - 1))
                    last.then_inc(y_bank, 1)

                @block.tensor
                def _(pe):
                    for s in (xs_turned, hid_bank, act_turned, y_bank):
                        pe.sem_inc(s, 2)
                    pe.wait_ge(ew_loaded, 64)
                    turn_rows(0, 0)
                    turn_rows(0, 1)
                    load = expert_loader(pe)
                    gate_and_up(0, 0, load(0))

                    def step(it, n, e):
                        gate_and_up(it, n + 1, e)
                        turn_rows(it, n + 2)
                        down(it, n - 1, e)
                        turn_act(it, n)

                    run_steps(pe, step, load)

                def rows_out(it, n):
                    if not there(it, n):
                        return
                    it, u = it + n // 2, n % 2
                    nc.scalar.wait_ge(xs_turned, seen(it, u))
                    nc.scalar.wait_ge(hid_bank, seen(it, u - 2))
                    nc.scalar.copy(xsT[u][:].rearrange("p c n -> p (c n)"), xbank[u][:, 0:HC * P]
                                   ).then_inc(xsT_ready, 1)

                def gate_curve(it, n):
                    if not there(it, n):
                        return
                    it, u = it + n // 2, n % 2
                    nc.scalar.wait_ge(gate_ready, seen(it, u))
                    nc.scalar.wait_ge(glu_ready, seen(it, u - 2))
                    nc.scalar.activation(gate_tanh[u][:], hid[u][:, 0:I], ACT.Tanh, scale=ALPHA / 2
                                         ).then_inc(tanh_ready, 1)

                def act_out(it, n):
                    if not there(it, n):
                        return
                    it, u = it + n // 2, n % 2
                    nc.scalar.wait_ge(act_turned, seen(it, u))
                    nc.scalar.wait_ge(y_bank, seen(it, u - 2))
                    nc.scalar.copy(act_T[u][:].rearrange("p c n -> p (c n)"), abank[u][:, 0:HC * P]
                                   ).then_inc(act_T_ready, 1)

                def store(it, n):
                    if not there(it, n):
                        return
                    it, u = it + n // 2, n % 2
                    nc.scalar.wait_ge(y_ready, seen(it, u))
                    nc.scalar.dma_start(ys_v[it, u], ys[u][:]).then_inc(y_stored[u], 16)

                @block.scalar
                def _(act):
                    for u in range(2):
                        act.sem_inc(y_stored[u], 16)
                    for s in (xsT_ready, tanh_ready, act_T_ready):
                        act.sem_inc(s, 2)
                    rows_out(0, 0)
                    rows_out(0, 1)
                    gate_curve(0, 0)

                    def step(it, n, e):
                        rows_out(it, n + 2)
                        gate_curve(it, n + 1)
                        store(it, n - 1)
                        act_out(it, n)

                    run_steps(act, step)
                    for u in range(2):
                        act.wait_ge(y_stored[u], 16 * (NIT3 + 1))

                def hidden(it, n, experts_of):
                    if not there(it, n):
                        return
                    e = experts_of[n]
                    it, u = it + n // 2, n % 2
                    nc.vector.wait_ge(hid_bank, seen(it, u))
                    nc.vector.tensor_tensor(hid[u][:], hbank[u],
                                            gub_sb[:, bass.ds(e, 1), :].rearrange("p o n -> p (o n)"), ALU.add
                                            ).then_inc(hid_ready, 1)

                def gate(it, n):
                    if not there(it, n):
                        return
                    it, u = it + n // 2, n % 2
                    nc.vector.wait_ge(hid_ready, seen(it, u))
                    nc.vector.tensor_scalar(hid[u][:, 0:I], hid[u][:, 0:I], LIMIT, None, ALU.min
                                            ).then_inc(gate_ready, 1)

                def activate(it, n):
                    if not there(it, n):
                        return
                    it, u = it + n // 2, n % 2
                    nc.vector.wait_ge(tanh_ready, seen(it, u))
                    nc.vector.scalar_tensor_tensor(out=glu[u][:], in0=gate_tanh[u][:], scalar=1.0,
                                                   in1=hid[u][:, 0:I], op0=ALU.add, op1=ALU.mult
                                                   ).then_inc(glu_ready, 1)
                    nc.vector.tensor_scalar(up[u][:], hid[u][:, I:], LIMIT, -LIMIT, ALU.min, ALU.max
                                            ).then_inc(up_ready, 1)
                    nc.vector.wait_ge(glu_ready, seen(it, u))
                    nc.vector.wait_ge(up_ready, seen(it, u))
                    nc.vector.wait_ge(act_turned, seen(it, u - 2))
                    nc.vector.scalar_tensor_tensor(out=act_in[u][:], in0=up[u][:], scalar=1.0, in1=glu[u][:],
                                                   op0=ALU.add, op1=ALU.mult).then_inc(act_ready, 1)

                def output(it, n, experts_of):
                    if not there(it, n):
                        return
                    e = experts_of[n]
                    it, u = it + n // 2, n % 2
                    nc.vector.wait_ge(y_bank, seen(it, u))
                    nc.vector.wait_ge(y_stored[u], 16 * (it + 1))
                    nc.vector.scalar_tensor_tensor(out=ys[u][:], in0=ybank[u][:, 0:D], scalar=0.5,
                                                   in1=dnb_sb[:, bass.ds(e, 1), :].rearrange("p o n -> p (o n)"),
                                                   op0=ALU.mult, op1=ALU.add).then_inc(y_ready, 1)

                @block.vector
                def _(dve):
                    for s in (hid_ready, gate_ready, glu_ready, up_ready, act_ready, y_ready):
                        dve.sem_inc(s, 2)
                    load = expert_loader(dve)
                    hidden(0, 0, load(0))
                    gate(0, 0)

                    def step(it, n, e):
                        activate(it, n)
                        hidden(it, n + 1, e)
                        gate(it, n + 1)
                        output(it, n - 1, e)

                    run_steps(dve, step, load)

        with ExitStack() as ph:
            xr = [sb(f"xr{h}", [P, CT, D], where=ph) for h in range(2)]
            yg = [sb(f"yg{h}", [P, CT, TOP_K, D], where=ph) for h in range(2)]
            yslot = [sb(f"yslot{h}", [P, CT, TOP_K], U32, where=ph) for h in range(2)]
            yw = [sb(f"yw{h}", [P, CT, TOP_K], where=ph) for h in range(2)]
            d1x = sb("d1x", [P, NH, CT], where=ph)
            d1e = sb("d1e", [P, NH // 2, CT, 2], where=ph)
            sq = sb("sq", [P, NH // 2, CT * 2 * DH], where=ph)
            square_sum = sb("square_sum", [P, NH // 2, CT * 2 * DH // GROUP], where=ph)
            root = sb("root", [P, NH // 2, CT * 2 * DH // GROUP], where=ph)
            On = sb("On", [P, CT, D], where=ph)
            OnT = sb("OnT", [P, CT, HC, P], where=ph)
            ff = [sb(f"ff{h}", [P, CT, D], where=ph) for h in range(2)]
            ft = [sb(f"ft{h}", [P, CT, D], where=ph) for h in range(2)]

            xr_loaded = [sem(f"xr_loaded{h}") for h in range(2)]
            picked = sem("picked")
            gather_begun = sem("gather_begun")
            y_gathered = [sem(f"y_gathered{h}") for h in range(2)]
            sq_ready = sem("sq_ready")
            d1_step = sem("d1_step")
            summed = sem("summed")
            ms_ready = sem("ms_ready")
            root_ready = sem("root_ready")
            recip_ready = sem("recip_ready")
            on_ready = sem("on_ready")
            on_turned = sem("on_turned")
            onT_ready = sem("onT_ready")
            att_bank = sem("att_bank")
            ff_half = sem("ff_half")
            ff_ready = sem("ff_ready")
            ft_ready = sem("ft_ready")
            silu_ready = sem("silu_ready")
            gated = sem("gated")
            res_ready = sem("res_ready")
            stored = [sem(f"stored{h}") for h in range(2)]
            tbank = [bank[2][:, 0:CH], bank[2][:, CH:]]
            wbank = [bank6, bank7]
            HT = CT // 2
            half_gain = math.sqrt(GROUP) * (1.0 - L_INIT) / 2

            with nc.Block() as block:
                @block.sync
                def _(sp):
                    x_v = x.rearrange("(b h t p) d -> b h p t d", b=B, h=2, p=P)
                    out_v = out.rearrange("(b h t p) d -> b h p t d", b=B, h=2, p=P)

                    def load_x(b, h):
                        sp.dma_start(xr[h][:], x_v[b, h]).then_inc(xr_loaded[h], 16)

                    def store(b, h):
                        sp.wait_ge(res_ready, credited(b, 2, h))
                        sp.dma_start(out_v[b, h], xr[h][:]).then_inc(stored[h], 16)

                    for h in range(2):
                        load_x(0, h)
                    with sp.Fori(0, B - 1) as b:
                        for h in range(2):
                            store(b, h)
                            sp.wait_ge(stored[h], 16 * (b + 1))
                            load_x(b + 1, h)
                    for h in range(2):
                        store(B - 1, h)
                    for h in range(2):
                        sp.wait_ge(stored[h], 16 * B)

                @block.gpsimd
                def _(pool):
                    pool.sem_inc(picked, 4)
                    with pool.Fori(0, B) as b:
                        for h in range(2):
                            pool.wait_ge(ff_ready, credited(b, 2, h - 2))
                            c = b * QT + h * CT
                            nc.gpsimd.tensor_copy(yslot[h][:], slot_of[:, bass.ds(c, CT), :]).then_inc(picked, 1)
                            nc.gpsimd.tensor_copy(yw[h][:], weight[:, bass.ds(c, CT), :]).then_inc(picked, 1)
                            pool.wait_ge(picked, credited(b, 4, 2 * h + 1))
                            pool.sem_inc(gather_begun, 1)
                            for i in range(CT):
                                for k in range(TOP_K):
                                    pool.indirect_dma_start(
                                        yg[h][:, i, k, :], None, ys_dram,
                                        bass.IndirectOffsetOnAxis(yslot[h][:, i, k:k + 1], 0)
                                    ).then_inc(y_gathered[h], 16)

                def outputs(b, h):
                    return VO[:, bass.ds(b * (NH // 2), NH // 2), h * CT:(h + 1) * CT, :].rearrange(
                        "p j t d -> p j (t d)")

                def run_chunks(eng, first, second):
                    def batch(b, more):
                        for h in range(2):
                            if more or h == 0:
                                first(b + (h + 1) // 2, (h + 1) % 2)
                            second(b, h)

                    first(0, 0)
                    with eng.Fori(0, B - 1) as b:
                        batch(b, True)
                    batch(B - 1, False)

                @block.tensor
                def _(pe):
                    for s in (on_turned, att_bank):
                        pe.sem_inc(s, 4)

                    def project(b, h):
                        pe.wait_ge(on_ready, credited(b, 4, 2 * h + 1))
                        for k in range(2):
                            pe.wait_ge(onT_ready, credited(b, 4, 2 * h + k - 2))
                            for t in range(HT):
                                for c in range(HC):
                                    n = t * HC + c
                                    last = nc.tensor.transpose(tbank[k][:, n * P:(n + 1) * P],
                                                               On[:, k * HT + t, c * P:(c + 1) * P], ident[:])
                            last.then_inc(on_turned, 1)
                        pe.wait_ge(gated, credited(b, 2, h - 1))
                        for k in range(2):
                            pe.wait_ge(onT_ready, credited(b, 4, 2 * h + k))
                            for t in range(HT):
                                for c in range(HC):
                                    last = nc.tensor.matmul(wbank[k][:, t * D:(t + 1) * D],
                                                            OnT[:, k * HT + t, c, :], wo_sb[:, c, :],
                                                            start=(c == 0), stop=(c == HC - 1))
                            last.then_inc(att_bank, 1)

                    with pe.Fori(0, B) as b:
                        for h in range(2):
                            project(b, h)

                @block.scalar
                def _(act):
                    act.sem_inc(onT_ready, 4)
                    for s in (sq_ready, ff_half, root_ready, ft_ready):
                        act.sem_inc(s, 2)

                    def squares(b, h):
                        act.wait_ge(ms_ready, credited(b, 2, h - 1))
                        nc.scalar.activation(sq[:], outputs(b, h), ACT.Square).then_inc(sq_ready, 1)

                    def first_expert(b, h):
                        act.wait_ge(res_ready, credited(b, 2, h - 2))
                        act.wait_ge(y_gathered[h], 16 * CT * TOP_K * (b + 1))
                        act.wait_ge(picked, credited(b, 4, 2 * h + 1))
                        for i in range(CT):
                            last = nc.scalar.activation(ff[h][:, i, :], yg[h][:, i, 0, :], ACT.Copy,
                                                        scale=yw[h][:, i, 0:1])
                        last.then_inc(ff_half, 1)

                    def curves(b, h):
                        act.wait_ge(on_ready, credited(b, 4, 2 * h - 1))
                        act.wait_ge(ms_ready, credited(b, 2, h))
                        nc.scalar.activation(root[:], square_sum[:], ACT.Sqrt, scale=1.0 / half_gain ** 2
                                             ).then_inc(root_ready, 1)
                        act.wait_ge(res_ready, credited(b, 2, h - 2))
                        act.wait_ge(ff_ready, credited(b, 2, h))
                        nc.scalar.activation(ft[h][:], ff[h][:], ACT.Tanh, scale=0.5).then_inc(ft_ready, 1)

                    def turned_out(b, h):
                        act.wait_ge(att_bank, credited(b, 4, 2 * h - 1))
                        for k in range(2):
                            act.wait_ge(on_turned, credited(b, 4, 2 * h + k))
                            nc.scalar.copy(OnT[:, k * HT:(k + 1) * HT, :, :].rearrange("p t c n -> p (t c n)"),
                                           tbank[k]).then_inc(onT_ready, 1)

                    squares(0, 0)
                    first_expert(0, 0)
                    curves(0, 0)

                    def batch(b, more):
                        for h in range(2):
                            after = (b + (h + 1) // 2, (h + 1) % 2)
                            if more or h == 0:
                                squares(*after)
                            turned_out(b, h)
                            if more or h == 0:
                                first_expert(*after)
                                curves(*after)

                    with act.Fori(0, B - 1) as b:
                        batch(b, True)
                    batch(B - 1, False)

                @block.vector
                def _(dve):
                    for s in (on_ready, d1_step):
                        dve.sem_inc(s, 4)
                    for s in (summed, ms_ready, recip_ready, ff_ready, silu_ready, gated, res_ready):
                        dve.sem_inc(s, 2)

                    def normalise(b, h):
                        nc.vector.tensor_copy(d1x[:], d1_all[:, bass.ds(b * NH, NH), h * CT:(h + 1) * CT]
                                              ).then_inc(d1_step, 1)
                        dve.wait_ge(d1_step, credited(b, 4, 2 * h))
                        d1p = d1x[:].rearrange("p (j u) t -> p j u t", u=2)
                        nc.vector.tensor_tensor(d1e[:].rearrange("p j t u -> p j u t"), d1p, d1p, ALU.mult
                                                ).then_inc(d1_step, 1)
                        dve.wait_ge(sq_ready, credited(b, 2, h))
                        dve.wait_ge(root_ready, credited(b, 2, h - 1))
                        nc.vector.tensor_reduce(square_sum[:], sq[:].rearrange("p j (a c) -> p j a c", c=GROUP), AX.X,
                                                ALU.add).then_inc(summed, 1)
                        dve.wait_ge(d1_step, credited(b, 4, 2 * h + 1))
                        dve.wait_ge(summed, credited(b, 2, h))
                        per_head = square_sum[:].rearrange("p j (n a) -> p (j n) a", a=DH // GROUP)
                        nc.vector.scalar_tensor_tensor(
                            out=per_head, in0=d1e[:].rearrange("p j t u -> p (j t u)").unsqueeze(2)
                            .broadcast_to([P, CT * NH, DH // GROUP]), scalar=GROUP * RMS_EPS, in1=per_head,
                            op0=ALU.mult, op1=ALU.add).then_inc(ms_ready, 1)
                        dve.wait_ge(ff_half, credited(b, 2, h))
                        dve.wait_ge(y_gathered[h], 16 * CT * TOP_K * (b + 1))
                        for i in range(CT):
                            last = nc.vector.scalar_tensor_tensor(
                                out=ff[h][:, i, :], in0=yg[h][:, i, 1, :], scalar=yw[h][:, i, 1:2],
                                in1=ff[h][:, i, :], op0=ALU.mult, op1=ALU.add)
                        last.then_inc(ff_ready, 1)
                        dve.wait_ge(root_ready, credited(b, 2, h))
                        nc.vector.reciprocal(root[:], root[:]).then_inc(recip_ready, 1)
                        dve.wait_ge(recip_ready, credited(b, 2, h))
                        dve.wait_ge(on_turned, credited(b, 4, 2 * h - 1))
                        for k in range(2):
                            for j in range(2 * k, 2 * k + 2):
                                to = On[:, :, j * 2 * DH:(j + 1) * 2 * DH].rearrange(
                                    "p t (a c) -> p t a c", c=GROUP)
                                o4 = VO[:, bass.ds(b * (NH // 2) + j, 1), h * CT:(h + 1) * CT, :].rearrange(
                                    "p o t (a c) -> p (o t) a c", c=GROUP)
                                r4 = root[:, j, :].rearrange("p (t a) -> p t a", t=CT).unsqueeze(3).broadcast_to(
                                    [P, CT, 2 * DH // GROUP, GROUP])
                                last = nc.vector.tensor_tensor(to, o4, r4, ALU.mult)
                            last.then_inc(on_ready, 1)

                    def finish(b, h):
                        dve.wait_ge(ft_ready, credited(b, 2, h))
                        nc.vector.scalar_tensor_tensor(out=ft[h][:], in0=ft[h][:], scalar=1.0, in1=ff[h][:],
                                                       op0=ALU.add, op1=ALU.mult).then_inc(silu_ready, 1)
                        dve.wait_ge(silu_ready, credited(b, 2, h))
                        for k in range(2):
                            dve.wait_ge(att_bank, credited(b, 4, 2 * h + k))
                            part = ft[h][:, k * HT:(k + 1) * HT, :].rearrange("p t d -> p (t d)")
                            last = nc.vector.tensor_tensor(part, part, wbank[k][:], ALU.mult)
                        last.then_inc(gated, 1)
                        dve.wait_ge(gated, credited(b, 2, h))
                        dve.wait_ge(xr_loaded[h], 16 * (b + 1))
                        nc.vector.tensor_tensor(xr[h][:], ft[h][:], xr[h][:], ALU.add).then_inc(res_ready, 1)

                    run_chunks(dve, normalise, finish)


def kernel(L0_attn_x, L0_attn_l_q1, L0_attn_l_k1, L0_attn_l_q2, L0_attn_l_k2, L0_attn_wq, L0_attn_wk, L0_attn_wv,
           L0_attn_wo, L0_ffn_router_weight, L0_ffn_router_bias, L0_ffn_gate_up_proj, L0_ffn_gate_up_proj_bias,
           L0_ffn_down_proj, L0_ffn_down_proj_bias):
    import numpy as np
    import concourse.bacc as bacc
    from concourse.bass_utils import run_bass_kernel_spmd

    def heads(w):
        return np.asarray(w).reshape(2, NH, DH, D).transpose(3, 1, 0, 2).reshape(D, 2 * NH * DH)

    arrays = {
        "x": np.asarray(L0_attn_x).reshape(T, D),
        "wqk": np.concatenate([heads(L0_attn_wq), heads(L0_attn_wk)], axis=1),
        "wv": np.asarray(L0_attn_wv).T,
        "wo": np.asarray(L0_attn_wo).T,
        "lam": np.stack([np.asarray(a) for a in (L0_attn_l_q1, L0_attn_l_k1, L0_attn_l_q2, L0_attn_l_k2)]),
        "rw": np.asarray(L0_ffn_router_weight).T,
        "rb": np.asarray(L0_ffn_router_bias),
        "gu": np.asarray(L0_ffn_gate_up_proj).reshape(E, D, I, 2).transpose(1, 0, 3, 2).reshape(D, E, 2 * I),
        "gub": np.asarray(L0_ffn_gate_up_proj_bias).reshape(E, I, 2).transpose(0, 2, 1).reshape(E, 2 * I),
        "dn": np.asarray(L0_ffn_down_proj).transpose(1, 0, 2),
        "dnb": np.asarray(L0_ffn_down_proj_bias),
    }
    arrays = {name: np.ascontiguousarray(a) for name, a in arrays.items()}
    nc = bacc.Bacc("TRN2", target_bir_lowering=False, num_devices=1)
    args = [nc.dram_tensor(name, a.shape, mybir.dt.from_np(a.dtype), kind="ExternalInput").ap()
            for name, a in arrays.items()]
    out = nc.dram_tensor("out", (T, D), F32, kind="ExternalOutput").ap()
    build(nc, *args, out)
    r = run_bass_kernel_spmd(nc, [arrays], core_ids=[0])
    return r.results[0]["out"].reshape(B, S, D)
```
